# Optimizing a Trainium2 kernel written in Bass

```python
import numpy as np
import jax
import jax.numpy as jnp

def _softmax(x, axis=-1):
    return jax.nn.softmax(x, axis=axis)

def _gelu(x):
    return jax.nn.gelu(x, approximate=True)

def _silu(x):
    return jax.nn.silu(x)

def _sigmoid(x):
    return jax.nn.sigmoid(x)

def _layernorm(x, axis=-1, eps=1e-05):
    m = jnp.mean(x, axis=axis, keepdims=True)
    v = jnp.var(x, axis=axis, keepdims=True)
    return (x - m) / jnp.sqrt(v + eps)

def _scatter_add(tgt, idx, src, axis=0):
    return tgt.at[idx].add(src)

def _segment_sum(src, seg, n):
    return jax.ops.segment_sum(src, seg, n)
kernel_name = 'mk_gnn_resnorm_d2_gnn_r8_6b0fd6'

def setup_inputs(seed: int=0):
    np.random.seed(seed)
    _w = jnp.asarray

    def _rec_inputs():
        import jax
        import jax.numpy as jnp
        _gk = jax.random.key(seed)
        x = -0.0002117 + 1 * jax.random.normal(jax.random.fold_in(_gk, 1), (6250, 256), jnp.float32)
        _s = jax.random.randint(jax.random.fold_in(_gk, 2), (50000,), 0, 6250, jnp.int32)
        _d = jax.random.randint(jax.random.fold_in(_gk, 3), (50000,), 0, 6250, jnp.int32)
        _loop = jnp.arange(6250, dtype=jnp.int32)
        src = jnp.concatenate([_s, _d, _loop])
        dst = jnp.concatenate([_d, _s, _loop])
        _o = jnp.argsort(dst, stable=True)
        src = src[_o]
        dst = dst[_o]
        edge_type_500 = jax.random.randint(jax.random.fold_in(_gk, 12), (106250,), 0, 500, jnp.int32)
        edge_weight = jax.random.uniform(jax.random.fold_in(_gk, 13), (106250,), jnp.float32, 0.0, 1)
        return (x, src, dst, edge_type_500, edge_weight)
    x, src, dst, edge_type_500, edge_weight = _rec_inputs()

    def _L0_gnn_setup():
        import jax, jax.numpy as jnp
        import numpy as np
        N_NODES = 12500
        N_EDGES = 400000
        C = 256
        key = jax.random.key(seed)
        k1, k2, k3, k4 = jax.random.split(key, 4)
        x = jax.random.normal(k1, (N_NODES, C), dtype=jnp.float32)
        edge_weight = jax.random.uniform(k2, (N_EDGES,), dtype=jnp.float32)
        row = jax.random.randint(k3, (N_EDGES,), 0, N_NODES)
        col = jax.random.randint(k4, (N_EDGES,), 0, N_NODES)
        edge_index = jnp.stack([row, col]).astype(jnp.int64)
        return {'x': x, 'edge_weight': edge_weight, 'edge_index': edge_index}
    _L0_gnn_all = _L0_gnn_setup()
    _L0_gnn_in = {k: v for k, v in _L0_gnn_all.items() if k in ()}
    del _L0_gnn_all

    def _L1_gnn_setup():
        import jax, jax.numpy as jnp
        import numpy as np
        G = (1.0, 1.0)

        def to_hypercomplex(x, n_blades):
            return x.reshape(*x.shape[:-1], n_blades, -1).swapaxes(-2, -1)

        def clifford_kernel_2d(w, g):
            g0, g1 = g
            k0 = jnp.concatenate([w[0], g0 * w[1], g1 * w[2], -g0 * g1 * w[3]], axis=1)
            k1 = jnp.concatenate([w[1], w[0], -g1 * w[3], g1 * w[2]], axis=1)
            k2 = jnp.concatenate([w[2], g0 * w[3], w[0], -g0 * w[1]], axis=1)
            k3 = jnp.concatenate([w[3], w[2], w[1], w[0]], axis=1)
            return jnp.concatenate([k0, k1, k2, k3], axis=0)

        def clifford_linear(x, w, b, g=G):
            N = x.shape[0]
            k = clifford_kernel_2d(w, g)
            xf = x.swapaxes(-2, -1).reshape(N, -1)
            out = xf @ k.T + b.reshape(-1)
            C_out = w.shape[1]
            return out.reshape(N, 4, C_out).swapaxes(-2, -1)
        key = jax.random.key(seed)
        ks = jax.random.split(key, 10)
        N, E, R, emb_dim = (12500, 75000, 500, 256)
        C = emb_dim // 4
        s = 0.05
        return {'h': jax.random.normal(ks[0], (N, emb_dim), jnp.float32), 'edge_index': jax.random.randint(ks[1], (2, E), 0, N, jnp.int64), 'edge_type': jax.random.randint(ks[2], (E,), 0, R, jnp.int64), 'relation_emb': jax.random.normal(ks[3], (R, emb_dim), jnp.float32), 'msg_w': jax.random.normal(ks[4], (4, C, C), jnp.float32) * s, 'msg_b': jax.random.normal(ks[5], (4, C), jnp.float32) * s, 'upd_w': jax.random.normal(ks[6], (4, C, C), jnp.float32) * s, 'upd_b': jax.random.normal(ks[7], (4, C), jnp.float32) * s, 'gate_w': jax.random.normal(ks[8], (1, emb_dim), jnp.float32) * s, 'gate_b': jax.random.normal(ks[9], (1,), jnp.float32) * s}
    _L1_gnn_all = _L1_gnn_setup()
    _L1_gnn_in = {k: v for k, v in _L1_gnn_all.items() if k in ('relation_emb', 'msg_w', 'msg_b', 'upd_w', 'upd_b', 'gate_w', 'gate_b')}
    del _L1_gnn_all
    return {'x': x, 'src': src, 'dst': dst, 'edge_type_500': edge_type_500, 'edge_weight': edge_weight, 'L1_gnn_relation_emb': _L1_gnn_in['relation_emb'], 'L1_gnn_msg_w': _L1_gnn_in['msg_w'], 'L1_gnn_msg_b': _L1_gnn_in['msg_b'], 'L1_gnn_upd_w': _L1_gnn_in['upd_w'], 'L1_gnn_upd_b': _L1_gnn_in['upd_b'], 'L1_gnn_gate_w': _L1_gnn_in['gate_w'], 'L1_gnn_gate_b': _L1_gnn_in['gate_b']}

def reference(x, src, dst, edge_type_500, edge_weight, L1_gnn_relation_emb, L1_gnn_msg_w, L1_gnn_msg_b, L1_gnn_upd_w, L1_gnn_upd_b, L1_gnn_gate_w, L1_gnn_gate_b):
    import jax
    import jax.numpy as jnp

    def _L0_gnn_ref(x, edge_weight, edge_index):
        import jax, jax.numpy as jnp
        import numpy as np
        N_NODES = 12500
        N_EDGES = 400000
        C = 256
        n = x.shape[0]
        c_half = x.shape[-1] // 2
        row, col = (edge_index[0], edge_index[1])
        ones = jnp.ones(edge_index.shape[1], dtype=x.dtype)
        deg_row = jax.ops.segment_sum(ones, row, num_segments=n)
        deg_col = jax.ops.segment_sum(ones, col, num_segments=n)
        w = edge_weight[:, None]
        msg_fwd = w * x[col, :c_half]
        x_fwd = jax.ops.segment_sum(msg_fwd, row, num_segments=n)
        x_fwd = x_fwd / jnp.clip(deg_row, 1.0)[:, None]
        msg_bwd = w * x[row, c_half:]
        x_bwd = jax.ops.segment_sum(msg_bwd, col, num_segments=n)
        x_bwd = x_bwd / jnp.clip(deg_col, 1.0)[:, None]
        return jnp.concatenate([x_fwd, x_bwd], axis=-1)

    def _L1_gnn_ref(h, edge_index, edge_type, relation_emb, msg_w, msg_b, upd_w, upd_b, gate_w, gate_b):
        import jax, jax.numpy as jnp
        import numpy as np
        G = (1.0, 1.0)

        def to_hypercomplex(x, n_blades):
            return x.reshape(*x.shape[:-1], n_blades, -1).swapaxes(-2, -1)

        def clifford_kernel_2d(w, g):
            g0, g1 = g
            k0 = jnp.concatenate([w[0], g0 * w[1], g1 * w[2], -g0 * g1 * w[3]], axis=1)
            k1 = jnp.concatenate([w[1], w[0], -g1 * w[3], g1 * w[2]], axis=1)
            k2 = jnp.concatenate([w[2], g0 * w[3], w[0], -g0 * w[1]], axis=1)
            k3 = jnp.concatenate([w[3], w[2], w[1], w[0]], axis=1)
            return jnp.concatenate([k0, k1, k2, k3], axis=0)

        def clifford_linear(x, w, b, g=G):
            N = x.shape[0]
            k = clifford_kernel_2d(w, g)
            xf = x.swapaxes(-2, -1).reshape(N, -1)
            out = xf @ k.T + b.reshape(-1)
            C_out = w.shape[1]
            return out.reshape(N, 4, C_out).swapaxes(-2, -1)
        n_blades = 4
        num_nodes = h.shape[0]
        h_hc = to_hypercomplex(h, n_blades)
        r_hc = to_hypercomplex(relation_emb, n_blades)
        src, dst = (edge_index[0], edge_index[1])
        h_src = h_hc[src]
        r_uv = r_hc[edge_type]
        m = clifford_linear(h_src * r_uv, msg_w, msg_b)
        gate = jax.nn.sigmoid(r_uv.reshape(r_uv.shape[0], -1) @ gate_w.T + gate_b)
        m = m * gate[:, :, None]
        ones = jnp.ones_like(src, dtype=jnp.float32)
        deg_src = jax.ops.segment_sum(ones, src, num_segments=num_nodes)
        deg_dst = jax.ops.segment_sum(ones, dst, num_segments=num_nodes)
        norm = jnp.maximum(deg_src[src] * deg_dst[dst], 1.0) ** (-0.5)
        m = m * norm[:, None, None]
        h_agg = jax.ops.segment_sum(m, dst, num_segments=num_nodes)
        h_out = clifford_linear(h_hc + h_agg, upd_w, upd_b)
        return h_out.reshape(num_nodes, -1)
    edge_index = jnp.stack([src, dst])
    x = _layernorm(x + _L0_gnn_ref(x, edge_weight, edge_index), axis=-1)
    x = _layernorm(x + _L1_gnn_ref(x, edge_index, edge_type_500, L1_gnn_relation_emb, L1_gnn_msg_w, L1_gnn_msg_b, L1_gnn_upd_w, L1_gnn_upd_b, L1_gnn_gate_w, L1_gnn_gate_b), axis=-1)
    return x

_drawn_inputs = setup_inputs


def setup_inputs(seed=0):
    import zlib

    import numpy as np

    out = dict(_drawn_inputs(seed))
    spreads = {}
    factors = {'L1_gnn_msg_b': 3.506, 'L1_gnn_gate_w': 2.774}
    for name, (base, spread) in spreads.items():
        noise = np.random.default_rng([zlib.crc32(name.encode()), seed]).standard_normal(out[name].shape)
        drawn = base * np.exp(spread * noise) if base else spread * noise
        out[name] = jnp.asarray(drawn.astype(out[name].dtype))
    for name, factor in factors.items():
        out[name] = (out[name] * factor).astype(out[name].dtype)
    return out
```

```python
from contextlib import ExitStack

import concourse.bass as bass
from concourse import mybir

ALU = mybir.AluOpType
ACT = mybir.ActivationFunctionType
F32 = mybir.dt.float32
BF16 = mybir.dt.bfloat16
I32 = mybir.dt.int32
AX_X = mybir.AxisListType.X
ds = bass.ds

P = 128
UNROLL = 4
COPIES = UNROLL


def build_gnn(nc, x, src, dst, edge_type, edge_weight, rel, msg_w, msg_b, upd_w, upd_b, gate_w, gate_b, out):
    N, C = x.shape
    H = C // 2
    E = src.shape[0]
    R = rel.shape[0]
    NB = -(-N // P)
    NBX = NB + 1
    LAST = N - (NB - 1) * P
    ER = max(d for d in range(1, P + 1) if E % d == 0)
    EC = E // ER
    T = -(-((E + NB * (P - 1)) // P) // (2 * UNROLL)) * 2 * UNROLL
    G = T // UNROLL
    PAIRS = G // 2
    RT = max(d for d in range(1, P + 1) if R % d == 0)
    RK = R // RT
    W0 = H + 2
    W1 = C + 2
    ROWS = -(-(N + P) // P) * P
    EPS = 1e-5
    B4 = 4
    CB = C // B4
    NCUM = NBX + 3
    FB = 5
    assert EC % FB == 0 and C == 2 * P

    rec_dram = nc.dram_tensor("edge_records", [E + P, 4], F32).ap()
    sum_dram = [nc.dram_tensor(f"source_sums_{k}", [ROWS, W0], F32).ap() for k in range(COPIES)]
    h_dram = nc.dram_tensor("scaled_nodes", [NB * P, W1], F32).ap()
    r_dram = nc.dram_tensor("gated_relations", [R, W1], F32).ap()
    x_halves = x.rearrange("n (h c) -> (n h) c", h=2)

    with ExitStack() as ctx:
        def sb(name, shape, dt):
            return ctx.enter_context(nc.sbuf_tensor(name, shape, dt))

        def sem(name):
            return ctx.enter_context(nc.semaphore(name))

        bank = [ctx.enter_context(nc.psum_tensor(f"bank{k}", [P, 512], F32)) for k in range(8)]

        nodes = sb("nodes", [P, NBX * C], F32)
        acc0 = sb("acc0", [P, NBX * W0], F32)
        acc1 = sb("acc1", [P, NBX * W1], F32)
        records = sb("records", [P, T * 4], F32)
        tile_base = sb("tile_base", [P, T], F32)
        tile_block = sb("tile_block", [1, T], I32)
        tile_offset = sb("tile_offset", [1, T], I32)
        iota_free = sb("iota_free", [P, P], F32)
        iota_part = sb("iota_part", [P, 1], F32)
        spare = sb("spare", [P, 1], F32)
        ident = sb("ident", [P, P], F32)
        earlier = sb("earlier", [P, P], F32)
        later = sb("later", [P, P], F32)
        ones = sb("ones", [P, P], F32)
        ones_bf = sb("ones_bf", [P, 1], BF16)
        eps_col = sb("eps_col", [P, 1], F32)
        dst_scale = sb("dst_scale", [P, NB], F32)
        upd_t = sb("upd_t", [P, 2 * C], F32)
        both_t = sb("both_t", [P, 2 * C], F32)
        msg_bias = sb("msg_bias", [P, C], F32)
        upd_bias = sb("upd_bias", [P, C], F32)

        cum = sb("cum", [P, NCUM], F32)
        bucket = sb("bucket", [P, NBX], F32)
        first_pos = sb("first_pos", [P, NBX], F32)
        limits = sb("limits", [P, NBX + 1], F32)
        next_dst = sb("next_dst", [P, 1], I32)
        next_dst_f = sb("next_dst_f", [P, 1], F32)
        starts = sb("starts", [P, 8], F32)
        starts_i = sb("starts_i", [P, 2], I32)
        disorder = sb("disorder", [1, 1], I32)
        pad_rec = sb("pad_rec", [P, 4], F32)
        fb_idx = sb("fb_idx", [P, FB], I32)
        fb_rec = sb("fb_rec", [P, FB * 4], F32)
        dst_i, src_i, wgt_f, typ_i = (acc1[0:ER, k * EC:(k + 1) * EC] for k in range(4))
        dst_i, src_i, typ_i = dst_i.bitcast(I32), src_i.bitcast(I32), typ_i.bitcast(I32)
        rec4 = acc1[0:ER, 4 * EC:8 * EC]
        dst_f = acc1[0:ER, 8 * EC:9 * EC]
        work_a, work_b, work_c, pos = (acc1[0:ER, k * EC:(k + 1) * EC] for k in range(9, 13))
        pos_i = work_a.bitcast(I32)
        in_block = acc1[0:NBX, 9 * EC:9 * EC + T]
        below_next = acc1[0:NBX, 11 * EC:11 * EC + T]
        iota_t = acc1[:, 13 * EC:13 * EC + T]
        assert 13 * EC + T <= NBX * W1
        w_nat = sb("w_nat", [P, 4 * C], F32)
        gate_wb = sb("gate_wb", [P, C], F32)
        gate_bb = sb("gate_bb", [P, 1], F32)
        gate_z = sb("gate_z", [P, RK], F32)
        gate = sb("gate", [P, RK], F32)
        bias_raw = sb("bias_raw", [P, C], F32)
        bias_col = sb("bias_col", [P, 2], F32)

        ring = sb("ring", [P, 2 * UNROLL * W1 * 2], F32)
        hg = [ring[:, q * UNROLL * W1:(q + 1) * UNROLL * W1] for q in range(2)]
        rg = [ring[:, (2 + q) * UNROLL * W1:(3 + q) * UNROLL * W1] for q in range(2)]
        xg = [ring[:, q * UNROLL * H:(q + 1) * UNROLL * H] for q in range(2)]
        combined = [ring[:, (2 * H + q * W0) * UNROLL:(2 * H + (q + 1) * W0) * UNROLL] for q in range(2)]
        same = ring[:, 2 * (H + W0) * UNROLL:(3 * H + 2 * W0) * UNROLL]
        same_earlier = ring[:, (3 * H + 2 * W0) * UNROLL:(4 * H + 2 * W0) * UNROLL]
        spread_sb = ring[:, (4 * H + 2 * W0) * UNROLL:(5 * H + 2 * W0) * UNROLL]
        onehot = [sb(f"onehot{q}", [P, UNROLL * P], BF16) for q in range(2)]
        onehot_w = [sb(f"onehot_w{q}", [P, UNROLL * P], F32) for q in range(2)]
        local = [sb(f"local{q}", [P, UNROLL], F32) for q in range(2)]
        not_neg = sb("not_neg", [P, UNROLL], F32)
        valid = sb("valid", [P, UNROLL], F32)
        src_rel = sb("src_rel", [P, UNROLL], F32)
        src_key = [sb(f"src_key{q}", [P, UNROLL], F32) for q in range(2)]
        n_earlier = sb("n_earlier", [P, UNROLL], F32)
        first_rel = sb("first_rel", [P, UNROLL], F32)
        gather_idx = [sb(f"gather_idx{q}", [P, UNROLL], I32) for q in range(2)]
        type_idx = [sb(f"type_idx{q}", [P, UNROLL], I32) for q in range(2)]
        scatter_idx = [sb(f"scatter_idx{q}", [P, UNROLL], I32) for q in range(2)]
        product = [sb(f"product{q}", [P, UNROLL * W1], F32) for q in range(2)]
        assert RK <= UNROLL
        rel_sb, rel_out = product[0][:, 0:RK * C], product[1][:, 0:RK * W1]

        sums4 = [ring[:, q * COPIES * W0:(q + 1) * COPIES * W0] for q in range(2)]
        sums = sb("sums", [P, W0], F32)
        y_node = sb("y_node", [P, C], F32)
        deg = sb("deg", [P, 2], F32)
        rdeg = sb("rdeg", [P, 2], F32)
        stats = sb("stats", [P, 6], F32)
        mean_var = sb("mean_var", [P, 2], F32)
        roots = sb("roots", [P, 3], F32)
        rroots = [sb(f"rroots{q}", [P, 3], F32) for q in range(2)]
        h_rows = [product[q][:, 0:W1] for q in range(2)]
        turned = [onehot_w[q] for q in range(2)]
        staged = [rg[q][:, 0:2 * C] for q in range(2)]
        agg_part = sb("agg_part", [P, C], F32)
        x_bias = sb("x_bias", [P, C], F32)
        y_out = [sb(f"y_out{q}", [P, C], F32) for q in range(2)]

        wait_holder = sem("wait_holder")
        edges_in = sem("edges_in")
        x_in = sem("x_in")
        x_tail_in = sem("x_tail_in")
        tail_zero = sem("tail_zero")
        const_iota = sem("const_iota")
        const_done = sem("const_done")
        weights_in = sem("weights_in")
        prep = sem("prep")
        acc0_zero = sem("acc0_zero")
        zeroed = sem("zeroed")
        pad_stored = sem("pad_stored")
        counted = sem("counted")
        starts_done = sem("starts_done")
        table_sel = sem("table_sel")
        prep_pe = sem("prep_pe")
        disorder_set = sem("disorder_set")
        rec_built = sem("rec_built")
        pos_ready = sem("pos_ready")
        fb_copied = sem("fb_copied")
        rec_stored = sem("rec_stored")
        rec_ready = sem("rec_ready")
        tables_ready = sem("tables_ready")
        rel_ready = sem("rel_ready")
        gate_lin = sem("gate_lin")
        gate_ready = sem("gate_ready")
        rel_stored = sem("rel_stored")
        negated = sem("negated")
        fold_ready = sem("fold_ready")
        rec_in = sem("rec_in")
        idx_ready = sem("idx_ready")
        x_gathered = [sem(f"x_gathered{q}") for q in range(2)]
        local_ready = sem("local_ready")
        onehot_ready = sem("onehot_ready")
        onehot_w_ready = sem("onehot_w_ready")
        not_neg_ready = sem("not_neg_ready")
        valid_ready = sem("valid_ready")
        src_rel_ready = sem("src_rel_ready")
        key_ready = sem("key_ready")
        keys_spread = sem("keys_spread")
        same_ready = sem("same_ready")
        same_earlier_ready = sem("same_earlier_ready")
        n_earlier_ready = sem("n_earlier_ready")
        degree_ready = sem("degree_ready")
        first_ready = sem("first_ready")
        scatter_idx_ready = sem("scatter_idx_ready")
        spread_done = sem("spread_done")
        spread_copied = sem("spread_copied")
        summed = sem("summed")
        acc0_added = sem("acc0_added")
        combined_done = sem("combined_done")
        combined_copied = sem("combined_copied")
        added = sem("added")
        sums_in = [sem(f"sums_in{q}") for q in range(2)]
        node0 = sem("node0")
        roots_ready = sem("roots_ready")
        h_built = sem("h_built")
        rdeg_ready = sem("rdeg_ready")
        y_ready = sem("y_ready")
        y1_ready = sem("y1_ready")
        dst_scale_set = sem("dst_scale_set")
        h_stored = [sem(f"h_stored{q}") for q in range(2)]
        acc1_zero = sem("acc1_zero")
        idx1_ready = sem("idx1_ready")
        rows_gathered = [sem(f"rows_gathered{q}") for q in range(2)]
        local1_ready = sem("local1_ready")
        onehot1_ready = sem("onehot1_ready")
        product_ready = sem("product_ready")
        summed1 = sem("summed1")
        acc1_added = sem("acc1_added")
        staged_ready = sem("staged_ready")
        turned_done = sem("turned_done")
        turned_copied = sem("turned_copied")
        linear_done = sem("linear_done")
        node1 = sem("node1")
        std_ready = sem("std_ready")
        out_stored = [sem(f"out_stored{q}") for q in range(2)]

        def tiles(ap, n):
            return ap.rearrange("p (s c) -> p s c", s=n)

        block = ctx.enter_context(nc.Block())

        @block.sync
        def _(sp):
            def as_rows(a):
                return a.rearrange("(p c) -> p c", p=ER)
            sp.dma_start(dst_i, as_rows(dst)).then_inc(edges_in, 16)
            sp.dma_start(src_i, as_rows(src)).then_inc(edges_in, 16)
            sp.dma_start(wgt_f, as_rows(edge_weight)).then_inc(edges_in, 16)
            sp.dma_start(typ_i, as_rows(edge_type)).then_inc(edges_in, 16)
            sp.dma_start(next_dst[0:ER - 1, :], as_rows(dst)[1:ER, 0:1], allow_slow_non_contiguous=True).then_inc(edges_in, 16)
            sp.dma_start(tiles(nodes[:, 0:(NB - 1) * C], NB - 1),
                         x[0:(NB - 1) * P, :].rearrange("(b p) c -> p b c", p=P)).then_inc(x_in, 16)
            sp.wait_ge(tail_zero, 1)
            sp.dma_start(nodes[0:LAST, (NB - 1) * C:NB * C], x[(NB - 1) * P:N, :]).then_inc(x_tail_in, 16)
            sp.wait_ge(acc0_zero, 1)
            for k in range(COPIES):
                sp.dma_start(sum_dram[k].rearrange("(p r) c -> p (r c)", p=P),
                             acc0[:, 0:ROWS // P * W0]).then_inc(zeroed, 16)
            sp.wait_ge(tables_ready, 1)
            sp.wait_ge(rec_ready, 1)
            with sp.Fori(0, PAIRS) as i:
                for s in range(2 * UNROLL):
                    off = sp.value_load(tile_offset[0:1, ds(i * (2 * UNROLL) + s, 1)], min_val=0, max_val=E)
                    sp.dma_start(records[:, ds(i * (8 * UNROLL) + 4 * s, 4)],
                                 rec_dram[ds(off, P), :]).then_inc(rec_in, 16)
                sp.wait_ge(rec_in, i * (32 * UNROLL) + 32 * UNROLL)
                sp.sem_inc(wait_holder, 1)

            sp.wait_ge(added, G * UNROLL * 16)

            def load_sums(b, q):
                for k in range(COPIES):
                    sp.dma_start(sums4[q][:, k * W0:(k + 1) * W0], sum_dram[k][ds(b * P, P), :]).then_inc(sums_in[q], 16)

            def store_h(b, q, n):
                sp.wait_ge(h_built, n + 2)
                sp.dma_start(h_dram[ds(b * P, P), :], h_rows[q]).then_inc(h_stored[q], 16)

            load_sums(0, 0)
            load_sums(1, 1)
            with sp.Fori(0, (NB - 1) // 2 - 1) as i:
                for q in range(2):
                    store_h(i * 2 + q, q, i * 2 + q + 1)
                    load_sums(i * 2 + q + 2, q)
            for q in range(2):
                store_h(NB - 3 + q, q, NB - 2 + q)
                if q == 0:
                    load_sums(NB - 1, 0)
            store_h(NB - 1, 0, NB)

            def store_out(b, q, n, rows=P):
                sp.wait_ge(node1, 8 * n)
                sp.dma_start(out[ds(b * P, rows), :], y_out[q][0:rows, :]).then_inc(out_stored[q], 16)
            with sp.Fori(0, (NB - 1) // 2) as i:
                for q in range(2):
                    store_out(i * 2 + q, q, i * 2 + q + 1)
            store_out(NB - 1, 0, NB, LAST)
            sp.wait_ge(out_stored[0], 16 * ((NB + 1) // 2))
            sp.wait_ge(out_stored[1], 16 * (NB // 2))

        @block.gpsimd
        def _(pool):
            pool.iota(iota_free[:, :], pattern=[[1, P]], base=0, channel_multiplier=0,
                      allow_small_or_imprecise_dtypes=True).then_inc(const_iota, 1)
            pool.iota(iota_part[:, :], pattern=[[1, 1]], base=0, channel_multiplier=1,
                      allow_small_or_imprecise_dtypes=True).then_inc(const_iota, 1)
            pool.iota(spare[:, :], pattern=[[1, 1]], base=N, channel_multiplier=1,
                      allow_small_or_imprecise_dtypes=True).then_inc(const_iota, 1)
            pool.iota(limits[:, :], pattern=[[P, NBX + 1]], base=0, channel_multiplier=0,
                      allow_small_or_imprecise_dtypes=True).then_inc(const_iota, 1)
            pool.iota(iota_t, pattern=[[1, T]], base=0, channel_multiplier=0,
                      allow_small_or_imprecise_dtypes=True).then_inc(const_iota, 1)
            pool.memset(nodes[:, (NB - 1) * C:NBX * C], 0.0).then_inc(tail_zero, 1)
            pool.memset(pad_rec[:, 0:1], float(2 * NBX * P)).then_inc(const_iota, 1)
            pool.memset(pad_rec[:, 1:4], 0.0).then_inc(const_iota, 1)
            pool.wait_ge(const_iota, 7)
            pool.dma_start(rec_dram[E:E + P, :], pad_rec[:, :]).then_inc(pad_stored, 16)

            pool.wait_ge(rel_ready, 1)
            pool.dma_start(r_dram.rearrange("(k p) c -> p k c", p=RT),
                           tiles(rel_out[0:RT, :], RK)).then_inc(rel_stored, 16)

            pool.wait_ge(rec_built, 4)
            pool.wait_ge(disorder_set, 1)
            unsorted = pool.value_load(disorder[0:1, 0:1], min_val=0, max_val=2 * E)
            with pool.If(unsorted < 1):
                pool.dma_start(rec_dram[0:E, :].rearrange("(p c) f -> p (c f)", p=ER), rec4).then_inc(rec_stored, 16)
                pool.wait_ge(rec_stored, 16)
            with pool.Else():
                pool.wait_ge(pos_ready, 1)
                with pool.Fori(0, EC // FB) as j:
                    pool.tensor_copy(fb_idx[0:ER, :], pos_i[:, ds(j * FB, FB)]).then_inc(fb_copied, 1)
                    pool.tensor_copy(fb_rec[0:ER, :], rec4[:, ds(j * (4 * FB), 4 * FB)]).then_inc(fb_copied, 1)
                    pool.wait_ge(fb_copied, j * 2 + 2)
                    pool.sem_inc(wait_holder, 1)
                    for s in range(FB):
                        pool.indirect_dma_start(rec_dram[0:E, :], bass.IndirectOffsetOnAxis(ap=fb_idx[0:ER, s:s + 1], axis=0),
                                                fb_rec[0:ER, 4 * s:4 * s + 4], None).then_inc(rec_stored, 16)
                    pool.wait_ge(rec_stored, j * (16 * FB) + 16 * FB)
                    pool.sem_inc(wait_holder, 1)
            pool.wait_ge(pad_stored, 16)
            pool.sem_inc(rec_ready, 1)

            def gathers(n, q):
                pool.wait_ge(idx_ready, n)
                pool.wait_ge(summed, n)
                pool.sem_inc(wait_holder, 1)
                for s in range(UNROLL):
                    pool.indirect_dma_start(xg[q][:, s * H:(s + 1) * H], None, x_halves,
                                            bass.IndirectOffsetOnAxis(ap=gather_idx[q][:, s:s + 1], axis=0)
                                            ).then_inc(x_gathered[q], 16)

            def scatters(n, q, first=False):
                pool.wait_ge(scatter_idx_ready, n)
                pool.wait_ge(degree_ready, n)
                pool.wait_ge(combined_copied, n)
                if not first:
                    pool.wait_ge(added, (n - 1) * (16 * UNROLL))
                pool.sem_inc(wait_holder, 1)
                for s in range(UNROLL):
                    pool.indirect_dma_start(sum_dram[s], bass.IndirectOffsetOnAxis(ap=scatter_idx[q][:, s:s + 1], axis=0),
                                            combined[q][:, s * W0:(s + 1) * W0], None,
                                            compute_op=ALU.add).then_inc(added, 16)

            gathers(1, 0)
            pool.wait_ge(zeroed, 16 * COPIES)
            gathers(2, 1)
            scatters(1, 0, first=True)
            with pool.Fori(1, PAIRS) as i:
                gathers(i * 2 + 1, 0)
                scatters(i * 2, 1)
                gathers(i * 2 + 2, 1)
                scatters(i * 2 + 1, 0)
            scatters(G, 1)

            pool.wait_ge(rel_stored, 16)
            pool.wait_ge(h_stored[0], 16 * ((NB + 1) // 2))
            pool.wait_ge(h_stored[1], 16 * (NB // 2))

            with pool.Fori(0, PAIRS) as i:
                for q in range(2):
                    n = i * 2 + (q + 1)
                    pool.wait_ge(idx1_ready, n)
                    pool.wait_ge(product_ready, n)
                    pool.sem_inc(wait_holder, 1)
                    for s in range(UNROLL):
                        pool.indirect_dma_start(hg[q][:, s * W1:(s + 1) * W1], None, h_dram,
                                                bass.IndirectOffsetOnAxis(ap=gather_idx[q][:, s:s + 1], axis=0)
                                                ).then_inc(rows_gathered[q], 16)
                        pool.indirect_dma_start(rg[q][:, s * W1:(s + 1) * W1], None, r_dram,
                                                bass.IndirectOffsetOnAxis(ap=type_idx[q][:, s:s + 1], axis=0)
                                                ).then_inc(rows_gathered[q], 16)

        @block.scalar
        def _(act):
            def blocks(w):
                return [[w[0], w[1], w[2], w[3]], [w[1], w[0], w[3], w[2]],
                        [w[2], w[3], w[0], w[1]], [w[3], w[2], w[1], w[0]]]
            for m, w in enumerate((msg_w, upd_w)):
                for o, line in enumerate(blocks(w)):
                    for c, piece in enumerate(line):
                        p0, c0 = (o % 2) * CB, (2 * m + o // 2) * C + c * CB
                        act.dma_start(w_nat[p0:p0 + CB, c0:c0 + CB], piece).then_inc(weights_in, 16)
            act.dma_start(tiles(rel_sb[0:RT, :], RK), rel.rearrange("(k p) c -> p k c", p=RT)).then_inc(weights_in, 16)
            act.dma_start(gate_wb[:, :], gate_w.broadcast_to([P, C])).then_inc(weights_in, 16)
            act.dma_start(gate_bb[:, :], gate_b.rearrange("(a b) -> a b", b=1).broadcast_to([P, 1])).then_inc(weights_in, 16)
            act.dma_start(bias_raw[:, :], upd_b.rearrange("(a b) c -> a (b c)", a=1).broadcast_to([P, C])
                          ).then_inc(weights_in, 16)
            act.dma_start(bias_col[:, :], msg_b.rearrange("(k b) c -> (b c) k", k=2), allow_slow_non_contiguous=True).then_inc(weights_in, 16)
            n_weights = 16 * (2 * B4 * B4 + 5)
            act.wait_ge(weights_in, n_weights)
            for m in range(2):
                for o, c in ((0, 3), (1, 2), (2, 3)):
                    p0, c0 = (o % 2) * CB, (2 * m + o // 2) * C + c * CB
                    act.mul(w_nat[p0:p0 + CB, c0:c0 + CB], w_nat[p0:p0 + CB, c0:c0 + CB], -1.0).then_inc(negated, 1)
            for k in range(2):
                act.wait_ge(prep_pe, 1 + k)
                act.copy(upd_t[:, k * C:(k + 1) * C].rearrange("p (c b) -> p b c", b=B4),
                         bank[6 + k][:, 0:C].rearrange("p (b c) -> p b c", b=B4)).then_inc(fold_ready, 1)
            for k in range(2):
                act.wait_ge(prep_pe, 3 + k)
                act.copy(both_t[:, k * C:(k + 1) * C], bank[6 + k][:, 0:C]).then_inc(fold_ready, 1)
            act.wait_ge(prep_pe, 5)
            act.copy(msg_bias[:, :], bank[5][:, 0:C]).then_inc(fold_ready, 1)

            act.wait_ge(gate_lin, RK + 1)
            act.activation(gate[0:RT, :], gate_z[0:RT, :], ACT.Sigmoid, bias=gate_bb[0:RT, :]).then_inc(gate_ready, 1)

            def rec_col(i, q, f):
                return records[:, ds(i * (8 * UNROLL) + 4 * UNROLL * q, 4 * UNROLL)].rearrange(
                    "p (s f) -> p s f", f=4)[:, :, f]

            def indices(i, q, peel):
                act.wait_ge(rec_in, i * (32 * UNROLL) + 32 * UNROLL)
                if not peel:
                    act.wait_ge(x_gathered[q], i * (16 * UNROLL))
                act.activation(gather_idx[q][:, :], rec_col(i, q, 1), ACT.Copy, scale=2.0, bias=1.0).then_inc(idx_ready, 1)

            def copies(i, q, peel):
                n = i * 2 + (q + 1)
                act.wait_ge(spread_done, n)
                act.copy(spread_sb, bank[1][:, :]).then_inc(spread_copied, 1)
                act.wait_ge(combined_done, n)
                if not peel:
                    act.wait_ge(added, (n - 2) * (16 * UNROLL))
                act.copy(tiles(combined[q], UNROLL)[:, :, 0:H], tiles(bank[2][:, :], UNROLL)).then_inc(combined_copied, 1)

            indices(0, 0, True)
            indices(0, 1, True)
            copies(0, 0, True)
            indices(1, 0, False)
            copies(0, 1, True)
            with act.Fori(1, PAIRS - 1) as i:
                indices(i, 1, False)
                copies(i, 0, False)
                indices(i + 1, 0, False)
                copies(i, 1, False)
            indices(PAIRS - 1, 1, False)
            copies(PAIRS - 1, 0, False)
            copies(PAIRS - 1, 1, False)

            act.sem_inc(roots_ready, 2)
            act.sem_inc(h_built, 2)

            def node_roots(b, q, n, i):
                act.wait_ge(node0, n * 8 - 8 + 3)
                act.activation(roots[:, 0:2], deg[:, :], ACT.Sqrt).then_inc(roots_ready, 1)
                act.wait_ge(node0, n * 8 - 8 + 6)
                act.activation(roots[:, 2:3], mean_var[:, 1:2], ACT.Sqrt, bias=eps_col[:, :]).then_inc(roots_ready, 1)
                act.wait_ge(node0, n * 8)
                if i is not None:
                    act.wait_ge(h_stored[q], i * 16)
                act.mul(h_rows[q][:, 0:C], nodes[:, ds(b * C, C)], rroots[q][:, 0:1])
                act.copy(h_rows[q][:, C:C + 2], rroots[q][:, 0:2]).then_inc(h_built, 1)

            act.wait_ge(rel_stored, 16)
            node_roots(0, 0, 1, None)
            node_roots(1, 1, 2, None)
            with act.Fori(1, (NB - 1) // 2) as i:
                for q in range(2):
                    node_roots(i * 2 + q, q, i * 2 + (q + 1), i)
            node_roots(NB - 1, 0, NB, (NB - 1) // 2)

            def indices1(i, q, peel):
                if not peel:
                    act.wait_ge(rows_gathered[q], i * (32 * UNROLL))
                act.copy(gather_idx[q][:, :], rec_col(i, q, 1))
                act.copy(type_idx[q][:, :], rec_col(i, q, 3)).then_inc(idx1_ready, 1)
            for q in range(2):
                indices1(0, q, True)
            with act.Fori(1, PAIRS) as i:
                for q in range(2):
                    indices1(i, q, False)

            def stage(b, q):
                act.copy(staged[q][:, 0:C], nodes[:, ds(b * C, C)])
                act.copy(staged[q][:, C:2 * C], acc1[:, ds(b * W1, C)]).then_inc(staged_ready, 1)

            def turn(n, q):
                act.wait_ge(turned_done, n)
                act.copy(turned[q][:, :], bank[q][:, :]).then_inc(turned_copied, 1)
                act.wait_ge(node1, n * 8 - 8 + 5)
                act.activation(roots[:, 2:3], mean_var[:, 1:2], ACT.Sqrt, bias=eps_col[:, :]).then_inc(std_ready, 1)
            act.wait_ge(acc1_added, UNROLL * (G + 1))
            stage(0, 0)
            with act.Fori(0, (NB - 1) // 2) as i:
                for q in range(2):
                    stage(i * 2 + (q + 1), 1 - q)
                    turn(i * 2 + (q + 1), q)
            turn(NB, 0)

        @block.vector
        def _(dve):
            count = [0]

            def link(ins):
                count[0] += 1
                ins.then_inc(prep, 1)
                dve.wait_ge(prep, count[0])

            dve.memset(acc0[:, :], 0.0).then_inc(acc0_zero, 1)
            dve.memset(ones[:, :], 1.0).then_inc(const_done, 1)
            dve.memset(ones_bf[:, :], 1.0).then_inc(const_done, 1)
            dve.memset(eps_col[:, :], EPS).then_inc(const_done, 1)
            dve.wait_ge(const_iota, 7)
            dve.tensor_scalar(ident[:, :], iota_free[:, :], iota_part[:, :], None, ALU.is_equal).then_inc(const_done, 1)
            dve.tensor_scalar(earlier[:, :], iota_free[:, :], iota_part[:, :], None, ALU.is_lt).then_inc(const_done, 1)
            dve.tensor_scalar(later[:, :], iota_free[:, :], iota_part[:, :], None, ALU.is_gt).then_inc(const_done, 1)

            dve.wait_ge(edges_in, 80)
            rec_fields = rec4.rearrange("p (c f) -> p f c", f=4)
            link(dve.tensor_copy(dst_f, dst_i))
            dve.tensor_copy(rec_fields[:, 0, :], dst_f).then_inc(rec_built, 1)
            dve.tensor_copy(rec_fields[:, 1, :], src_i).then_inc(rec_built, 1)
            dve.tensor_copy(rec_fields[:, 2, :], wgt_f).then_inc(rec_built, 1)
            dve.tensor_copy(rec_fields[:, 3, :], typ_i).then_inc(rec_built, 1)

            link(dve.memset(cum[:, :], 0.0))
            link(dve.memset(cum[0:ER, NB:NB + 2], float(EC)))
            for b in range(1, NB):
                dve.tensor_scalar(work_a, dst_f, float(b * P), 0.0, ALU.is_lt, ALU.add,
                                  accum_out=cum[0:ER, b:b + 1]).then_inc(counted, 1)
                dve.wait_ge(counted, b)
            link(dve.tensor_tensor(work_a[:, 0:EC - 1], dst_f[:, 0:EC - 1], dst_f[:, 1:EC], ALU.is_gt))
            link(dve.tensor_reduce(cum[0:ER, NBX + 1:NBX + 2], work_a[:, 0:EC - 1], AX_X, ALU.add))
            link(dve.tensor_copy(next_dst_f[0:ER - 1, :], next_dst[0:ER - 1, :]))
            link(dve.tensor_tensor(cum[0:ER - 1, NBX + 2:NBX + 3], dst_f[0:ER - 1, EC - 1:EC], next_dst_f[0:ER - 1, :],
                                   ALU.is_gt))
            link(dve.tensor_tensor(cum[0:ER, NBX + 1:NBX + 2], cum[0:ER, NBX + 1:NBX + 2],
                                   cum[0:ER, NBX + 2:NBX + 3], ALU.add))
            dve.tensor_tensor(bucket[0:ER, :], cum[0:ER, 1:NBX + 1], cum[0:ER, 0:NBX], ALU.subtract).then_inc(counted, 1)

            dve.wait_ge(prep_pe, 6)
            dve.tensor_copy(disorder[:, :], bank[4][0:1, 2:3]).then_inc(disorder_set, 1)
            link(dve.tensor_copy(starts[0:NBX, 0:2], bank[4][0:NBX, 0:2]))
            link(dve.tensor_tensor(starts[0:NBX, 2:3], starts[0:NBX, 1:2], starts[0:NBX, 0:1], ALU.subtract))
            link(dve.tensor_scalar(starts_i[0:NBX, 0:1], starts[0:NBX, 2:3], float(P - 1), None, ALU.add))
            link(dve.tensor_scalar(starts_i[0:NBX, 1:2], starts_i[0:NBX, 0:1], P.bit_length() - 1, None,
                                   ALU.arith_shift_right))
            dve.tensor_copy(starts[0:NBX, 3:4], starts_i[0:NBX, 1:2]).then_inc(starts_done, 1)
            dve.wait_ge(prep_pe, 7)
            link(dve.tensor_copy(starts[0:NBX, 4:5], bank[4][0:NBX, 8:9]))
            link(dve.tensor_scalar(starts[0:NBX, 5:6], starts[0:NBX, 4:5], -float(P), None, ALU.mult))
            link(dve.tensor_tensor(starts[0:NBX, 5:6], starts[0:NBX, 5:6], starts[0:NBX, 0:1], ALU.add))
            link(dve.tensor_scalar(starts[0:NBX, 6:7], iota_part[0:NBX, :], float(NB), float(T), ALU.is_ge, ALU.mult))
            link(dve.tensor_tensor(starts[0:NBX, 6:7], starts[0:NBX, 6:7], starts[0:NBX, 3:4], ALU.add))
            link(dve.tensor_tensor(starts[0:NBX, 6:7], starts[0:NBX, 6:7], starts[0:NBX, 4:5], ALU.add))
            link(dve.tensor_scalar(starts[0:NBX, 7:8], iota_part[0:NBX, :], float(P), None, ALU.mult))
            link(dve.tensor_scalar(below_next, iota_t[0:NBX, :], starts[0:NBX, 6:7], None, ALU.is_lt))
            dve.scalar_tensor_tensor(out=in_block, in0=iota_t[0:NBX, :], scalar=starts[0:NBX, 4:5], in1=below_next,
                                     op0=ALU.is_ge, op1=ALU.mult).then_inc(table_sel, 1)
            dve.wait_ge(prep_pe, 8)
            TH = T // 2
            off_f = acc1[0:1, 11 * EC:11 * EC + T]
            for k in range(2):
                sl = slice(k * TH, (k + 1) * TH)
                link(dve.tensor_copy(tile_base[:, sl], bank[4 + 2 * k][:, 0:TH]))
                link(dve.scalar_tensor_tensor(out=off_f[:, sl], in0=iota_t[0:1, sl], scalar=float(P),
                                              in1=bank[5 + 2 * k][0:1, 0:TH], op0=ALU.mult, op1=ALU.add))
            link(dve.tensor_scalar(tile_offset[:, :], off_f, float(E), None, ALU.min))
            dve.tensor_scalar(tile_block[:, :], tile_base[0:1, :], 1.0 / P, None, ALU.mult).then_inc(tables_ready, 1)

            dve.wait_ge(weights_in, 16 * (2 * B4 * B4 + 5))
            link(dve.memset(rel_out[0:RT, :], 0.0))
            for k in range(RK):
                dve.tensor_tensor(rel_out[0:RT, k * W1:k * W1 + C].rearrange("p (b c) -> p b c", b=B4),
                                  rel_sb[0:RT, k * C:(k + 1) * C].rearrange("p (b c) -> p b c", b=B4),
                                  gate_wb[0:RT, :].rearrange("p (c b) -> p b c", b=B4), ALU.mult).then_inc(gate_lin, 1)
            dve.wait_ge(gate_lin, RK)
            dve.tensor_reduce(gate_z[0:RT, :], tiles(rel_out[0:RT, :], RK), AX_X, ALU.add).then_inc(gate_lin, 1)
            dve.wait_ge(gate_ready, 1)
            for k in range(RK):
                link(dve.tensor_scalar(rel_out[0:RT, k * W1:k * W1 + C], rel_sb[0:RT, k * C:(k + 1) * C],
                                       gate[0:RT, k:k + 1], None, ALU.mult))
            dve.tensor_copy(tiles(rel_out[0:RT, :], RK)[:, :, C:C + 1].rearrange("p k a -> p (k a)"),
                            gate[0:RT, :]).then_inc(rel_ready, 1)
            link(dve.tensor_copy(upd_bias[:, :].rearrange("p (c b) -> p b c", b=B4),
                                 bias_raw[:, :].rearrange("p (b c) -> p b c", b=B4)))

            unsorted = dve.value_load(disorder[0:1, 0:1], min_val=0, max_val=2 * E)
            with dve.If(unsorted > 0):
                dve.wait_ge(prep_pe, 9)
                dve.tensor_copy(first_pos[0:ER, :], bank[3][0:ER, 0:NBX]).then_inc(counted, 1)
                dve.wait_ge(counted, NB + 1)
                dve.memset(pos, -1.0).then_inc(counted, 1)
                with dve.Fori(0, NB) as b:
                    base = b * 5 + (NB + 2)
                    dve.tensor_scalar(work_b, dst_f, limits[0:ER, ds(b, 1)], None, ALU.is_ge).then_inc(counted, 1)
                    dve.wait_ge(counted, base + 1)
                    dve.scalar_tensor_tensor(out=work_b, in0=dst_f, scalar=limits[0:ER, ds(b + 1, 1)], in1=work_b,
                                             op0=ALU.is_lt, op1=ALU.mult).then_inc(counted, 1)
                    dve.wait_ge(counted, base + 2)
                    dve.tensor_tensor_scan(work_c, ones[0:ER, 0:1].broadcast_to([ER, EC]), work_b,
                                           first_pos[0:ER, ds(b, 1)], ALU.mult, ALU.add).then_inc(counted, 1)
                    dve.wait_ge(counted, base + 3)
                    dve.tensor_tensor(work_c, work_c, work_b, ALU.mult).then_inc(counted, 1)
                    dve.wait_ge(counted, base + 4)
                    dve.tensor_tensor(pos, pos, work_c, ALU.add).then_inc(counted, 1)
                    dve.wait_ge(counted, base + 5)
                dve.tensor_copy(pos_i, pos).then_inc(pos_ready, 1)

            for q in range(2):
                link(dve.memset(combined[q], 0.0))
            dve.wait_ge(zeroed, 16 * COPIES)
            dve.wait_ge(x_in, 16)
            dve.wait_ge(x_tail_in, 16)

            def field(i, q, f):
                return records[:, ds(i * (8 * UNROLL) + 4 * UNROLL * q, 4 * UNROLL)].rearrange(
                    "p (s f) -> p s f", f=4)[:, :, f]

            def bcast(ap):
                return ap.unsqueeze(2).broadcast_to([P, UNROLL, P])

            def every(ap):
                return ap.unsqueeze(1).broadcast_to([P, UNROLL, P])

            def edges0(i, q, peel):
                n = i * 2 + (q + 1)
                dve.wait_ge(rec_in, i * (32 * UNROLL) + 32 * UNROLL)
                dve.tensor_tensor(local[q][:, :], field(i, q, 0),
                                  tile_base[:, ds(i * (2 * UNROLL) + q * UNROLL, UNROLL)],
                                  ALU.subtract).then_inc(local_ready, 1)
                dve.wait_ge(local_ready, n)
                dve.wait_ge(summed, n)
                dve.tensor_tensor(tiles(onehot[q][:, :], UNROLL), every(iota_free[:, :]), bcast(local[q][:, :]),
                                  ALU.is_equal).then_inc(onehot_ready, 1)
                dve.tensor_scalar(not_neg[:, :], local[q][:, :], 0.0, None, ALU.is_ge).then_inc(not_neg_ready, 1)
                dve.wait_ge(not_neg_ready, n)
                dve.scalar_tensor_tensor(out=valid[:, :], in0=local[q][:, :], scalar=float(P), in1=not_neg[:, :],
                                         op0=ALU.is_lt, op1=ALU.mult).then_inc(valid_ready, 1)
                dve.wait_ge(valid_ready, n)
                dve.scalar_tensor_tensor(out=src_rel[:, :], in0=field(i, q, 1), scalar=spare[:, :], in1=valid[:, :],
                                         op0=ALU.subtract, op1=ALU.mult).then_inc(src_rel_ready, 1)
                dve.wait_ge(src_rel_ready, n)
                dve.tensor_scalar(src_key[q][:, :], src_rel[:, :], spare[:, :], None, ALU.add).then_inc(key_ready, 1)
                dve.wait_ge(onehot_ready, n)
                dve.tensor_tensor(tiles(onehot_w[q][:, :], UNROLL), tiles(onehot[q][:, :], UNROLL),
                                  bcast(field(i, q, 2)), ALU.mult).then_inc(onehot_w_ready, 1)
                dve.wait_ge(key_ready, n)
                dve.wait_ge(keys_spread, n)
                dve.tensor_tensor(tiles(same, UNROLL), tiles(bank[0][:, :], UNROLL), bcast(src_key[q][:, :]),
                                  ALU.is_equal).then_inc(same_ready, 1)
                dve.wait_ge(same_ready, n)
                dve.tensor_tensor(tiles(same_earlier, UNROLL), tiles(same, UNROLL), every(earlier[:, :]),
                                  ALU.mult).then_inc(same_earlier_ready, 1)
                if not peel:
                    dve.wait_ge(added, (n - 2) * (16 * UNROLL))
                dve.tensor_reduce(tiles(combined[q], UNROLL)[:, :, H], tiles(same, UNROLL), AX_X,
                                  ALU.add).then_inc(degree_ready, 1)
                dve.wait_ge(same_earlier_ready, n)
                dve.tensor_reduce(n_earlier[:, :], tiles(same_earlier, UNROLL), AX_X, ALU.add).then_inc(n_earlier_ready, 1)
                dve.wait_ge(n_earlier_ready, n)
                dve.scalar_tensor_tensor(out=first_rel[:, :], in0=n_earlier[:, :], scalar=0.0, in1=src_rel[:, :],
                                         op0=ALU.is_equal, op1=ALU.mult).then_inc(first_ready, 1)
                dve.wait_ge(first_ready, n)
                dve.tensor_scalar(scatter_idx[q][:, :], first_rel[:, :], spare[:, :], None,
                                  ALU.add).then_inc(scatter_idx_ready, 1)
                dve.wait_ge(summed, n + 2)
                for s in range(UNROLL):
                    b = dve.value_load(tile_block[0:1, ds(i * (2 * UNROLL) + q * UNROLL + s, 1)], min_val=0, max_val=NB)
                    here = acc0[:, ds(b * W0, H + 1)]
                    dve.wait_ge(acc0_added, n * UNROLL + s)
                    dve.tensor_tensor(here, here, bank[3 + s // 2][:, (s % 2) * C:(s % 2) * C + H + 1],
                                      ALU.add).then_inc(acc0_added, 1)

            dve.sem_inc(acc0_added, UNROLL)
            for q in range(2):
                edges0(0, q, True)
            with dve.Fori(1, PAIRS) as i:
                for q in range(2):
                    edges0(i, q, False)

            dve.memset(acc1[:, :], 0.0).then_inc(acc1_zero, 1)
            dve.wait_ge(acc0_added, UNROLL * (G + 1))

            def nodes0(b, q, n, i):
                def at(k):
                    return n * 8 - 8 + k
                dve.wait_ge(sums_in[q], i * (16 * COPIES) + 16 * COPIES)
                dve.tensor_reduce(sums[:, :], sums4[q].rearrange("p (k c) -> p c k", k=COPIES), AX_X,
                                  ALU.add).then_inc(node0, 1)
                dve.wait_ge(node0, at(1))
                dve.wait_ge(roots_ready, n * 2)
                dve.tensor_scalar(deg[:, 0:1], sums[:, H:H + 1], 1.0, None, ALU.max).then_inc(node0, 1)
                dve.tensor_scalar(deg[:, 1:2], acc0[:, ds(b * W0 + H, 1)], 1.0, None, ALU.max).then_inc(node0, 1)
                dve.wait_ge(node0, at(3))
                dve.reciprocal(rdeg[:, :], deg[:, :]).then_inc(rdeg_ready, 1)
                dve.wait_ge(rdeg_ready, n)
                dve.scalar_tensor_tensor(out=y_node[:, 0:H], in0=sums[:, 0:H], scalar=rdeg[:, 0:1],
                                         in1=nodes[:, ds(b * C, H)], op0=ALU.mult, op1=ALU.add).then_inc(y_ready, 1)
                dve.scalar_tensor_tensor(out=y_node[:, H:C], in0=acc0[:, ds(b * W0, H)], scalar=rdeg[:, 1:2],
                                         in1=nodes[:, ds(b * C + H, H)], op0=ALU.mult, op1=ALU.add).then_inc(y_ready, 1)
                dve.wait_ge(y_ready, n * 2)
                dve.bn_stats(stats[:, :], y_node[:, :]).then_inc(node0, 1)
                dve.wait_ge(node0, at(4))
                dve.sem_inc(wait_holder, 1)
                dve.bn_aggr(mean_var[:, :], stats[:, :]).then_inc(node0, 2)
                dve.wait_ge(roots_ready, n * 2 + 2)
                dve.wait_ge(h_built, n)
                dve.reciprocal(rroots[q][:, :], roots[:, :]).then_inc(node0, 1)
                dve.wait_ge(node0, at(7))
                dve.tensor_copy(dst_scale[:, ds(b, 1)], rroots[q][:, 1:2]).then_inc(dst_scale_set, 1)
                dve.tensor_scalar(nodes[:, ds(b * C, C)], y_node[:, :], mean_var[:, 0:1], rroots[q][:, 2:3],
                                  ALU.subtract, ALU.mult).then_inc(node0, 1)
                dve.wait_ge(node0, at(8))

            with dve.Fori(0, (NB - 1) // 2) as i:
                for q in range(2):
                    nodes0(i * 2 + q, q, i * 2 + (q + 1), i)
            nodes0(NB - 1, 0, NB, (NB - 1) // 2)
            dve.wait_ge(acc1_zero, 1)

            def edges1(i, q):
                n = i * 2 + (q + 1)
                dve.tensor_tensor(local[q][:, :], field(i, q, 0),
                                  tile_base[:, ds(i * (2 * UNROLL) + q * UNROLL, UNROLL)],
                                  ALU.subtract).then_inc(local1_ready, 1)
                dve.wait_ge(local1_ready, n)
                dve.wait_ge(summed1, n)
                dve.tensor_tensor(tiles(onehot_w[q][:, :], UNROLL), every(iota_free[:, :]), bcast(local[q][:, :]),
                                  ALU.is_equal).then_inc(onehot1_ready, 1)
                dve.wait_ge(rows_gathered[q], i * (32 * UNROLL) + 32 * UNROLL)
                dve.tensor_tensor(product[q][:, :], hg[q], rg[q], ALU.mult).then_inc(product_ready, 1)
                dve.wait_ge(summed1, n + 2)
                for s in range(UNROLL):
                    b = dve.value_load(tile_block[0:1, ds(i * (2 * UNROLL) + q * UNROLL + s, 1)], min_val=0, max_val=NB)
                    here = acc1[:, ds(b * W1, C + 1)]
                    dve.wait_ge(acc1_added, n * UNROLL + s)
                    dve.tensor_tensor(here, here, bank[4 * q + s][:, 0:C + 1], ALU.add).then_inc(acc1_added, 1)

            dve.sem_inc(product_ready, 2)
            dve.sem_inc(acc1_added, UNROLL)
            with dve.Fori(0, PAIRS) as i:
                for q in range(2):
                    edges1(i, q)

            def nodes1(b, q, n, i):
                def at(k):
                    return n * 8 - 8 + k
                dve.tensor_tensor(x_bias[:, :], nodes[:, ds(b * C, C)], upd_bias[:, :], ALU.add).then_inc(node1, 1)
                dve.wait_ge(linear_done, n)
                dve.scalar_tensor_tensor(out=agg_part[:, :], in0=msg_bias[:, :], scalar=acc1[:, ds(b * W1 + C, 1)],
                                         in1=bank[4 + q][:, 0:C], op0=ALU.mult, op1=ALU.add).then_inc(node1, 1)
                dve.wait_ge(node1, at(2))
                dve.scalar_tensor_tensor(out=agg_part[:, :], in0=agg_part[:, :], scalar=dst_scale[:, ds(b, 1)],
                                         in1=bank[2 + q][:, 0:C], op0=ALU.mult, op1=ALU.add).then_inc(node1, 1)
                dve.wait_ge(node1, at(3))
                dve.tensor_tensor(y_node[:, :], agg_part[:, :], x_bias[:, :], ALU.add).then_inc(y1_ready, 1)
                dve.wait_ge(y1_ready, n)
                dve.bn_stats(stats[:, :], y_node[:, :]).then_inc(node1, 1)
                dve.wait_ge(node1, at(4))
                dve.sem_inc(wait_holder, 1)
                dve.bn_aggr(mean_var[:, :], stats[:, :]).then_inc(node1, 1)
                dve.wait_ge(std_ready, n)
                dve.reciprocal(rroots[q][:, 2:3], roots[:, 2:3]).then_inc(node1, 2)
                dve.wait_ge(node1, at(7))
                if i is not None:
                    dve.wait_ge(out_stored[q], i * 16)
                dve.tensor_scalar(y_out[q][:, :], y_node[:, :], mean_var[:, 0:1], rroots[q][:, 2:3],
                                  ALU.subtract, ALU.mult).then_inc(node1, 1)
                dve.wait_ge(node1, at(8))

            dve.wait_ge(fold_ready, 5)
            nodes1(0, 0, 1, None)
            nodes1(1, 1, 2, None)
            with dve.Fori(1, (NB - 1) // 2) as i:
                for q in range(2):
                    nodes1(i * 2 + q, q, i * 2 + (q + 1), i)
            nodes1(NB - 1, 0, NB, (NB - 1) // 2)

        @block.tensor
        def _(pe):
            pe.wait_ge(const_done, 6)
            pe.wait_ge(weights_in, 16 * (2 * B4 * B4 + 5))
            pe.wait_ge(negated, 6)
            for k in range(2):
                for o in range(2):
                    mm = pe.transpose(bank[6 + k][:, o * P:(o + 1) * P],
                                      w_nat[:, (2 + o) * C + k * P:(2 + o) * C + (k + 1) * P], ident[:, :])
                mm.then_inc(prep_pe, 1)
            pe.wait_ge(fold_ready, 2)
            for k in range(2):
                for o in range(2):
                    mm = pe.matmul(bank[6 + k][:, 0:C], w_nat[:, o * C + k * P:o * C + (k + 1) * P],
                                   upd_t[:, o * C:(o + 1) * C], start=(o == 0), stop=(o == 1))
                mm.then_inc(prep_pe, 1)
            for o in range(2):
                mm = pe.matmul(bank[5][:, 0:C], bias_col[:, o:o + 1].broadcast_to([P, P]),
                               upd_t[:, o * C:(o + 1) * C], start=(o == 0), stop=(o == 1))
            mm.then_inc(prep_pe, 1)

            pe.wait_ge(counted, NB)
            pe.matmul(bank[4][0:NBX, 0:1], cum[0:ER, 0:NBX], ones[0:ER, 0:1], start=True, stop=True)
            pe.matmul(bank[4][0:NBX, 1:2], cum[0:ER, 1:NBX + 1], ones[0:ER, 0:1], start=True, stop=True)
            pe.matmul(bank[4][0:1, 2:3], cum[0:ER, NBX + 1:NBX + 2], ones[0:ER, 0:1], start=True,
                      stop=True).then_inc(prep_pe, 1)
            pe.wait_ge(starts_done, 1)
            pe.matmul(bank[4][0:NBX, 8:9], later[0:NBX, 0:NBX], starts[0:NBX, 3:4], start=True,
                      stop=True).then_inc(prep_pe, 1)
            pe.wait_ge(table_sel, 1)
            pe.wait_ge(fold_ready, 5)
            TH = T // 2
            for k in range(2):
                for f in range(2):
                    mm = pe.matmul(bank[4 + 2 * k + f][:, 0:TH],
                                   starts[0:NBX, (7, 5)[f]:(7, 5)[f] + 1].broadcast_to([NBX, P]),
                                   in_block[:, k * TH:(k + 1) * TH], start=True, stop=True)
            mm.then_inc(prep_pe, 1)
            pe.matmul(bank[3][0:ER, 0:NBX], later[0:ER, 0:ER], bucket[0:ER, :], start=True, stop=False)
            pe.matmul(bank[3][0:ER, 0:NBX], ones[0:ER, 0:ER], cum[0:ER, 0:NBX], start=False,
                      stop=True).then_inc(prep_pe, 1)

            pe.sem_inc(summed, 2)
            pe.wait_ge(x_in, 16)
            pe.wait_ge(x_tail_in, 16)
            pe.wait_ge(tables_ready, 1)
            with pe.Fori(0, PAIRS) as i:
                for q in range(2):
                    n = i * 2 + (q + 1)
                    pe.wait_ge(key_ready, n)
                    for s in range(UNROLL):
                        mm = pe.matmul(bank[0][:, s * P:(s + 1) * P], src_key[q][:, s:s + 1].broadcast_to([P, P]),
                                       ident[:, :], start=True, stop=True)
                    mm.then_inc(keys_spread, 1)
                    pe.wait_ge(onehot_w_ready, n)
                    pe.wait_ge(same_ready, n)
                    for s in range(UNROLL):
                        mm = pe.matmul(bank[1][:, s * P:(s + 1) * P], onehot_w[q][:, s * P:(s + 1) * P],
                                       same[:, s * P:(s + 1) * P], start=True, stop=True)
                    mm.then_inc(spread_done, 1)
                    pe.wait_ge(x_gathered[q], i * (16 * UNROLL) + 16 * UNROLL)
                    pe.wait_ge(acc0_added, n * UNROLL)
                    for s in range(UNROLL):
                        c0 = (s % 2) * C
                        pe.matmul(bank[3 + s // 2][:, c0:c0 + H], onehot_w[q][:, s * P:(s + 1) * P],
                                  xg[q][:, s * H:(s + 1) * H], start=True, stop=True)
                        mm = pe.matmul(bank[3 + s // 2][:, c0 + H:c0 + H + 1], onehot[q][:, s * P:(s + 1) * P],
                                       ones_bf[:, :], start=True, stop=True)
                    mm.then_inc(summed, 1)
                    pe.wait_ge(spread_copied, n)
                    for s in range(UNROLL):
                        b = pe.value_load(tile_block[0:1, ds(i * (2 * UNROLL) + q * UNROLL + s, 1)], min_val=0, max_val=NB)
                        mm = pe.matmul(bank[2][:, s * P:(s + 1) * P], spread_sb[:, s * P:(s + 1) * P],
                                       nodes[:, ds(b * C, H)], start=True, stop=True)
                    mm.then_inc(combined_done, 1)

            pe.sem_inc(summed1, 2)
            with pe.Fori(0, PAIRS) as i:
                for q in range(2):
                    n = i * 2 + (q + 1)
                    pe.wait_ge(onehot1_ready, n)
                    pe.wait_ge(product_ready, n + 2)
                    pe.wait_ge(acc1_added, n * UNROLL)
                    for s in range(UNROLL):
                        mm = pe.matmul(bank[4 * q + s][:, 0:C + 1], onehot_w[q][:, s * P:(s + 1) * P],
                                       product[q][:, s * W1:s * W1 + C + 1], start=True, stop=True)
                    mm.then_inc(summed1, 1)

            def node_products(b, q, n):
                pe.wait_ge(staged_ready, n)
                for k in range(4):
                    mm = pe.transpose(bank[q][:, k * P:(k + 1) * P], staged[q][:, k * P:(k + 1) * P], ident[:, :])
                mm.then_inc(turned_done, 1)
                pe.wait_ge(turned_copied, n)
                for m, w in enumerate((upd_t, both_t)):
                    for k in range(2):
                        mm = pe.matmul(bank[2 + 2 * m + q][:, 0:C], turned[q][:, (2 * m + k) * P:(2 * m + k + 1) * P],
                                       w[:, k * C:(k + 1) * C], start=(k == 0), stop=(k == 1))
                mm.then_inc(linear_done, 1)

            pe.wait_ge(acc1_added, UNROLL * (G + 1))
            node_products(0, 0, 1)
            node_products(1, 1, 2)
            with pe.Fori(1, (NB - 1) // 2) as i:
                for q in range(2):
                    pe.wait_ge(node1, i * 16 + (8 * q - 13))
                    node_products(i * 2 + q, q, i * 2 + (q + 1))
            pe.wait_ge(node1, 8 * (NB - 3) + 3)
            node_products(NB - 1, 0, NB)


_INS = ['x', 'src', 'dst', 'edge_type_500', 'edge_weight', 'L1_gnn_relation_emb', 'L1_gnn_msg_w', 'L1_gnn_msg_b',
        'L1_gnn_upd_w', 'L1_gnn_upd_b', 'L1_gnn_gate_w', 'L1_gnn_gate_b']


def kernel(**inputs):
    import numpy as _np
    import concourse.bacc as _bacc
    from concourse import mybir as _mybir
    from concourse.bass_utils import run_bass_kernel_spmd as _run

    nc = _bacc.Bacc("TRN2", target_bir_lowering=False, num_devices=1)
    arrays, args = {}, []
    for name in _INS:
        a = _np.ascontiguousarray(inputs[name])
        arrays[f"in_{name}_dram"] = a
        args.append(nc.dram_tensor(f"in_{name}_dram", a.shape, _mybir.dt.from_np(a.dtype), kind="ExternalInput").ap())
    shape = tuple(inputs['x'].shape)
    args.append(nc.dram_tensor("out_0_dram", shape, _mybir.dt.float32, kind="ExternalOutput").ap())
    build_gnn(nc, *args)
    r = _run(nc, [arrays], core_ids=[0])
    return r.results[0]["out_0_dram"]
```

```python
from contextlib import ExitStack

import concourse.bass as bass
from concourse import mybir

ALU = mybir.AluOpType
ACT = mybir.ActivationFunctionType
F32 = mybir.dt.float32
BF16 = mybir.dt.bfloat16
I32 = mybir.dt.int32
AX_X = mybir.AxisListType.X
ds = bass.ds

P = 128
UNROLL = 4
COPIES = UNROLL


def build_gnn(nc, x, src, dst, edge_type, edge_weight, rel, msg_w, msg_b, upd_w, upd_b, gate_w, gate_b, out):
    N, C = x.shape
    H = C // 2
    E = src.shape[0]
    R = rel.shape[0]
    NB = -(-N // P)
    NBX = NB + 1
    LAST = N - (NB - 1) * P
    ER = max(d for d in range(1, P + 1) if E % d == 0)
    EC = E // ER
    T = -(-((E + NB * (P - 1)) // P) // (2 * UNROLL)) * 2 * UNROLL
    G = T // UNROLL
    PAIRS = G // 2
    RT = max(d for d in range(1, P + 1) if R % d == 0)
    RK = R // RT
    W0 = H + 2
    W1 = C + 2
    ROWS = -(-(N + P) // P) * P
    EPS = 1e-5
    B4 = 4
    CB = C // B4
    NCUM = NBX + 3
    FB = 5
    assert EC % FB == 0 and C == 2 * P

    rec_dram = nc.dram_tensor("edge_records", [E + P, 4], F32).ap()
    sum_dram = [nc.dram_tensor(f"source_sums_{k}", [ROWS, W0], F32).ap() for k in range(COPIES)]
    h_dram = nc.dram_tensor("scaled_nodes", [NB * P, W1], F32).ap()
    r_dram = nc.dram_tensor("gated_relations", [R, W1], F32).ap()
    x_halves = x.rearrange("n (h c) -> (n h) c", h=2)

    with ExitStack() as ctx:
        def sb(name, shape, dt):
            return ctx.enter_context(nc.sbuf_tensor(name, shape, dt))

        def sem(name):
            return ctx.enter_context(nc.semaphore(name))

        bank = [ctx.enter_context(nc.psum_tensor(f"bank{k}", [P, 512], F32)) for k in range(8)]

        nodes = sb("nodes", [P, NBX * C], F32)
        acc0 = sb("acc0", [P, NBX * W0], F32)
        acc1 = sb("acc1", [P, NBX * W1], F32)
        records = sb("records", [P, T * 4], F32)
        tile_base = sb("tile_base", [P, T], F32)
        tile_block = sb("tile_block", [1, T], I32)
        tile_offset = sb("tile_offset", [1, T], I32)
        iota_free = sb("iota_free", [P, P], F32)
        iota_part = sb("iota_part", [P, 1], F32)
        spare = sb("spare", [P, 1], F32)
        ident = sb("ident", [P, P], F32)
        earlier = sb("earlier", [P, P], F32)
        later = sb("later", [P, P], F32)
        ones = sb("ones", [P, P], F32)
        ones_bf = sb("ones_bf", [P, 1], BF16)
        dst_scale = sb("dst_scale", [P, NB], F32)
        upd_t = sb("upd_t", [P, 2 * C], F32)
        both_t = sb("both_t", [P, 2 * C], F32)
        msg_bias = sb("msg_bias", [P, C], F32)
        upd_bias = sb("upd_bias", [P, C], F32)

        cum = sb("cum", [P, NCUM], F32)
        bucket = sb("bucket", [P, NBX], F32)
        first_pos = sb("first_pos", [P, NBX], F32)
        limits = sb("limits", [P, NBX + 1], F32)
        next_dst = sb("next_dst", [P, 1], I32)
        next_dst_f = sb("next_dst_f", [P, 1], F32)
        starts = sb("starts", [P, 8], F32)
        starts_i = sb("starts_i", [P, 2], I32)
        disorder = sb("disorder", [1, 1], I32)
        pad_rec = sb("pad_rec", [P, 4], F32)
        fb_idx = sb("fb_idx", [P, FB], I32)
        fb_rec = sb("fb_rec", [P, FB * 4], F32)
        dst_i, src_i, wgt_f, typ_i = (acc1[0:ER, k * EC:(k + 1) * EC] for k in range(4))
        dst_i, src_i, typ_i = dst_i.bitcast(I32), src_i.bitcast(I32), typ_i.bitcast(I32)
        rec4 = acc1[0:ER, 4 * EC:8 * EC]
        dst_f = acc1[0:ER, 8 * EC:9 * EC]
        work_a, work_b, work_c, pos = (acc1[0:ER, k * EC:(k + 1) * EC] for k in range(9, 13))
        pos_i = work_a.bitcast(I32)
        in_block = acc1[0:NBX, 9 * EC:9 * EC + T]
        below_next = acc1[0:NBX, 11 * EC:11 * EC + T]
        iota_t = acc1[:, 13 * EC:13 * EC + T]
        assert 13 * EC + T <= NBX * W1
        w_nat = sb("w_nat", [P, 4 * C], F32)
        gate_wb = sb("gate_wb", [P, C], F32)
        gate_bb = sb("gate_bb", [P, 1], F32)
        gate_z = sb("gate_z", [P, RK], F32)
        gate = sb("gate", [P, RK], F32)
        bias_raw = sb("bias_raw", [P, C], F32)
        bias_col = sb("bias_col", [P, 2], F32)

        ring = sb("ring", [P, 2 * UNROLL * W1 * 2], F32)
        hg = [ring[:, q * UNROLL * W1:(q + 1) * UNROLL * W1] for q in range(2)]
        rg = [ring[:, (2 + q) * UNROLL * W1:(3 + q) * UNROLL * W1] for q in range(2)]
        xg = [ring[:, q * UNROLL * H:(q + 1) * UNROLL * H] for q in range(2)]
        combined = [ring[:, (2 * H + q * W0) * UNROLL:(2 * H + (q + 1) * W0) * UNROLL] for q in range(2)]
        same = ring[:, 2 * (H + W0) * UNROLL:(3 * H + 2 * W0) * UNROLL]
        same_earlier = ring[:, (3 * H + 2 * W0) * UNROLL:(4 * H + 2 * W0) * UNROLL]
        spread_sb = ring[:, (4 * H + 2 * W0) * UNROLL:(5 * H + 2 * W0) * UNROLL]
        onehot = [sb(f"onehot{q}", [P, UNROLL * P], BF16) for q in range(2)]
        onehot_w = [sb(f"onehot_w{q}", [P, UNROLL * P], F32) for q in range(2)]
        local = [sb(f"local{q}", [P, UNROLL], F32) for q in range(2)]
        not_neg = sb("not_neg", [P, UNROLL], F32)
        valid = sb("valid", [P, UNROLL], F32)
        src_rel = [sb(f"src_rel{q}", [P, UNROLL], F32) for q in range(2)]
        src_key = [sb(f"src_key{q}", [P, UNROLL], F32) for q in range(2)]
        n_earlier = sb("n_earlier", [P, UNROLL], F32)
        first_rel = sb("first_rel", [P, UNROLL], F32)
        gather_idx = [sb(f"gather_idx{q}", [P, UNROLL], I32) for q in range(2)]
        type_idx = [sb(f"type_idx{q}", [P, UNROLL], I32) for q in range(2)]
        scatter_idx = [sb(f"scatter_idx{q}", [P, UNROLL], I32) for q in range(2)]
        product = [sb(f"product{q}", [P, UNROLL * W1], F32) for q in range(2)]
        assert RK <= UNROLL
        rel_sb, rel_out = product[0][:, 0:RK * C], product[1][:, 0:RK * W1]

        sums4 = [ring[:, q * COPIES * W0:(q + 1) * COPIES * W0] for q in range(2)]
        sums = sb("sums", [P, W0], F32)
        y_node = [sb(f"y_node{q}", [P, C], F32) for q in range(2)]
        deg_dst = sb("deg_dst", [P, NB], F32)
        rdeg_dst = sb("rdeg_dst", [P, NB], F32)
        root_dst = sb("root_dst", [P, NB], F32)
        under_root = [sb(f"under_root{q}", [P, 2], F32) for q in range(2)]
        rdeg_src = sb("rdeg_src", [P, 1], F32)
        stats = sb("stats", [P, 6], F32)
        mean_var = [sb(f"mean_var{q}", [P, 2], F32) for q in range(2)]
        roots = [sb(f"roots{q}", [P, 2], F32) for q in range(2)]
        rroots = [sb(f"rroots{q}", [P, 2], F32) for q in range(2)]
        h_rows = [product[q][:, 0:W1] for q in range(2)]
        turned = [onehot_w[q] for q in range(2)]
        staged = [rg[q][:, 0:2 * C] for q in range(2)]
        agg_part = ring[:, 0:C]
        x_bias = [ring[:, (1 + q) * C:(2 + q) * C] for q in range(2)]
        y_out = [product[q][:, 0:C] for q in range(2)]

        wait_holder = sem("wait_holder")
        edges_in = sem("edges_in")
        x_in = sem("x_in")
        x_tail_in = sem("x_tail_in")
        tail_zero = sem("tail_zero")
        const_iota = sem("const_iota")
        const_done = sem("const_done")
        weights_in = sem("weights_in")
        prep = sem("prep")
        acc0_zero = sem("acc0_zero")
        zeroed = sem("zeroed")
        pad_stored = sem("pad_stored")
        counted = sem("counted")
        starts_done = sem("starts_done")
        table_sel = sem("table_sel")
        prep_pe = sem("prep_pe")
        disorder_set = sem("disorder_set")
        rec_built = sem("rec_built")
        pos_ready = sem("pos_ready")
        fb_copied = sem("fb_copied")
        rec_stored = sem("rec_stored")
        rec_ready = sem("rec_ready")
        tables_ready = sem("tables_ready")
        rel_ready = sem("rel_ready")
        gate_lin = sem("gate_lin")
        gate_ready = sem("gate_ready")
        rel_stored = sem("rel_stored")
        negated = sem("negated")
        fold_ready = sem("fold_ready")
        rec_in = sem("rec_in")
        idx_ready = sem("idx_ready")
        x_gathered = [sem(f"x_gathered{q}") for q in range(2)]
        local_ready = sem("local_ready")
        onehot_ready = sem("onehot_ready")
        onehot_w_ready = sem("onehot_w_ready")
        not_neg_ready = sem("not_neg_ready")
        valid_ready = sem("valid_ready")
        src_rel_ready = sem("src_rel_ready")
        key_ready = sem("key_ready")
        keys_spread = sem("keys_spread")
        same_ready = sem("same_ready")
        same_earlier_ready = sem("same_earlier_ready")
        n_earlier_ready = sem("n_earlier_ready")
        degree_ready = sem("degree_ready")
        first_ready = sem("first_ready")
        scatter_idx_ready = sem("scatter_idx_ready")
        spread_done = sem("spread_done")
        spread_copied = sem("spread_copied")
        summed = sem("summed")
        acc0_added = sem("acc0_added")
        combined_done = sem("combined_done")
        combined_copied = sem("combined_copied")
        added = sem("added")
        sums_in = [sem(f"sums_in{q}") for q in range(2)]
        block_summed = sem("block_summed")
        deg_src_ready = sem("deg_src_ready")
        rdeg_ready = sem("rdeg_ready")
        y_ready = sem("y_ready")
        stats_ready = sem("stats_ready")
        var_ready = sem("var_ready")
        eps_added = sem("eps_added")
        roots_ready = sem("roots_ready")
        rroots_ready = sem("rroots_ready")
        x1_ready = sem("x1_ready")
        deg_dst_ready = sem("deg_dst_ready")
        root_dst_ready = sem("root_dst_ready")
        dst_scale_ready = sem("dst_scale_ready")
        h_built = sem("h_built")
        h_stored = [sem(f"h_stored{q}") for q in range(2)]
        acc1_zero = sem("acc1_zero")
        idx1_ready = sem("idx1_ready")
        rows_gathered = [sem(f"rows_gathered{q}") for q in range(2)]
        local1_ready = sem("local1_ready")
        onehot1_ready = sem("onehot1_ready")
        product_ready = sem("product_ready")
        summed1 = sem("summed1")
        acc1_added = sem("acc1_added")
        staged_ready = sem("staged_ready")
        turned_done = sem("turned_done")
        turned_copied = sem("turned_copied")
        linear_done = sem("linear_done")
        x_bias_ready = sem("x_bias_ready")
        bias_added = sem("bias_added")
        agg_ready = sem("agg_ready")
        linear_taken = sem("linear_taken")
        y1_ready = sem("y1_ready")
        stats1_ready = sem("stats1_ready")
        var1_ready = sem("var1_ready")
        eps1_added = sem("eps1_added")
        std_ready = sem("std_ready")
        rstd_ready = sem("rstd_ready")
        out_built = sem("out_built")
        out_stored = [sem(f"out_stored{q}") for q in range(2)]

        def tiles(ap, n):
            return ap.rearrange("p (s c) -> p s c", s=n)

        block = ctx.enter_context(nc.Block())

        @block.sync
        def _(sp):
            def as_rows(a):
                return a.rearrange("(p c) -> p c", p=ER)
            sp.dma_start(dst_i, as_rows(dst)).then_inc(edges_in, 16)
            sp.dma_start(src_i, as_rows(src)).then_inc(edges_in, 16)
            sp.dma_start(wgt_f, as_rows(edge_weight)).then_inc(edges_in, 16)
            sp.dma_start(typ_i, as_rows(edge_type)).then_inc(edges_in, 16)
            sp.dma_start(next_dst[0:ER - 1, :], as_rows(dst)[1:ER, 0:1], allow_slow_non_contiguous=True).then_inc(edges_in, 16)
            sp.dma_start(tiles(nodes[:, 0:(NB - 1) * C], NB - 1),
                         x[0:(NB - 1) * P, :].rearrange("(b p) c -> p b c", p=P)).then_inc(x_in, 16)
            sp.wait_ge(tail_zero, 1)
            sp.dma_start(nodes[0:LAST, (NB - 1) * C:NB * C], x[(NB - 1) * P:N, :]).then_inc(x_tail_in, 16)
            sp.wait_ge(acc0_zero, 1)
            for k in range(COPIES):
                sp.dma_start(sum_dram[k].rearrange("(p r) c -> p (r c)", p=P),
                             acc0[:, 0:ROWS // P * W0]).then_inc(zeroed, 16)
            sp.wait_ge(tables_ready, 1)
            sp.wait_ge(rec_ready, 1)
            with sp.Fori(0, PAIRS) as i:
                for s in range(2 * UNROLL):
                    off = sp.value_load(tile_offset[0:1, ds(i * (2 * UNROLL) + s, 1)], min_val=0, max_val=E)
                    sp.dma_start(records[:, ds(i * (8 * UNROLL) + 4 * s, 4)],
                                 rec_dram[ds(off, P), :]).then_inc(rec_in, 16)
                sp.wait_ge(rec_in, i * (32 * UNROLL) + 32 * UNROLL)
                sp.sem_inc(wait_holder, 1)

            sp.wait_ge(added, G * UNROLL * 16)

            def load_sums(b, q):
                for k in range(COPIES):
                    sp.dma_start(sums4[q][:, k * W0:(k + 1) * W0], sum_dram[k][ds(b * P, P), :]).then_inc(sums_in[q], 16)

            def store_h(b, q, n):
                sp.wait_ge(h_built, n + 2)
                sp.dma_start(h_dram[ds(b * P, P), :], h_rows[q]).then_inc(h_stored[q], 16)

            load_sums(0, 0)
            load_sums(1, 1)
            with sp.Fori(0, (NB - 1) // 2 - 1) as i:
                for q in range(2):
                    sp.wait_ge(block_summed, i * 2 + (q + 1))
                    load_sums(i * 2 + (q + 2), q)
                    store_h(i * 2 + q, q, i * 2 + (q + 1))
            sp.wait_ge(block_summed, NB - 2)
            load_sums(NB - 1, 0)
            store_h(NB - 3, 0, NB - 2)
            store_h(NB - 2, 1, NB - 1)
            store_h(NB - 1, 0, NB)

            def store_out(b, q, n, rows=P):
                sp.wait_ge(out_built, n)
                sp.dma_start(out[ds(b * P, rows), :], y_out[q][0:rows, :]).then_inc(out_stored[q], 16)
            with sp.Fori(0, (NB - 1) // 2) as i:
                for q in range(2):
                    store_out(i * 2 + q, q, i * 2 + (q + 1))
            store_out(NB - 1, 0, NB, LAST)
            sp.wait_ge(out_stored[0], 16 * ((NB + 1) // 2))
            sp.wait_ge(out_stored[1], 16 * (NB // 2))

        @block.gpsimd
        def _(pool):
            pool.iota(iota_free[:, :], pattern=[[1, P]], base=0, channel_multiplier=0,
                      allow_small_or_imprecise_dtypes=True).then_inc(const_iota, 1)
            pool.iota(iota_part[:, :], pattern=[[1, 1]], base=0, channel_multiplier=1,
                      allow_small_or_imprecise_dtypes=True).then_inc(const_iota, 1)
            pool.iota(spare[:, :], pattern=[[1, 1]], base=N, channel_multiplier=1,
                      allow_small_or_imprecise_dtypes=True).then_inc(const_iota, 1)
            pool.iota(limits[:, :], pattern=[[P, NBX + 1]], base=0, channel_multiplier=0,
                      allow_small_or_imprecise_dtypes=True).then_inc(const_iota, 1)
            pool.iota(iota_t, pattern=[[1, T]], base=0, channel_multiplier=0,
                      allow_small_or_imprecise_dtypes=True).then_inc(const_iota, 1)
            pool.memset(nodes[:, (NB - 1) * C:NBX * C], 0.0).then_inc(tail_zero, 1)
            pool.memset(pad_rec[:, 0:1], float(2 * NBX * P)).then_inc(const_iota, 1)
            pool.memset(pad_rec[:, 1:4], 0.0).then_inc(const_iota, 1)
            pool.wait_ge(const_iota, 7)
            pool.dma_start(rec_dram[E:E + P, :], pad_rec[:, :]).then_inc(pad_stored, 16)

            pool.wait_ge(rel_ready, 1)
            pool.dma_start(r_dram.rearrange("(k p) c -> p k c", p=RT),
                           tiles(rel_out[0:RT, :], RK)).then_inc(rel_stored, 16)

            pool.wait_ge(rec_built, 4)
            pool.wait_ge(disorder_set, 1)
            unsorted = pool.value_load(disorder[0:1, 0:1], min_val=0, max_val=2 * E)
            with pool.If(unsorted < 1):
                pool.dma_start(rec_dram[0:E, :].rearrange("(p c) f -> p (c f)", p=ER), rec4).then_inc(rec_stored, 16)
                pool.wait_ge(rec_stored, 16)
            with pool.Else():
                pool.wait_ge(pos_ready, 1)
                with pool.Fori(0, EC // FB) as j:
                    pool.tensor_copy(fb_idx[0:ER, :], pos_i[:, ds(j * FB, FB)]).then_inc(fb_copied, 1)
                    pool.tensor_copy(fb_rec[0:ER, :], rec4[:, ds(j * (4 * FB), 4 * FB)]).then_inc(fb_copied, 1)
                    pool.wait_ge(fb_copied, j * 2 + 2)
                    pool.sem_inc(wait_holder, 1)
                    for s in range(FB):
                        pool.indirect_dma_start(rec_dram[0:E, :], bass.IndirectOffsetOnAxis(ap=fb_idx[0:ER, s:s + 1], axis=0),
                                                fb_rec[0:ER, 4 * s:4 * s + 4], None).then_inc(rec_stored, 16)
                    pool.wait_ge(rec_stored, j * (16 * FB) + 16 * FB)
                    pool.sem_inc(wait_holder, 1)
            pool.wait_ge(pad_stored, 16)
            pool.sem_inc(rec_ready, 1)

            def gathers(n, q):
                pool.wait_ge(idx_ready, n)
                pool.wait_ge(summed, n)
                pool.sem_inc(wait_holder, 1)
                for s in range(UNROLL):
                    pool.indirect_dma_start(xg[q][:, s * H:(s + 1) * H], None, x_halves,
                                            bass.IndirectOffsetOnAxis(ap=gather_idx[q][:, s:s + 1], axis=0)
                                            ).then_inc(x_gathered[q], 16)

            def scatters(n, q, first=False):
                pool.wait_ge(scatter_idx_ready, n)
                pool.wait_ge(degree_ready, n)
                pool.wait_ge(combined_copied, n)
                if not first:
                    pool.wait_ge(added, (n - 1) * (16 * UNROLL))
                pool.sem_inc(wait_holder, 1)
                for s in range(UNROLL):
                    pool.indirect_dma_start(sum_dram[s], bass.IndirectOffsetOnAxis(ap=scatter_idx[q][:, s:s + 1], axis=0),
                                            combined[q][:, s * W0:(s + 1) * W0], None,
                                            compute_op=ALU.add).then_inc(added, 16)

            gathers(1, 0)
            pool.wait_ge(zeroed, 16 * COPIES)
            gathers(2, 1)
            scatters(1, 0, first=True)
            with pool.Fori(1, PAIRS) as i:
                gathers(i * 2 + 1, 0)
                scatters(i * 2, 1)
                gathers(i * 2 + 2, 1)
                scatters(i * 2 + 1, 0)
            scatters(G, 1)

            pool.wait_ge(rel_stored, 16)
            pool.wait_ge(h_stored[0], 16 * ((NB + 1) // 2))
            pool.wait_ge(h_stored[1], 16 * (NB // 2))

            with pool.Fori(0, PAIRS) as i:
                for q in range(2):
                    n = i * 2 + (q + 1)
                    pool.wait_ge(idx1_ready, n)
                    pool.wait_ge(product_ready, n)
                    pool.sem_inc(wait_holder, 1)
                    for s in range(UNROLL):
                        pool.indirect_dma_start(hg[q][:, s * W1:(s + 1) * W1], None, h_dram,
                                                bass.IndirectOffsetOnAxis(ap=gather_idx[q][:, s:s + 1], axis=0)
                                                ).then_inc(rows_gathered[q], 16)
                        pool.indirect_dma_start(rg[q][:, s * W1:(s + 1) * W1], None, r_dram,
                                                bass.IndirectOffsetOnAxis(ap=type_idx[q][:, s:s + 1], axis=0)
                                                ).then_inc(rows_gathered[q], 16)

            def add_bias(b, q, n):
                pool.wait_ge(bias_added, n)
                pool.sem_inc(wait_holder, 1)
                pool.tensor_tensor(x_bias[q], nodes[:, ds(b * C, C)], upd_bias[:, :], ALU.add).then_inc(x_bias_ready, 1)
            pool.wait_ge(product_ready, G + 2)
            with pool.Fori(0, (NB - 1) // 2) as i:
                for q in range(2):
                    add_bias(i * 2 + q, q, i * 2 + (q + 1))
            add_bias(NB - 1, 0, NB)

        @block.scalar
        def _(act):
            def blocks(w):
                return [[w[0], w[1], w[2], w[3]], [w[1], w[0], w[3], w[2]],
                        [w[2], w[3], w[0], w[1]], [w[3], w[2], w[1], w[0]]]
            for m, w in enumerate((msg_w, upd_w)):
                for o, line in enumerate(blocks(w)):
                    for c, piece in enumerate(line):
                        p0, c0 = (o % 2) * CB, (2 * m + o // 2) * C + c * CB
                        act.dma_start(w_nat[p0:p0 + CB, c0:c0 + CB], piece).then_inc(weights_in, 16)
            act.dma_start(tiles(rel_sb[0:RT, :], RK), rel.rearrange("(k p) c -> p k c", p=RT)).then_inc(weights_in, 16)
            act.dma_start(gate_wb[:, :], gate_w.broadcast_to([P, C])).then_inc(weights_in, 16)
            act.dma_start(gate_bb[:, :], gate_b.rearrange("(a b) -> a b", b=1).broadcast_to([P, 1])).then_inc(weights_in, 16)
            act.dma_start(bias_raw[:, :], upd_b.rearrange("(a b) c -> a (b c)", a=1).broadcast_to([P, C])
                          ).then_inc(weights_in, 16)
            act.dma_start(bias_col[:, :], msg_b.rearrange("(k b) c -> (b c) k", k=2), allow_slow_non_contiguous=True).then_inc(weights_in, 16)
            n_weights = 16 * (2 * B4 * B4 + 5)
            act.wait_ge(weights_in, n_weights)
            for m in range(2):
                for o, c in ((0, 3), (1, 2), (2, 3)):
                    p0, c0 = (o % 2) * CB, (2 * m + o // 2) * C + c * CB
                    act.mul(w_nat[p0:p0 + CB, c0:c0 + CB], w_nat[p0:p0 + CB, c0:c0 + CB], -1.0).then_inc(negated, 1)
            for k in range(2):
                act.wait_ge(prep_pe, 1 + k)
                act.copy(upd_t[:, k * C:(k + 1) * C].rearrange("p (c b) -> p b c", b=B4),
                         bank[6 + k][:, 0:C].rearrange("p (b c) -> p b c", b=B4)).then_inc(fold_ready, 1)
            for k in range(2):
                act.wait_ge(prep_pe, 3 + k)
                act.copy(both_t[:, k * C:(k + 1) * C], bank[6 + k][:, 0:C]).then_inc(fold_ready, 1)
            act.wait_ge(prep_pe, 5)
            act.copy(msg_bias[:, :], bank[5][:, 0:C]).then_inc(fold_ready, 1)

            act.wait_ge(gate_lin, RK + 1)
            act.activation(gate[0:RT, :], gate_z[0:RT, :], ACT.Sigmoid, bias=gate_bb[0:RT, :]).then_inc(gate_ready, 1)

            def rec_col(i, q, f):
                return records[:, ds(i * (8 * UNROLL) + 4 * UNROLL * q, 4 * UNROLL)].rearrange(
                    "p (s f) -> p s f", f=4)[:, :, f]

            def indices(i, q, peel):
                act.wait_ge(rec_in, i * (32 * UNROLL) + 32 * UNROLL)
                if not peel:
                    act.wait_ge(x_gathered[q], i * (16 * UNROLL))
                act.activation(gather_idx[q][:, :], rec_col(i, q, 1), ACT.Copy, scale=2.0, bias=1.0).then_inc(idx_ready, 1)

            def copies(i, q, peel):
                n = i * 2 + (q + 1)
                act.wait_ge(spread_done, n)
                act.copy(spread_sb, bank[2][:, :]).then_inc(spread_copied, 1)
                act.wait_ge(combined_done, n)
                if not peel:
                    act.wait_ge(added, (n - 2) * (16 * UNROLL))
                act.copy(tiles(combined[q], UNROLL)[:, :, 0:H], tiles(bank[3][:, :], UNROLL)).then_inc(combined_copied, 1)

            indices(0, 0, True)
            indices(0, 1, True)
            copies(0, 0, True)
            indices(1, 0, False)
            copies(0, 1, True)
            with act.Fori(1, PAIRS - 1) as i:
                indices(i, 1, False)
                copies(i, 0, False)
                indices(i + 1, 0, False)
                copies(i, 1, False)
            indices(PAIRS - 1, 1, False)
            copies(PAIRS - 1, 0, False)
            copies(PAIRS - 1, 1, False)

            act.sem_inc(h_built, 2)
            act.wait_ge(rel_stored, 16)
            act.wait_ge(deg_dst_ready, 1)
            act.activation(root_dst[:, :], deg_dst[:, :], ACT.Sqrt).then_inc(root_dst_ready, 1)

            def node_roots(q, n):
                act.wait_ge(eps_added, n)
                act.activation(roots[q][:, :], under_root[q][:, :], ACT.Sqrt).then_inc(roots_ready, 1)

            def scaled_rows(b, q, n, i):
                act.wait_ge(x1_ready, n)
                if i is not None:
                    act.wait_ge(h_stored[q], i * 16)
                act.mul(h_rows[q][:, 0:C], nodes[:, ds(b * C, C)], rroots[q][:, 0:1])
                act.copy(h_rows[q][:, C:C + 2], rroots[q][:, :]).then_inc(h_built, 1)

            node_roots(0, 1)
            node_roots(1, 2)
            scaled_rows(0, 0, 1, None)
            node_roots(0, 3)
            scaled_rows(1, 1, 2, None)
            with act.Fori(1, (NB - 1) // 2) as i:
                for q in range(2):
                    node_roots(1 - q, i * 2 + (q + 2))
                    scaled_rows(i * 2 + q, q, i * 2 + (q + 1), i)
            scaled_rows(NB - 1, 0, NB, (NB - 1) // 2)

            def indices1(i, q, peel):
                if not peel:
                    act.wait_ge(rows_gathered[q], i * (32 * UNROLL))
                act.copy(gather_idx[q][:, :], rec_col(i, q, 1))
                act.copy(type_idx[q][:, :], rec_col(i, q, 3)).then_inc(idx1_ready, 1)
            for q in range(2):
                indices1(0, q, True)
            with act.Fori(1, PAIRS) as i:
                for q in range(2):
                    indices1(i, q, False)

            def stage(b, q):
                act.copy(staged[q][:, 0:C], nodes[:, ds(b * C, C)])
                act.copy(staged[q][:, C:2 * C], acc1[:, ds(b * W1, C)]).then_inc(staged_ready, 1)

            def copy_turned(q, n):
                act.wait_ge(turned_done, n)
                act.copy(turned[q][:, :], bank[q][:, :]).then_inc(turned_copied, 1)

            def root(q, n):
                act.wait_ge(eps1_added, n)
                act.activation(roots[q][:, 1:2], under_root[q][:, 1:2], ACT.Sqrt).then_inc(std_ready, 1)

            act.wait_ge(acc1_added, UNROLL * (G + 1))
            stage(0, 0)
            stage(1, 1)
            copy_turned(0, 1)
            with act.Fori(0, (NB - 3) // 2) as i:
                for q in range(2):
                    copy_turned(1 - q, i * 2 + (q + 2))
                    stage(i * 2 + (q + 2), q)
                    root(q, i * 2 + (q + 1))
            copy_turned(1, NB - 1)
            stage(NB - 1, 0)
            root(0, NB - 2)
            copy_turned(0, NB)
            root(1, NB - 1)
            root(0, NB)

        @block.vector
        def _(dve):
            count = [0]

            def link(ins):
                count[0] += 1
                ins.then_inc(prep, 1)
                dve.wait_ge(prep, count[0])

            dve.memset(acc0[:, :], 0.0).then_inc(acc0_zero, 1)
            dve.memset(ones[:, :], 1.0).then_inc(const_done, 1)
            dve.memset(ones_bf[:, :], 1.0).then_inc(const_done, 1)
            dve.wait_ge(const_iota, 7)
            dve.tensor_scalar(ident[:, :], iota_free[:, :], iota_part[:, :], None, ALU.is_equal).then_inc(const_done, 1)
            dve.tensor_scalar(earlier[:, :], iota_free[:, :], iota_part[:, :], None, ALU.is_lt).then_inc(const_done, 1)
            dve.tensor_scalar(later[:, :], iota_free[:, :], iota_part[:, :], None, ALU.is_gt).then_inc(const_done, 1)

            dve.wait_ge(edges_in, 80)
            rec_fields = rec4.rearrange("p (c f) -> p f c", f=4)
            link(dve.tensor_copy(dst_f, dst_i))
            dve.tensor_copy(rec_fields[:, 0, :], dst_f).then_inc(rec_built, 1)
            dve.tensor_copy(rec_fields[:, 1, :], src_i).then_inc(rec_built, 1)
            dve.tensor_copy(rec_fields[:, 2, :], wgt_f).then_inc(rec_built, 1)
            dve.tensor_copy(rec_fields[:, 3, :], typ_i).then_inc(rec_built, 1)

            link(dve.memset(cum[:, :], 0.0))
            link(dve.memset(cum[0:ER, NB:NB + 2], float(EC)))
            for b in range(1, NB):
                dve.tensor_scalar(work_a, dst_f, float(b * P), 0.0, ALU.is_lt, ALU.add,
                                  accum_out=cum[0:ER, b:b + 1]).then_inc(counted, 1)
                dve.wait_ge(counted, b)
            link(dve.tensor_tensor(work_a[:, 0:EC - 1], dst_f[:, 0:EC - 1], dst_f[:, 1:EC], ALU.is_gt))
            link(dve.tensor_reduce(cum[0:ER, NBX + 1:NBX + 2], work_a[:, 0:EC - 1], AX_X, ALU.add))
            link(dve.tensor_copy(next_dst_f[0:ER - 1, :], next_dst[0:ER - 1, :]))
            link(dve.tensor_tensor(cum[0:ER - 1, NBX + 2:NBX + 3], dst_f[0:ER - 1, EC - 1:EC], next_dst_f[0:ER - 1, :],
                                   ALU.is_gt))
            link(dve.tensor_tensor(cum[0:ER, NBX + 1:NBX + 2], cum[0:ER, NBX + 1:NBX + 2],
                                   cum[0:ER, NBX + 2:NBX + 3], ALU.add))
            dve.tensor_tensor(bucket[0:ER, :], cum[0:ER, 1:NBX + 1], cum[0:ER, 0:NBX], ALU.subtract).then_inc(counted, 1)

            dve.wait_ge(prep_pe, 6)
            dve.tensor_copy(disorder[:, :], bank[4][0:1, 2:3]).then_inc(disorder_set, 1)
            link(dve.tensor_copy(starts[0:NBX, 0:2], bank[4][0:NBX, 0:2]))
            link(dve.tensor_tensor(starts[0:NBX, 2:3], starts[0:NBX, 1:2], starts[0:NBX, 0:1], ALU.subtract))
            link(dve.tensor_scalar(starts_i[0:NBX, 0:1], starts[0:NBX, 2:3], float(P - 1), None, ALU.add))
            link(dve.tensor_scalar(starts_i[0:NBX, 1:2], starts_i[0:NBX, 0:1], P.bit_length() - 1, None,
                                   ALU.arith_shift_right))
            dve.tensor_copy(starts[0:NBX, 3:4], starts_i[0:NBX, 1:2]).then_inc(starts_done, 1)
            dve.wait_ge(prep_pe, 7)
            link(dve.tensor_copy(starts[0:NBX, 4:5], bank[4][0:NBX, 8:9]))
            link(dve.tensor_scalar(starts[0:NBX, 5:6], starts[0:NBX, 4:5], -float(P), None, ALU.mult))
            link(dve.tensor_tensor(starts[0:NBX, 5:6], starts[0:NBX, 5:6], starts[0:NBX, 0:1], ALU.add))
            link(dve.tensor_scalar(starts[0:NBX, 6:7], iota_part[0:NBX, :], float(NB), float(T), ALU.is_ge, ALU.mult))
            link(dve.tensor_tensor(starts[0:NBX, 6:7], starts[0:NBX, 6:7], starts[0:NBX, 3:4], ALU.add))
            link(dve.tensor_tensor(starts[0:NBX, 6:7], starts[0:NBX, 6:7], starts[0:NBX, 4:5], ALU.add))
            link(dve.tensor_scalar(starts[0:NBX, 7:8], iota_part[0:NBX, :], float(P), None, ALU.mult))
            link(dve.tensor_scalar(below_next, iota_t[0:NBX, :], starts[0:NBX, 6:7], None, ALU.is_lt))
            dve.scalar_tensor_tensor(out=in_block, in0=iota_t[0:NBX, :], scalar=starts[0:NBX, 4:5], in1=below_next,
                                     op0=ALU.is_ge, op1=ALU.mult).then_inc(table_sel, 1)
            dve.wait_ge(prep_pe, 8)
            TH = T // 2
            off_f = acc1[0:1, 11 * EC:11 * EC + T]
            for k in range(2):
                sl = slice(k * TH, (k + 1) * TH)
                link(dve.tensor_copy(tile_base[:, sl], bank[4 + 2 * k][:, 0:TH]))
                link(dve.scalar_tensor_tensor(out=off_f[:, sl], in0=iota_t[0:1, sl], scalar=float(P),
                                              in1=bank[5 + 2 * k][0:1, 0:TH], op0=ALU.mult, op1=ALU.add))
            link(dve.tensor_scalar(tile_offset[:, :], off_f, float(E), None, ALU.min))
            dve.tensor_scalar(tile_block[:, :], tile_base[0:1, :], 1.0 / P, None, ALU.mult).then_inc(tables_ready, 1)

            dve.wait_ge(weights_in, 16 * (2 * B4 * B4 + 5))
            link(dve.memset(rel_out[0:RT, :], 0.0))
            for k in range(RK):
                dve.tensor_tensor(rel_out[0:RT, k * W1:k * W1 + C].rearrange("p (b c) -> p b c", b=B4),
                                  rel_sb[0:RT, k * C:(k + 1) * C].rearrange("p (b c) -> p b c", b=B4),
                                  gate_wb[0:RT, :].rearrange("p (c b) -> p b c", b=B4), ALU.mult).then_inc(gate_lin, 1)
            dve.wait_ge(gate_lin, RK)
            dve.tensor_reduce(gate_z[0:RT, :], tiles(rel_out[0:RT, :], RK), AX_X, ALU.add).then_inc(gate_lin, 1)
            dve.wait_ge(gate_ready, 1)
            for k in range(RK):
                link(dve.tensor_scalar(rel_out[0:RT, k * W1:k * W1 + C], rel_sb[0:RT, k * C:(k + 1) * C],
                                       gate[0:RT, k:k + 1], None, ALU.mult))
            dve.tensor_copy(tiles(rel_out[0:RT, :], RK)[:, :, C:C + 1].rearrange("p k a -> p (k a)"),
                            gate[0:RT, :]).then_inc(rel_ready, 1)
            link(dve.tensor_copy(upd_bias[:, :].rearrange("p (c b) -> p b c", b=B4),
                                 bias_raw[:, :].rearrange("p (b c) -> p b c", b=B4)))

            unsorted = dve.value_load(disorder[0:1, 0:1], min_val=0, max_val=2 * E)
            with dve.If(unsorted > 0):
                dve.wait_ge(prep_pe, 9)
                dve.tensor_copy(first_pos[0:ER, :], bank[3][0:ER, 0:NBX]).then_inc(counted, 1)
                dve.wait_ge(counted, NB + 1)
                dve.memset(pos, -1.0).then_inc(counted, 1)
                with dve.Fori(0, NB) as b:
                    base = b * 5 + (NB + 2)
                    dve.tensor_scalar(work_b, dst_f, limits[0:ER, ds(b, 1)], None, ALU.is_ge).then_inc(counted, 1)
                    dve.wait_ge(counted, base + 1)
                    dve.scalar_tensor_tensor(out=work_b, in0=dst_f, scalar=limits[0:ER, ds(b + 1, 1)], in1=work_b,
                                             op0=ALU.is_lt, op1=ALU.mult).then_inc(counted, 1)
                    dve.wait_ge(counted, base + 2)
                    dve.tensor_tensor_scan(work_c, ones[0:ER, 0:1].broadcast_to([ER, EC]), work_b,
                                           first_pos[0:ER, ds(b, 1)], ALU.mult, ALU.add).then_inc(counted, 1)
                    dve.wait_ge(counted, base + 3)
                    dve.tensor_tensor(work_c, work_c, work_b, ALU.mult).then_inc(counted, 1)
                    dve.wait_ge(counted, base + 4)
                    dve.tensor_tensor(pos, pos, work_c, ALU.add).then_inc(counted, 1)
                    dve.wait_ge(counted, base + 5)
                dve.tensor_copy(pos_i, pos).then_inc(pos_ready, 1)

            for q in range(2):
                link(dve.memset(combined[q], 0.0))
            dve.wait_ge(zeroed, 16 * COPIES)
            dve.wait_ge(x_in, 16)
            dve.wait_ge(x_tail_in, 16)

            def field(i, q, f):
                return records[:, ds(i * (8 * UNROLL) + 4 * UNROLL * q, 4 * UNROLL)].rearrange(
                    "p (s f) -> p s f", f=4)[:, :, f]

            def bcast(ap):
                return ap.unsqueeze(2).broadcast_to([P, UNROLL, P])

            def every(ap):
                return ap.unsqueeze(1).broadcast_to([P, UNROLL, P])

            def keys(i, q):
                n = i * 2 + (q + 1)
                dve.wait_ge(rec_in, i * (32 * UNROLL) + 32 * UNROLL)
                dve.tensor_tensor(local[q][:, :], field(i, q, 0),
                                  tile_base[:, ds(i * (2 * UNROLL) + q * UNROLL, UNROLL)],
                                  ALU.subtract).then_inc(local_ready, 1)
                dve.wait_ge(local_ready, n)
                dve.tensor_scalar(not_neg[:, :], local[q][:, :], 0.0, None, ALU.is_ge).then_inc(not_neg_ready, 1)
                dve.wait_ge(not_neg_ready, n)
                dve.scalar_tensor_tensor(out=valid[:, :], in0=local[q][:, :], scalar=float(P), in1=not_neg[:, :],
                                         op0=ALU.is_lt, op1=ALU.mult).then_inc(valid_ready, 1)
                dve.wait_ge(valid_ready, n)
                dve.scalar_tensor_tensor(out=src_rel[q][:, :], in0=field(i, q, 1), scalar=spare[:, :], in1=valid[:, :],
                                         op0=ALU.subtract, op1=ALU.mult).then_inc(src_rel_ready, 1)
                dve.wait_ge(src_rel_ready, n)
                dve.tensor_scalar(src_key[q][:, :], src_rel[q][:, :], spare[:, :], None, ALU.add).then_inc(key_ready, 1)
                dve.wait_ge(summed, n)
                dve.tensor_tensor(tiles(onehot[q][:, :], UNROLL), every(iota_free[:, :]), bcast(local[q][:, :]),
                                  ALU.is_equal).then_inc(onehot_ready, 1)
                dve.wait_ge(onehot_ready, n)
                dve.tensor_tensor(tiles(onehot_w[q][:, :], UNROLL), tiles(onehot[q][:, :], UNROLL),
                                  bcast(field(i, q, 2)), ALU.mult).then_inc(onehot_w_ready, 1)

            def equal_sources(q, n):
                dve.wait_ge(keys_spread, n)
                dve.tensor_tensor(tiles(same, UNROLL), tiles(bank[q][:, :], UNROLL), bcast(src_key[q][:, :]),
                                  ALU.is_equal).then_inc(same_ready, 1)

            def first_of_equal(q, n, peel):
                dve.wait_ge(same_ready, n)
                dve.tensor_tensor(tiles(same_earlier, UNROLL), tiles(same, UNROLL), every(earlier[:, :]),
                                  ALU.mult).then_inc(same_earlier_ready, 1)
                if not peel:
                    dve.wait_ge(added, (n - 2) * (16 * UNROLL))
                dve.tensor_reduce(tiles(combined[q], UNROLL)[:, :, H], tiles(same, UNROLL), AX_X,
                                  ALU.add).then_inc(degree_ready, 1)
                dve.wait_ge(same_earlier_ready, n)
                dve.tensor_reduce(n_earlier[:, :], tiles(same_earlier, UNROLL), AX_X, ALU.add).then_inc(n_earlier_ready, 1)
                dve.wait_ge(n_earlier_ready, n)
                dve.scalar_tensor_tensor(out=first_rel[:, :], in0=n_earlier[:, :], scalar=0.0, in1=src_rel[q][:, :],
                                         op0=ALU.is_equal, op1=ALU.mult).then_inc(first_ready, 1)
                dve.wait_ge(first_ready, n)
                dve.tensor_scalar(scatter_idx[q][:, :], first_rel[:, :], spare[:, :], None,
                                  ALU.add).then_inc(scatter_idx_ready, 1)

            def add_sums(i, q, n):
                dve.wait_ge(summed, n + 2)
                for s in range(UNROLL):
                    b = dve.value_load(tile_block[0:1, ds(i * (2 * UNROLL) + (q * UNROLL + s), 1)], min_val=0, max_val=NB)
                    here = acc0[:, ds(b * W0, H + 1)]
                    dve.wait_ge(acc0_added, n * UNROLL + s)
                    dve.tensor_tensor(here, here, bank[4 + s // 2][:, (s % 2) * C:(s % 2) * C + H + 1],
                                      ALU.add).then_inc(acc0_added, 1)

            def edges0(i, peel=False, last=False):
                for q in range(2):
                    n = i * 2 + (q + 1)
                    equal_sources(q, n)
                    if q == 0:
                        keys(i, 1)
                    elif not last:
                        keys(i + 1, 0)
                    first_of_equal(q, n, peel)
                    add_sums(i, q, n)

            dve.sem_inc(acc0_added, UNROLL)
            keys(0, 0)
            edges0(0, peel=True)
            with dve.Fori(1, PAIRS - 1) as i:
                edges0(i)
            edges0(PAIRS - 1, last=True)

            dve.memset(acc1[:, :], 0.0).then_inc(acc1_zero, 1)
            dve.wait_ge(acc0_added, UNROLL * (G + 1))
            dve.tensor_scalar(deg_dst[:, :], acc0[:, 0:NB * W0].rearrange("p (b w) -> p b w", w=W0)[:, :, H], 1.0, None,
                              ALU.max).then_inc(deg_dst_ready, 1)
            dve.wait_ge(deg_dst_ready, 1)
            dve.reciprocal(rdeg_dst[:, :], deg_dst[:, :]).then_inc(dst_scale_ready, 1)
            dve.wait_ge(root_dst_ready, 1)
            dve.reciprocal(dst_scale[:, :], root_dst[:, :]).then_inc(dst_scale_ready, 1)
            dve.wait_ge(dst_scale_ready, 2)

            def mean_and_var(q, n, y_sem, stats_sem, var_sem, eps_sem):
                dve.bn_stats(stats[:, :], y_node[q][:, :]).then_inc(stats_sem, 1)
                dve.wait_ge(stats_sem, n)
                dve.sem_inc(wait_holder, 1)
                dve.bn_aggr(mean_var[q][:, :], stats[:, :]).then_inc(var_sem, 1)
                dve.wait_ge(var_sem, n)
                dve.tensor_scalar(under_root[q][:, 1:2], mean_var[q][:, 1:2], EPS, None, ALU.add).then_inc(eps_sem, 1)

            def residual0(b, q, n, i):
                dve.wait_ge(sums_in[q], i * (16 * COPIES) + 16 * COPIES)
                dve.tensor_reduce(sums[:, :], sums4[q].rearrange("p (k c) -> p c k", k=COPIES), AX_X,
                                  ALU.add).then_inc(block_summed, 1)
                dve.wait_ge(block_summed, n)
                dve.tensor_scalar(under_root[q][:, 0:1], sums[:, H:H + 1], 1.0, None, ALU.max).then_inc(deg_src_ready, 1)
                dve.scalar_tensor_tensor(out=y_node[q][:, H:C], in0=acc0[:, ds(b * W0, H)], scalar=rdeg_dst[:, ds(b, 1)],
                                         in1=nodes[:, ds(b * C + H, H)], op0=ALU.mult, op1=ALU.add).then_inc(y_ready, 1)
                dve.wait_ge(deg_src_ready, n)
                dve.reciprocal(rdeg_src[:, :], under_root[q][:, 0:1]).then_inc(rdeg_ready, 1)
                dve.wait_ge(rdeg_ready, n)
                dve.scalar_tensor_tensor(out=y_node[q][:, 0:H], in0=sums[:, 0:H], scalar=rdeg_src[:, 0:1],
                                         in1=nodes[:, ds(b * C, H)], op0=ALU.mult, op1=ALU.add).then_inc(y_ready, 1)
                dve.wait_ge(y_ready, n * 2)
                mean_and_var(q, n, y_ready, stats_ready, var_ready, eps_added)

            def normalise0(b, q, n):
                dve.wait_ge(roots_ready, n)
                dve.wait_ge(h_built, n)
                dve.reciprocal(rroots[q][:, :], roots[q][:, :]).then_inc(rroots_ready, 1)
                dve.wait_ge(rroots_ready, n)
                dve.tensor_scalar(nodes[:, ds(b * C, C)], y_node[q][:, :], mean_var[q][:, 0:1], rroots[q][:, 1:2],
                                  ALU.subtract, ALU.mult).then_inc(x1_ready, 1)

            residual0(0, 0, 1, 0)
            with dve.Fori(0, (NB - 1) // 2) as i:
                residual0(i * 2 + 1, 1, i * 2 + 2, i)
                normalise0(i * 2, 0, i * 2 + 1)
                residual0(i * 2 + 2, 0, i * 2 + 3, i + 1)
                normalise0(i * 2 + 1, 1, i * 2 + 2)
            normalise0(NB - 1, 0, NB)
            dve.wait_ge(acc1_zero, 1)

            def onehots(i, q):
                n = i * 2 + (q + 1)
                dve.tensor_tensor(local[q][:, :], field(i, q, 0),
                                  tile_base[:, ds(i * (2 * UNROLL) + q * UNROLL, UNROLL)],
                                  ALU.subtract).then_inc(local1_ready, 1)
                dve.wait_ge(local1_ready, n)
                dve.wait_ge(summed1, n)
                dve.tensor_tensor(tiles(onehot_w[q][:, :], UNROLL), every(iota_free[:, :]), bcast(local[q][:, :]),
                                  ALU.is_equal).then_inc(onehot1_ready, 1)

            def products(i, q):
                dve.wait_ge(rows_gathered[q], i * (32 * UNROLL) + 32 * UNROLL)
                dve.tensor_tensor(product[q][:, :], hg[q], rg[q], ALU.mult).then_inc(product_ready, 1)

            def add_sums1(i, q):
                n = i * 2 + (q + 1)
                dve.wait_ge(summed1, n + 2)
                for s in range(UNROLL):
                    b = dve.value_load(tile_block[0:1, ds(i * (2 * UNROLL) + (q * UNROLL + s), 1)], min_val=0, max_val=NB)
                    here = acc1[:, ds(b * W1, C + 1)]
                    dve.wait_ge(acc1_added, n * UNROLL + s)
                    dve.tensor_tensor(here, here, bank[4 * q + s][:, 0:C + 1], ALU.add).then_inc(acc1_added, 1)

            dve.sem_inc(product_ready, 2)
            dve.sem_inc(acc1_added, UNROLL)
            onehots(0, 0)
            onehots(0, 1)
            products(0, 0)
            products(0, 1)
            add_sums1(0, 0)
            onehots(1, 0)
            with dve.Fori(1, PAIRS - 1) as i:
                products(i, 0)
                add_sums1(i - 1, 1)
                onehots(i, 1)
                products(i, 1)
                add_sums1(i, 0)
                onehots(i + 1, 0)
            products(PAIRS - 1, 0)
            add_sums1(PAIRS - 2, 1)
            onehots(PAIRS - 1, 1)
            products(PAIRS - 1, 1)
            add_sums1(PAIRS - 1, 0)
            add_sums1(PAIRS - 1, 1)

            def residual1(b, q, n):
                dve.wait_ge(linear_done, n)
                dve.scalar_tensor_tensor(out=agg_part, in0=msg_bias[:, :], scalar=acc1[:, ds(b * W1 + C, 1)],
                                         in1=bank[4 + q][:, 0:C], op0=ALU.mult, op1=ALU.add).then_inc(agg_ready, 1)
                dve.wait_ge(agg_ready, n)
                dve.scalar_tensor_tensor(out=y_node[q][:, :], in0=agg_part, scalar=dst_scale[:, ds(b, 1)],
                                         in1=bank[2 + q][:, 0:C], op0=ALU.mult, op1=ALU.add).then_inc(linear_taken, 1)
                dve.wait_ge(linear_taken, n + 2)
                dve.wait_ge(x_bias_ready, n)
                dve.tensor_tensor(y_node[q][:, :], y_node[q][:, :], x_bias[q], ALU.add).then_inc(bias_added, 1)
                dve.wait_ge(bias_added, n + 2)
                mean_and_var(q, n, bias_added, stats1_ready, var1_ready, eps1_added)

            def normalise1(q, n, i):
                dve.wait_ge(std_ready, n)
                dve.reciprocal(rroots[q][:, 1:2], roots[q][:, 1:2]).then_inc(rstd_ready, 1)
                dve.wait_ge(rstd_ready, n)
                if i is not None:
                    dve.wait_ge(out_stored[q], i * 16)
                dve.tensor_scalar(y_out[q], y_node[q][:, :], mean_var[q][:, 0:1], rroots[q][:, 1:2],
                                  ALU.subtract, ALU.mult).then_inc(out_built, 1)

            dve.sem_inc(bias_added, 2)
            dve.sem_inc(linear_taken, 2)
            dve.wait_ge(fold_ready, 5)
            residual1(0, 0, 1)
            residual1(1, 1, 2)
            normalise1(0, 1, None)
            residual1(2, 0, 3)
            normalise1(1, 2, None)
            with dve.Fori(1, (NB - 1) // 2) as i:
                residual1(i * 2 + 1, 1, i * 2 + 2)
                normalise1(0, i * 2 + 1, i)
                residual1(i * 2 + 2, 0, i * 2 + 3)
                normalise1(1, i * 2 + 2, i)
            normalise1(0, NB, (NB - 1) // 2)

        @block.tensor
        def _(pe):
            pe.wait_ge(const_done, 5)
            pe.wait_ge(weights_in, 16 * (2 * B4 * B4 + 5))
            pe.wait_ge(negated, 6)
            for k in range(2):
                for o in range(2):
                    mm = pe.transpose(bank[6 + k][:, o * P:(o + 1) * P],
                                      w_nat[:, (2 + o) * C + k * P:(2 + o) * C + (k + 1) * P], ident[:, :])
                mm.then_inc(prep_pe, 1)
            pe.wait_ge(fold_ready, 2)
            for k in range(2):
                for o in range(2):
                    mm = pe.matmul(bank[6 + k][:, 0:C], w_nat[:, o * C + k * P:o * C + (k + 1) * P],
                                   upd_t[:, o * C:(o + 1) * C], start=(o == 0), stop=(o == 1))
                mm.then_inc(prep_pe, 1)
            for o in range(2):
                mm = pe.matmul(bank[5][:, 0:C], bias_col[:, o:o + 1].broadcast_to([P, P]),
                               upd_t[:, o * C:(o + 1) * C], start=(o == 0), stop=(o == 1))
            mm.then_inc(prep_pe, 1)

            pe.wait_ge(counted, NB)
            pe.matmul(bank[4][0:NBX, 0:1], cum[0:ER, 0:NBX], ones[0:ER, 0:1], start=True, stop=True)
            pe.matmul(bank[4][0:NBX, 1:2], cum[0:ER, 1:NBX + 1], ones[0:ER, 0:1], start=True, stop=True)
            pe.matmul(bank[4][0:1, 2:3], cum[0:ER, NBX + 1:NBX + 2], ones[0:ER, 0:1], start=True,
                      stop=True).then_inc(prep_pe, 1)
            pe.wait_ge(starts_done, 1)
            pe.matmul(bank[4][0:NBX, 8:9], later[0:NBX, 0:NBX], starts[0:NBX, 3:4], start=True,
                      stop=True).then_inc(prep_pe, 1)
            pe.wait_ge(table_sel, 1)
            pe.wait_ge(fold_ready, 5)
            TH = T // 2
            for k in range(2):
                for f in range(2):
                    mm = pe.matmul(bank[4 + 2 * k + f][:, 0:TH],
                                   starts[0:NBX, (7, 5)[f]:(7, 5)[f] + 1].broadcast_to([NBX, P]),
                                   in_block[:, k * TH:(k + 1) * TH], start=True, stop=True)
            mm.then_inc(prep_pe, 1)
            pe.matmul(bank[3][0:ER, 0:NBX], later[0:ER, 0:ER], bucket[0:ER, :], start=True, stop=False)
            pe.matmul(bank[3][0:ER, 0:NBX], ones[0:ER, 0:ER], cum[0:ER, 0:NBX], start=False,
                      stop=True).then_inc(prep_pe, 1)

            pe.sem_inc(summed, 2)
            pe.wait_ge(x_in, 16)
            pe.wait_ge(x_tail_in, 16)
            pe.wait_ge(tables_ready, 1)
            def spread_keys(q, n):
                pe.wait_ge(key_ready, n)
                for s in range(UNROLL):
                    mm = pe.matmul(bank[q][:, s * P:(s + 1) * P], src_key[q][:, s:s + 1].broadcast_to([P, P]),
                                   ident[:, :], start=True, stop=True)
                mm.then_inc(keys_spread, 1)

            def edges0(i, last=False):
                for q in range(2):
                    n = i * 2 + (q + 1)
                    pe.wait_ge(onehot_w_ready, n)
                    pe.wait_ge(same_ready, n)
                    for s in range(UNROLL):
                        mm = pe.matmul(bank[2][:, s * P:(s + 1) * P], onehot_w[q][:, s * P:(s + 1) * P],
                                       same[:, s * P:(s + 1) * P], start=True, stop=True)
                    mm.then_inc(spread_done, 1)
                    if not (last and q):
                        spread_keys(1 - q, n + 1)
                    pe.wait_ge(x_gathered[q], i * (16 * UNROLL) + 16 * UNROLL)
                    pe.wait_ge(acc0_added, n * UNROLL)
                    for s in range(UNROLL):
                        c0 = (s % 2) * C
                        pe.matmul(bank[4 + s // 2][:, c0:c0 + H], onehot_w[q][:, s * P:(s + 1) * P],
                                  xg[q][:, s * H:(s + 1) * H], start=True, stop=True)
                        mm = pe.matmul(bank[4 + s // 2][:, c0 + H:c0 + H + 1], onehot[q][:, s * P:(s + 1) * P],
                                       ones_bf[:, :], start=True, stop=True)
                    mm.then_inc(summed, 1)
                    pe.wait_ge(spread_copied, n)
                    for s in range(UNROLL):
                        b = pe.value_load(tile_block[0:1, ds(i * (2 * UNROLL) + (q * UNROLL + s), 1)],
                                          min_val=0, max_val=NB)
                        mm = pe.matmul(bank[3][:, s * P:(s + 1) * P], spread_sb[:, s * P:(s + 1) * P],
                                       nodes[:, ds(b * C, H)], start=True, stop=True)
                    mm.then_inc(combined_done, 1)

            spread_keys(0, 1)
            with pe.Fori(0, PAIRS - 1) as i:
                edges0(i)
            edges0(PAIRS - 1, last=True)

            pe.sem_inc(summed1, 2)
            with pe.Fori(0, PAIRS) as i:
                for q in range(2):
                    n = i * 2 + (q + 1)
                    pe.wait_ge(onehot1_ready, n)
                    pe.wait_ge(product_ready, n + 2)
                    pe.wait_ge(acc1_added, n * UNROLL)
                    for s in range(UNROLL):
                        mm = pe.matmul(bank[4 * q + s][:, 0:C + 1], onehot_w[q][:, s * P:(s + 1) * P],
                                       product[q][:, s * W1:s * W1 + C + 1], start=True, stop=True)
                    mm.then_inc(summed1, 1)

            def turn(q, n):
                pe.wait_ge(staged_ready, n)
                for k in range(4):
                    mm = pe.transpose(bank[q][:, k * P:(k + 1) * P], staged[q][:, k * P:(k + 1) * P], ident[:, :])
                mm.then_inc(turned_done, 1)

            def node_products(q, n):
                pe.wait_ge(turned_copied, n)
                pe.wait_ge(linear_taken, n)
                for m, w in enumerate((upd_t, both_t)):
                    for k in range(2):
                        mm = pe.matmul(bank[2 + 2 * m + q][:, 0:C], turned[q][:, (2 * m + k) * P:(2 * m + k + 1) * P],
                                       w[:, k * C:(k + 1) * C], start=(k == 0), stop=(k == 1))
                mm.then_inc(linear_done, 1)

            pe.wait_ge(acc1_added, UNROLL * (G + 1))
            turn(0, 1)
            with pe.Fori(0, (NB - 1) // 2) as i:
                for q in range(2):
                    turn(1 - q, i * 2 + (q + 2))
                    node_products(q, i * 2 + (q + 1))
            node_products(0, NB)


_INS = ['x', 'src', 'dst', 'edge_type_500', 'edge_weight', 'L1_gnn_relation_emb', 'L1_gnn_msg_w', 'L1_gnn_msg_b',
        'L1_gnn_upd_w', 'L1_gnn_upd_b', 'L1_gnn_gate_w', 'L1_gnn_gate_b']


def kernel(**inputs):
    import numpy as _np
    import concourse.bacc as _bacc
    from concourse import mybir as _mybir
    from concourse.bass_utils import run_bass_kernel_spmd as _run

    nc = _bacc.Bacc("TRN2", target_bir_lowering=False, num_devices=1)
    arrays, args = {}, []
    for name in _INS:
        a = _np.ascontiguousarray(inputs[name])
        arrays[f"in_{name}_dram"] = a
        args.append(nc.dram_tensor(f"in_{name}_dram", a.shape, _mybir.dt.from_np(a.dtype), kind="ExternalInput").ap())
    shape = tuple(inputs['x'].shape)
    args.append(nc.dram_tensor("out_0_dram", shape, _mybir.dt.float32, kind="ExternalOutput").ap())
    build_gnn(nc, *args)
    r = _run(nc, [arrays], core_ids=[0])
    return r.results[0]["out_0_dram"]
```

```python
from contextlib import ExitStack

import concourse.bass as bass
from concourse import mybir

ALU = mybir.AluOpType
ACT = mybir.ActivationFunctionType
F32 = mybir.dt.float32
BF16 = mybir.dt.bfloat16
I32 = mybir.dt.int32
AX_X = mybir.AxisListType.X
ds = bass.ds

P = 128
UNROLL = 4
BY_DMA = 2
BY_PE = UNROLL - BY_DMA
SUM_BANKS = 3
COPIES = UNROLL


def build_gnn(nc, x, src, dst, edge_type, edge_weight, rel, msg_w, msg_b, upd_w, upd_b, gate_w, gate_b, out):
    N, C = x.shape
    H = C // 2
    E = src.shape[0]
    R = rel.shape[0]
    NB = -(-N // P)
    NBX = NB + 1
    LAST = N - (NB - 1) * P
    ER = max(d for d in range(1, P + 1) if E % d == 0)
    EC = E // ER
    T = -(-((E + NB * (P - 1)) // P) // (2 * UNROLL)) * 2 * UNROLL
    G = T // UNROLL
    PAIRS = G // 2
    RT = max(d for d in range(1, P + 1) if R % d == 0)
    RK = R // RT
    W0 = H + 2
    W1 = C + 2
    ROWS = -(-(N + P) // P) * P
    EPS = 1e-5
    B4 = 4
    CB = C // B4
    BN = max(d for d in range(1, 2 * UNROLL) if NB % d == 0)
    BATCHES = NB // BN
    PIECES = [(0, UNROLL), (UNROLL, BN)]
    assert UNROLL < BN <= 7 and BATCHES % 2 and BATCHES > 3
    NCUM = NBX + 3
    ACT_FROM = NB - NB // 3 + 1
    FB = 5
    assert EC % FB == 0 and C == 2 * P

    rec_dram = nc.dram_tensor("edge_records", [E + P, 4], F32).ap()
    sum_dram = nc.dram_tensor("source_sums", [COPIES * ROWS, W0], F32).ap()
    h_dram = nc.dram_tensor("scaled_nodes", [NB * P, W1], F32).ap()
    r_dram = nc.dram_tensor("gated_relations", [R, W1], F32).ap()
    x_halves = x.rearrange("n (h c) -> (n h) c", h=2)

    with ExitStack() as ctx:
        def sb(name, shape, dt):
            return ctx.enter_context(nc.sbuf_tensor(name, shape, dt))

        def sem(name):
            return ctx.enter_context(nc.semaphore(name))

        bank = [ctx.enter_context(nc.psum_tensor(f"bank{k}", [P, 512], F32)) for k in range(8)]

        nodes = sb("nodes", [P, NBX * C], F32)
        acc0 = sb("acc0", [P, NBX * W0], F32)
        acc1 = sb("acc1", [P, NBX * W1], F32)
        records = sb("records", [P, T * 4], F32)
        tile_base = sb("tile_base", [P, T], F32)
        tables0 = sb("tables0", [P, 3 * T], I32)
        tile_offset = tables0[0:1, 0:T]
        node_col = tables0[0:1, T:2 * T]
        acc0_col = tables0[0:1, 2 * T:3 * T]
        acc1_col = sb("acc1_col", [1, T], I32)
        rel_rest = tables0.bitcast(F32)[0:RT, 0:RK * W1]
        rel_part = [tables0.bitcast(BF16)[0:RT, (2 + k) * RK * W1:(3 + k) * RK * W1] for k in range(3)]
        assert 5 * RK * W1 <= 2 * 3 * T and R <= 512
        iota_free = sb("iota_free", [P, P], F32)
        iota_part = sb("iota_part", [P, 1], F32)
        iota_type = sb("iota_type", [P, RK], F32)
        spare = sb("spare", [P, COPIES], F32)
        ident = sb("ident", [P, P], F32)
        earlier = sb("earlier", [P, P], F32)
        later = sb("later", [P, P], F32)
        ones = sb("ones", [P, P], F32)
        ones_bf = sb("ones_bf", [P, 1], BF16)
        dst_scale = sb("dst_scale", [P, NB], F32)
        upd_t = sb("upd_t", [P, 2 * C], F32)
        both_t = sb("both_t", [P, 2 * C], F32)
        msg_bias = sb("msg_bias", [P, C], F32)
        upd_bias = sb("upd_bias", [P, C], F32)

        cum = sb("cum", [P, NCUM], F32)
        cum_act = sb("cum_act", [P, NB], F32)
        odd = sb("odd", [P, NB], F32)
        block_bf = acc1[0:ER, 13 * EC + T:14 * EC + T].bitcast(BF16)[:, 0:EC]
        junk_bf = acc1[0:ER, 13 * EC + T:14 * EC + T].bitcast(BF16)[:, EC:2 * EC]
        assert 14 * EC + T <= NBX * W1
        bucket = sb("bucket", [P, NBX], F32)
        first_pos = sb("first_pos", [P, NBX], F32)
        limits = sb("limits", [P, NBX + 1], F32)
        next_dst = sb("next_dst", [P, 1], I32)
        next_dst_f = sb("next_dst_f", [P, 1], F32)
        starts = sb("starts", [P, 8], F32)
        starts_i = sb("starts_i", [P, 2], I32)
        disorder = sb("disorder", [1, 1], I32)
        pad_rec = sb("pad_rec", [P, 4], F32)
        fb_idx = sb("fb_idx", [P, FB], I32)
        fb_rec = sb("fb_rec", [P, FB * 4], F32)
        dst_i, src_i, wgt_f, typ_i = (acc1[0:ER, k * EC:(k + 1) * EC] for k in range(4))
        dst_i, src_i, typ_i = dst_i.bitcast(I32), src_i.bitcast(I32), typ_i.bitcast(I32)
        rec4 = acc1[0:ER, 4 * EC:8 * EC]
        dst_f = acc1[0:ER, 8 * EC:9 * EC]
        work_a, work_b, work_c, pos = (acc1[0:ER, k * EC:(k + 1) * EC] for k in range(9, 13))
        pos_i = work_a.bitcast(I32)
        in_block = acc1[0:NBX, 9 * EC:9 * EC + T]
        below_next = acc1[0:NBX, 11 * EC:11 * EC + T]
        iota_t = acc1[:, 13 * EC:13 * EC + T]
        assert 13 * EC + T <= NBX * W1
        w_nat = sb("w_nat", [P, 4 * C], F32)
        gate_wb = sb("gate_wb", [P, C], F32)
        gate_bb = sb("gate_bb", [P, 1], F32)
        gate_z = sb("gate_z", [P, RK], F32)
        gate = sb("gate", [P, RK], F32)
        bias_raw = sb("bias_raw", [P, C], F32)
        bias_col = sb("bias_col", [P, 2], F32)

        ring = sb("ring", [P, 2 * UNROLL * W1 * 2], F32)
        hg = [ring[:, q * UNROLL * W1:(q + 1) * UNROLL * W1] for q in range(2)]
        rg = [ring[:, (2 + q) * UNROLL * W1:(3 + q) * UNROLL * W1] for q in range(2)]
        xg = [ring[:, q * UNROLL * H:(q + 1) * UNROLL * H] for q in range(2)]
        combined = [ring[:, (2 * H + q * W0) * UNROLL:(2 * H + (q + 1) * W0) * UNROLL] for q in range(2)]
        same = ring[:, 2 * (H + W0) * UNROLL:(3 * H + 2 * W0) * UNROLL]
        same_earlier = ring[:, (3 * H + 2 * W0) * UNROLL:(4 * H + 2 * W0) * UNROLL]
        spread_sb = ring[:, (4 * H + 2 * W0) * UNROLL:(5 * H + 2 * W0) * UNROLL]
        onehot = [sb(f"onehot{q}", [P, UNROLL * P], BF16) for q in range(2)]
        onehot_w = [sb(f"onehot_w{q}", [P, UNROLL * P], F32) for q in range(2)]
        local = [sb(f"local{q}", [P, UNROLL], F32) for q in range(2)]
        not_neg = sb("not_neg", [P, UNROLL], F32)
        valid = sb("valid", [P, UNROLL], F32)
        src_rel = [sb(f"src_rel{q}", [P, UNROLL], F32) for q in range(2)]
        src_key = [sb(f"src_key{q}", [P, UNROLL], F32) for q in range(2)]
        n_earlier = sb("n_earlier", [P, UNROLL], F32)
        first_rel = sb("first_rel", [P, UNROLL], F32)
        gather_idx = [sb(f"gather_idx{q}", [P, UNROLL], I32) for q in range(2)]
        type_idx = [sb(f"type_idx{q}", [P, UNROLL], I32) for q in range(2)]
        type_col = [sb(f"type_col{q}", [P, BY_PE], F32) for q in range(2)]
        scatter_idx = [sb(f"scatter_idx{q}", [P, UNROLL], I32) for q in range(2)]
        type_onehot = [rg[q][0:RT, BY_DMA * W1:BY_DMA * W1 + RK * BY_PE * P // 2].bitcast(BF16) for q in range(2)]
        assert RK * BY_PE * P // 2 <= BY_PE * W1
        types_bf = onehot[0][:, 0:BY_PE * P]
        type_bank = bank[SUM_BANKS]
        row_bank = [[bank[SUM_BANKS + 1 + BY_PE * q + t] for t in range(BY_PE)] for q in range(2)]
        product = [sb(f"product{q}", [P, UNROLL * W1], F32) for q in range(2)]
        assert RK <= UNROLL
        rel_sb, rel_out = product[0][:, 0:RK * C], product[1][:, 0:RK * W1]

        sum_buf = [acc1[:, q * COPIES * BN * W0:(q + 1) * COPIES * BN * W0] for q in range(2)]
        y0 = [acc1[:, 2 * COPIES * BN * W0 + q * BN * C:2 * COPIES * BN * W0 + (q + 1) * BN * C] for q in range(2)]
        assert 2 * BN * (COPIES * W0 + C) <= NBX * W1
        h_rows = product
        deg_dst = sb("deg_dst", [P, NB], F32)
        rdeg_dst = sb("rdeg_dst", [P, NB], F32)
        root_dst = sb("root_dst", [P, NB], F32)
        rdeg_src = sb("rdeg_src", [P, BN], F32)
        stats = sb("stats", [P, 6 * BN], F32)
        mean_var = [sb(f"mean_var{q}", [P, 2 * BN], F32) for q in range(2)]
        under_root = [sb(f"under_root{q}", [P, 2 * BN], F32) for q in range(2)]
        roots = [sb(f"roots{q}", [P, 2 * BN], F32) for q in range(2)]
        rroots = [sb(f"rroots{q}", [P, 2 * BN], F32) for q in range(2)]
        turned_bank = bank[0]
        linear_bank = bank[1:1 + BN]
        turned = [onehot_w[q][:, 0:C] for q in range(2)]
        y1 = [ring[:, q * BN * C:(q + 1) * BN * C] for q in range(2)]
        assert 2 * BN * C <= 4 * UNROLL * W1
        staged = [product[q][:, 0:C] for q in range(2)]
        agg_part = [product[q][:, C:2 * C] for q in range(2)]

        wait_holder = sem("wait_holder")
        dst_in = sem("dst_in")
        edges_in = sem("edges_in")
        disorder_counted = sem("disorder_counted")
        counted_act = sem("counted_act")
        x_in = sem("x_in")
        x_tail_in = sem("x_tail_in")
        tail_zero = sem("tail_zero")
        const_iota = sem("const_iota")
        const_done = sem("const_done")
        weights_in = sem("weights_in")
        prep = sem("prep")
        acc0_zero = sem("acc0_zero")
        zeroed = sem("zeroed")
        pad_stored = sem("pad_stored")
        counted = sem("counted")
        starts_done = sem("starts_done")
        table_sel = sem("table_sel")
        prep_pe = sem("prep_pe")
        disorder_set = sem("disorder_set")
        rec_built = sem("rec_built")
        pos_ready = sem("pos_ready")
        fb_copied = sem("fb_copied")
        rec_stored = sem("rec_stored")
        rec_ready = sem("rec_ready")
        tables_ready = sem("tables_ready")
        rel_ready = sem("rel_ready")
        gate_lin = sem("gate_lin")
        gate_ready = sem("gate_ready")
        rel_stored = sem("rel_stored")
        negated = sem("negated")
        folded = sem("folded")
        fold_ready = sem("fold_ready")
        rec_in = sem("rec_in")
        idx_ready = sem("idx_ready")
        x_gathered = [sem(f"x_gathered{q}") for q in range(2)]
        local_ready = sem("local_ready")
        onehot_ready = sem("onehot_ready")
        onehot_w_ready = sem("onehot_w_ready")
        not_neg_ready = sem("not_neg_ready")
        valid_ready = sem("valid_ready")
        src_rel_ready = sem("src_rel_ready")
        key_ready = sem("key_ready")
        keys_spread = sem("keys_spread")
        same_ready = sem("same_ready")
        same_earlier_ready = sem("same_earlier_ready")
        n_earlier_ready = sem("n_earlier_ready")
        degree_ready = sem("degree_ready")
        first_ready = sem("first_ready")
        scatter_idx_ready = sem("scatter_idx_ready")
        spread_done = sem("spread_done")
        spread_copied = sem("spread_copied")
        summed = sem("summed")
        acc0_added = sem("acc0_added")
        combined_done = sem("combined_done")
        combined_copied = sem("combined_copied")
        added = [sem(f"added{s}") for s in range(UNROLL)]
        sums_in = [sem(f"sums_in{q}") for q in range(2)]
        copies_summed = sem("copies_summed")
        deg_src_ready = sem("deg_src_ready")
        rdeg_ready = sem("rdeg_ready")
        y_ready = sem("y_ready")
        stats_ready = sem("stats_ready")
        var_ready = sem("var_ready")
        eps_added = sem("eps_added")
        roots_ready = sem("roots_ready")
        rroots_ready = sem("rroots_ready")
        x1_ready = sem("x1_ready")
        deg_dst_ready = sem("deg_dst_ready")
        root_dst_ready = sem("root_dst_ready")
        dst_scale_ready = sem("dst_scale_ready")
        upd_plus_ready = sem("upd_plus_ready")
        x1_turned = sem("x1_turned")
        x1_turned_copied = sem("x1_turned_copied")
        x1_linear_done = sem("x1_linear_done")
        nodes_ready = sem("nodes_ready")
        h_built = sem("h_built")
        h_stored = [sem(f"h_stored{h}") for h in range(2)]
        acc1_zero = sem("acc1_zero")
        idx1_ready = sem("idx1_ready")
        rows_gathered = [sem(f"rows_gathered{q}") for q in range(2)]
        rel_loaded = sem("rel_loaded")
        rel_split = sem("rel_split")
        type_col_ready = sem("type_col_ready")
        types_spread = sem("types_spread")
        types_copied = sem("types_copied")
        type_onehot_ready = sem("type_onehot_ready")
        rel_rows_ready = sem("rel_rows_ready")
        local1_ready = sem("local1_ready")
        onehot1_ready = sem("onehot1_ready")
        product_ready = sem("product_ready")
        summed1 = sem("summed1")
        acc1_added = sem("acc1_added")
        staged_ready = sem("staged_ready")
        turned_done = sem("turned_done")
        turned_copied = sem("turned_copied")
        linear_done = sem("linear_done")
        agg_ready = sem("agg_ready")
        y1_ready = sem("y1_ready")
        stats1_ready = sem("stats1_ready")
        var1_ready = sem("var1_ready")
        eps1_added = sem("eps1_added")
        std_ready = sem("std_ready")
        rstd_ready = sem("rstd_ready")
        out_built = sem("out_built")
        out_stored = [sem(f"out_stored{q}") for q in range(2)]

        def blocks_of(ap, width, first, n):
            return ap.rearrange("(b p) c -> p b c", p=P)[:, ds(first, n), 0:width]

        def tiles(ap, n):
            return ap.rearrange("p (s c) -> p s c", s=n)

        def columns(engine, table, i, q, most):
            _, values = nc.values_load_multi_w_load_instructions(
                table[0:1, ds(i * (2 * UNROLL) + q * UNROLL, UNROLL)], engines=(engine,), min_val=0, max_val=most,
                skip_runtime_bounds_check_because="the table holds block numbers from 0 to NB times a row's width")
            return values

        GATHERED = 16 * (UNROLL + BY_DMA)

        block = ctx.enter_context(nc.Block())

        @block.sync
        def _(sp):
            def as_rows(a):
                return a.rearrange("(p c) -> p c", p=ER)
            sp.dma_start(dst_i, as_rows(dst)).then_inc(dst_in, 16)
            sp.dma_start(next_dst[0:ER - 1, :], as_rows(dst)[1:ER, 0:1], allow_slow_non_contiguous=True).then_inc(dst_in, 16)
            sp.dma_start(src_i, as_rows(src)).then_inc(edges_in, 16)
            sp.dma_start(wgt_f, as_rows(edge_weight)).then_inc(edges_in, 16)
            sp.dma_start(typ_i, as_rows(edge_type)).then_inc(edges_in, 16)
            sp.dma_start(tiles(nodes[:, 0:(NB - 1) * C], NB - 1),
                         x[0:(NB - 1) * P, :].rearrange("(b p) c -> p b c", p=P)).then_inc(x_in, 16)
            sp.wait_ge(tail_zero, 1)
            sp.dma_start(nodes[0:LAST, (NB - 1) * C:NB * C], x[(NB - 1) * P:N, :]).then_inc(x_tail_in, 16)
            sp.wait_ge(acc0_zero, 1)
            for k in range(COPIES):
                sp.dma_start(sum_dram[k * ROWS:(k + 1) * ROWS, :].rearrange("(p r) c -> p (r c)", p=P),
                             acc0[:, 0:ROWS // P * W0]).then_inc(zeroed, 16)
            sp.wait_ge(tables_ready, 3)
            sp.wait_ge(rec_ready, 1)
            with sp.Fori(0, PAIRS) as i:
                for s in range(2 * UNROLL):
                    off = sp.value_load(tile_offset[0:1, ds(i * (2 * UNROLL) + s, 1)], min_val=0, max_val=E)
                    sp.dma_start(records[:, ds(i * (8 * UNROLL) + 4 * s, 4)],
                                 rec_dram[ds(off, P), :]).then_inc(rec_in, 16)
                sp.wait_ge(rec_in, i * (32 * UNROLL) + 32 * UNROLL)
                sp.sem_inc(wait_holder, 1)

            sp.wait_ge(rel_ready, 1)
            sp.dma_start(r_dram.rearrange("(k p) c -> p k c", p=RT), tiles(rel_out[0:RT, :], RK)).then_inc(rel_stored, 16)

            for s in range(UNROLL):
                sp.wait_ge(added[s], G * 16)
            sp.wait_ge(summed, G + 2)

            def load_sums(g, q):
                for k in range(COPIES):
                    sp.dma_start(tiles(sum_buf[q][:, k * BN * W0:(k + 1) * BN * W0], BN),
                                 blocks_of(sum_dram[k * ROWS:(k + 1) * ROWS, :], W0, g * BN, BN)).then_inc(sums_in[q], 16)

            def store_h(g):
                for h, (first, end) in enumerate(PIECES):
                    sp.wait_ge(h_built, g * 2 + (h + 5))
                    sp.dma_start(blocks_of(h_dram, W1, g * BN + first, end - first),
                                 tiles(h_rows[h][:, 0:(end - first) * W1], end - first)).then_inc(h_stored[h], 16)

            def load_and_store(g, q):
                sp.wait_ge(y_ready, g + 1)
                load_sums(g + 2, q)
                store_h(g)

            load_sums(0, 0)
            load_sums(1, 1)
            with sp.Fori(0, (BATCHES - 3) // 2) as i:
                for q in range(2):
                    load_and_store(i * 2 + q, q)
            load_and_store(BATCHES - 3, 0)
            store_h(BATCHES - 2)
            store_h(BATCHES - 1)

            def store_out(g, q):
                sp.wait_ge(out_built, g + 1)
                sp.dma_start(blocks_of(out[0:(NB - 1) * P, :], C, g * BN, BN), tiles(y1[q], BN)).then_inc(out_stored[q], 16)

            with sp.Fori(0, (BATCHES - 1) // 2) as i:
                for q in range(2):
                    store_out(i * 2 + q, q)
            sp.wait_ge(out_built, BATCHES)
            sp.dma_start(out[(NB - 1) * P:N, :], y1[0][0:LAST, (BN - 1) * C:BN * C]).then_inc(out_stored[0], 16)
            sp.dma_start(blocks_of(out[0:(NB - 1) * P, :], C, NB - BN, BN - 1),
                         tiles(y1[0][:, 0:(BN - 1) * C], BN - 1)).then_inc(out_stored[0], 16)
            sp.wait_ge(out_stored[0], 16 * ((BATCHES + 1) // 2 + 1))
            sp.wait_ge(out_stored[1], 16 * (BATCHES // 2))

        @block.gpsimd
        def _(pool):
            pool.iota(iota_free[:, :], pattern=[[1, P]], base=0, channel_multiplier=0,
                      allow_small_or_imprecise_dtypes=True).then_inc(const_iota, 1)
            pool.iota(iota_part[:, :], pattern=[[1, 1]], base=0, channel_multiplier=1,
                      allow_small_or_imprecise_dtypes=True).then_inc(const_iota, 1)
            pool.iota(spare[:, :], pattern=[[ROWS, COPIES]], base=N, channel_multiplier=1,
                      allow_small_or_imprecise_dtypes=True).then_inc(const_iota, 1)
            pool.iota(limits[:, :], pattern=[[P, NBX + 1]], base=0, channel_multiplier=0,
                      allow_small_or_imprecise_dtypes=True).then_inc(const_iota, 1)
            pool.iota(iota_t, pattern=[[1, T]], base=0, channel_multiplier=0,
                      allow_small_or_imprecise_dtypes=True).then_inc(const_iota, 1)
            pool.iota(iota_type[:, :], pattern=[[RT, RK]], base=-(R // 2), channel_multiplier=1,
                      allow_small_or_imprecise_dtypes=True).then_inc(const_iota, 1)
            pool.iota(odd[:, :], pattern=[[2, NB]], base=-1, channel_multiplier=0,
                      allow_small_or_imprecise_dtypes=True).then_inc(const_iota, 1)
            pool.memset(nodes[:, (NB - 1) * C:NBX * C], 0.0).then_inc(tail_zero, 1)
            pool.memset(pad_rec[:, 0:1], float(2 * NBX * P)).then_inc(const_iota, 1)
            pool.memset(pad_rec[:, 1:4], 0.0).then_inc(const_iota, 1)
            pool.wait_ge(const_iota, 9)
            pool.dma_start(rec_dram[E:E + P, :], pad_rec[:, :]).then_inc(pad_stored, 16)

            rec_fields = rec4.rearrange("p (c f) -> p f c", f=4)
            pool.wait_ge(dst_in, 32)
            pool.tensor_copy(rec_fields[:, 0, :], dst_i).then_inc(rec_built, 1)
            pool.wait_ge(edges_in, 48)
            pool.tensor_copy(rec_fields[:, 1, :], src_i).then_inc(rec_built, 1)
            pool.tensor_copy(rec_fields[:, 2, :], wgt_f).then_inc(rec_built, 1)
            pool.tensor_copy(rec_fields[:, 3, :], typ_i).then_inc(rec_built, 1)
            pool.memset(acc0[:, :], 0.0).then_inc(acc0_zero, 1)

            pool.wait_ge(rec_built, 4)
            pool.wait_ge(disorder_set, 1)
            unsorted = pool.value_load(disorder[0:1, 0:1], min_val=0, max_val=2 * E)
            with pool.If(unsorted < 1):
                pool.dma_start(rec_dram[0:E, :].rearrange("(p c) f -> p (c f)", p=ER), rec4).then_inc(rec_stored, 16)
                pool.wait_ge(rec_stored, 16)
            with pool.Else():
                pool.wait_ge(pos_ready, 1)
                with pool.Fori(0, EC // FB) as j:
                    pool.tensor_copy(fb_idx[0:ER, :], pos_i[:, ds(j * FB, FB)]).then_inc(fb_copied, 1)
                    pool.tensor_copy(fb_rec[0:ER, :], rec4[:, ds(j * (4 * FB), 4 * FB)]).then_inc(fb_copied, 1)
                    pool.wait_ge(fb_copied, j * 2 + 2)
                    pool.sem_inc(wait_holder, 1)
                    for s in range(FB):
                        pool.indirect_dma_start(rec_dram[0:E, :], bass.IndirectOffsetOnAxis(ap=fb_idx[0:ER, s:s + 1], axis=0),
                                                fb_rec[0:ER, 4 * s:4 * s + 4], None).then_inc(rec_stored, 16)
                    pool.wait_ge(rec_stored, j * (16 * FB) + 16 * FB)
                    pool.sem_inc(wait_holder, 1)
            pool.wait_ge(pad_stored, 16)
            pool.sem_inc(rec_ready, 1)

            def may_gather(n):
                pool.wait_ge(idx_ready, n)
                pool.wait_ge(summed, n)
                pool.sem_inc(wait_holder, 1)

            def gather(s, q):
                pool.indirect_dma_start(xg[q][:, s * H:(s + 1) * H], None, x_halves,
                                        bass.IndirectOffsetOnAxis(ap=gather_idx[q][:, s:s + 1], axis=0)
                                        ).then_inc(x_gathered[q], 16)

            def may_add(n):
                pool.wait_ge(scatter_idx_ready, n)
                pool.wait_ge(degree_ready, n)
                pool.wait_ge(combined_copied, n)
                pool.sem_inc(wait_holder, 1)

            def add_rows(s, q, n, first=False):
                if not first:
                    pool.wait_ge(added[s], (n - 1) * 16)
                    pool.sem_inc(wait_holder, 1)
                pool.indirect_dma_start(sum_dram, bass.IndirectOffsetOnAxis(ap=scatter_idx[q][:, s:s + 1], axis=0),
                                        combined[q][:, s * W0:(s + 1) * W0], None,
                                        compute_op=ALU.add).then_inc(added[s], 16)

            def gathers_and_adds(n, q, first=False):
                may_gather(n + 1)
                gather(0, 1 - q)
                may_add(n)
                for s in range(UNROLL):
                    if s:
                        gather(s, 1 - q)
                    add_rows(s, q, n, first)

            may_gather(1)
            for s in range(UNROLL):
                gather(s, 0)
            pool.wait_ge(zeroed, 16 * COPIES)
            gathers_and_adds(1, 0, first=True)
            with pool.Fori(1, PAIRS) as i:
                gathers_and_adds(i * 2, 1)
                gathers_and_adds(i * 2 + 1, 0)
            may_add(G)
            for s in range(UNROLL):
                add_rows(s, 1, G)

            HALF = 2 * BN * W0
            def sum_copies(i, q, g):
                pool.wait_ge(sums_in[q], i * (16 * COPIES) + 16 * COPIES)
                pool.sem_inc(wait_holder, 1)
                pool.tensor_tensor(sum_buf[q][:, 0:HALF], sum_buf[q][:, 0:HALF], sum_buf[q][:, HALF:2 * HALF],
                                   ALU.add).then_inc(copies_summed, 1)
                pool.wait_ge(copies_summed, g * 2 + 1)
                pool.sem_inc(wait_holder, 1)
                pool.tensor_tensor(sum_buf[q][:, 0:HALF // 2], sum_buf[q][:, 0:HALF // 2], sum_buf[q][:, HALF // 2:HALF],
                                   ALU.add).then_inc(copies_summed, 1)

            sum_copies(0, 0, 0)
            sum_copies(0, 1, 1)

            pool.wait_ge(rel_stored, 16)
            pool.wait_ge(rec_in, 16 * T)
            pool.wait_ge(summed, G + 2)
            pool.wait_ge(acc0_added, UNROLL * (G + 1))
            pool.dma_start(tiles(rel_rest, RK), r_dram.rearrange("(k p) c -> p k c", p=RT)).then_inc(rel_loaded, 16)
            pool.wait_ge(rel_loaded, 16)
            for k in range(3):
                pool.tensor_copy(rel_part[k], rel_rest).then_inc(rel_split, 1)
                pool.wait_ge(rel_split, 2 * k + 1)
                if k < 2:
                    pool.tensor_tensor(rel_rest, rel_rest, rel_part[k], ALU.subtract).then_inc(rel_split, 1)
                    pool.wait_ge(rel_split, 2 * k + 2)

            with pool.Fori(1, (BATCHES - 1) // 2) as i:
                for q in range(2):
                    sum_copies(i, q, i * 2 + q)
            sum_copies((BATCHES - 1) // 2, 0, BATCHES - 1)

            for h in range(2):
                pool.wait_ge(h_stored[h], 16 * BATCHES)

            with pool.Fori(0, PAIRS) as i:
                for q in range(2):
                    n = i * 2 + (q + 1)
                    pool.wait_ge(idx1_ready, n)
                    pool.wait_ge(product_ready, n)
                    pool.sem_inc(wait_holder, 1)
                    for s in range(UNROLL):
                        pool.indirect_dma_start(hg[q][:, s * W1:(s + 1) * W1], None, h_dram,
                                                bass.IndirectOffsetOnAxis(ap=gather_idx[q][:, s:s + 1], axis=0)
                                                ).then_inc(rows_gathered[q], 16)
                        if s < BY_DMA:
                            pool.indirect_dma_start(rg[q][:, s * W1:(s + 1) * W1], None, r_dram,
                                                    bass.IndirectOffsetOnAxis(ap=type_idx[q][:, s:s + 1], axis=0)
                                                    ).then_inc(rows_gathered[q], 16)

        @block.scalar
        def _(act):
            def blocks(w):
                return [[w[0], w[1], w[2], w[3]], [w[1], w[0], w[3], w[2]],
                        [w[2], w[3], w[0], w[1]], [w[3], w[2], w[1], w[0]]]
            for m, w in enumerate((msg_w, upd_w)):
                for o, line in enumerate(blocks(w)):
                    for c, piece in enumerate(line):
                        p0, c0 = (o % 2) * CB, (2 * m + o // 2) * C + c * CB
                        act.dma_start(w_nat[p0:p0 + CB, c0:c0 + CB], piece).then_inc(weights_in, 16)
            act.dma_start(tiles(rel_sb[0:RT, :], RK), rel.rearrange("(k p) c -> p k c", p=RT)).then_inc(weights_in, 16)
            act.dma_start(gate_wb[:, :], gate_w.broadcast_to([P, C])).then_inc(weights_in, 16)
            act.dma_start(gate_bb[:, :], gate_b.rearrange("(a b) -> a b", b=1).broadcast_to([P, 1])).then_inc(weights_in, 16)
            act.dma_start(bias_raw[:, :], upd_b.rearrange("(a b) c -> a (b c)", a=1).broadcast_to([P, C])
                          ).then_inc(weights_in, 16)
            act.dma_start(bias_col[:, :], msg_b.rearrange("(k b) c -> (b c) k", k=2), allow_slow_non_contiguous=True).then_inc(weights_in, 16)
            act.wait_ge(counted, 1)
            act.wait_ge(const_iota, 9)
            for n, b in enumerate(range(ACT_FROM, NB)):
                act.activation(junk_bf, block_bf, ACT.Sign, bias=odd[0:ER, b:b + 1], scale=-2.0,
                               accum_out=cum_act[0:ER, b:b + 1]).then_inc(counted_act, 1)
                act.wait_ge(counted_act, n + 1)

            def rec_col(i, q, f):
                return records[:, ds(i * (8 * UNROLL) + 4 * UNROLL * q, 4 * UNROLL)].rearrange(
                    "p (s f) -> p s f", f=4)[:, :, f]

            def indices(i, q, peel):
                act.wait_ge(rec_in, i * (32 * UNROLL) + 32 * UNROLL)
                if not peel:
                    act.wait_ge(x_gathered[q], i * (16 * UNROLL))
                act.activation(gather_idx[q][:, :], rec_col(i, q, 1), ACT.Copy, scale=2.0, bias=1.0).then_inc(idx_ready, 1)

            def copies(i, q, peel):
                n = i * 2 + (q + 1)
                act.wait_ge(spread_done, n)
                act.copy(spread_sb, bank[2][:, :]).then_inc(spread_copied, 1)
                act.wait_ge(combined_done, n)
                if not peel:
                    for s in range(UNROLL):
                        act.wait_ge(added[s], (n - 2) * 16)
                act.copy(tiles(combined[q], UNROLL)[:, :, 0:H], tiles(bank[3][:, :], UNROLL)).then_inc(combined_copied, 1)

            indices(0, 0, True)
            indices(0, 1, True)
            copies(0, 0, True)
            indices(1, 0, False)
            copies(0, 1, True)
            act.wait_ge(gate_lin, RK + 1)
            act.activation(gate[0:RT, :], gate_z[0:RT, :], ACT.Sigmoid, bias=gate_bb[0:RT, :]).then_inc(gate_ready, 1)
            with act.Fori(1, PAIRS - 1) as i:
                indices(i, 1, False)
                copies(i, 0, False)
                indices(i + 1, 0, False)
                copies(i, 1, False)
            indices(PAIRS - 1, 1, False)
            copies(PAIRS - 1, 0, False)
            copies(PAIRS - 1, 1, False)

            act.wait_ge(weights_in, 16 * (2 * B4 * B4 + 5))
            for m in range(2):
                for o, c in ((0, 3), (1, 2), (2, 3)):
                    p0, c0 = (o % 2) * CB, (2 * m + o // 2) * C + c * CB
                    act.mul(w_nat[p0:p0 + CB, c0:c0 + CB], w_nat[p0:p0 + CB, c0:c0 + CB], -1.0).then_inc(negated, 1)
            for k in range(2):
                act.wait_ge(folded, 1 + k)
                act.copy(upd_t[:, k * C:(k + 1) * C].rearrange("p (c b) -> p b c", b=B4),
                         bank[6 + k][:, 0:C].rearrange("p (b c) -> p b c", b=B4)).then_inc(fold_ready, 1)
            for k in range(2):
                act.wait_ge(folded, 3 + k)
                act.copy(both_t[:, k * C:(k + 1) * C], bank[6 + k][:, 0:C]).then_inc(fold_ready, 1)
            act.wait_ge(folded, 5)
            act.copy(msg_bias[:, :], bank[5][:, 0:C]).then_inc(fold_ready, 1)

            act.sem_inc(h_built, 4)
            act.wait_ge(rel_stored, 16)
            act.wait_ge(deg_dst_ready, 1)
            act.activation(root_dst[:, :], deg_dst[:, :], ACT.Sqrt).then_inc(root_dst_ready, 1)

            def node_roots(q, n):
                act.wait_ge(eps_added, n)
                act.activation(roots[q][:, :], under_root[q][:, :], ACT.Sqrt).then_inc(roots_ready, 1)

            def scaled_rows(i, g, q, first):
                act.wait_ge(x1_ready, g + 1)
                for h, (j0, end) in enumerate(PIECES):
                    for j in range(j0, end):
                        p = (q * BN + j) % 2
                        act.wait_ge(x1_turned, i * (2 * BN) + (q * BN + j + 1))
                        act.copy(turned[p], turned_bank[:, 0:C]).then_inc(x1_turned_copied, 1)
                        if j == j0 and not first:
                            act.wait_ge(h_stored[h], g * 16)
                        act.mul(h_rows[h][:, (j - j0) * W1:(j - j0) * W1 + C], y0[q][:, j * C:(j + 1) * C],
                                rroots[q][:, 2 * j:2 * j + 1])
                    act.copy(tiles(h_rows[h][:, 0:(end - j0) * W1], end - j0)[:, :, C:C + 2],
                             tiles(rroots[q][:, 2 * j0:2 * end], end - j0)).then_inc(h_built, 1)

            node_roots(0, 1)
            scaled_rows(0, 0, 0, True)
            node_roots(1, 2)
            scaled_rows(0, 1, 1, False)
            with act.Fori(1, (BATCHES - 1) // 2) as i:
                for q in range(2):
                    node_roots(q, i * 2 + (q + 1))
                    scaled_rows(i, i * 2 + q, q, False)
            node_roots(0, BATCHES)
            scaled_rows((BATCHES - 1) // 2, BATCHES - 1, 0, False)

            def type_columns(i, q, peel):
                if not peel:
                    act.wait_ge(types_spread, i * 2 + (q - 1))
                act.copy(type_col[q][:, :], rec_col(i, q, 3)[:, BY_DMA:UNROLL]).then_inc(type_col_ready, 1)

            def copy_types(n, peel):
                act.wait_ge(types_spread, n)
                if not peel:
                    act.wait_ge(type_onehot_ready, n - 1)
                act.activation(types_bf, type_bank[:, 0:BY_PE * P], ACT.Copy, scale=1.0, bias=-float(R // 2)
                               ).then_inc(types_copied, 1)

            def indices1(i, q, peel):
                if not peel:
                    act.wait_ge(rows_gathered[q], i * GATHERED)
                act.copy(gather_idx[q][:, :], rec_col(i, q, 1))
                act.copy(type_idx[q][:, :], rec_col(i, q, 3)).then_inc(idx1_ready, 1)

            type_columns(0, 0, True)
            indices1(0, 0, True)
            type_columns(0, 1, True)
            copy_types(1, True)
            indices1(0, 1, True)
            with act.Fori(1, PAIRS) as i:
                for q in range(2):
                    type_columns(i, q, False)
                    copy_types(i * 2 + q, False)
                    indices1(i, q, False)
            copy_types(G, False)

            def stage(b, p):
                act.copy(staged[p], acc1[:, ds(b * W1, C)]).then_inc(staged_ready, 1)

            def copy_turned(b, p):
                act.wait_ge(turned_done, b + 1)
                act.copy(turned[p], turned_bank[:, 0:C]).then_inc(turned_copied, 1)

            def root(q, n):
                act.wait_ge(eps1_added, n)
                act.activation(roots[q][:, 0:BN], under_root[q][:, 0:BN], ACT.Sqrt).then_inc(std_ready, 1)

            def turn_batch(i, q, last=False):
                for j in range(BN):
                    b = i * (2 * BN) + (q * BN + j)
                    p = (q * BN + j) % 2
                    copy_turned(b, p)
                    if not last or j < BN - 2:
                        stage(b + 2, p)

            act.wait_ge(acc1_added, UNROLL * (G + 1))
            stage(0, 0)
            stage(1, 1)
            turn_batch(0, 0)
            turn_batch(0, 1)
            root(0, 1)
            with act.Fori(1, (BATCHES - 1) // 2) as i:
                turn_batch(i, 0)
                root(1, i * 2)
                turn_batch(i, 1)
                root(0, i * 2 + 1)
            turn_batch((BATCHES - 1) // 2, 0, last=True)
            root(1, BATCHES - 1)
            root(0, BATCHES)

        @block.vector
        def _(dve):
            count = [0]

            def link(ins):
                count[0] += 1
                ins.then_inc(prep, 1)
                dve.wait_ge(prep, count[0])

            dve.memset(ones[:, :], 1.0).then_inc(const_done, 1)
            dve.memset(ones_bf[:, :], 1.0).then_inc(const_done, 1)
            link(dve.memset(cum[:, :], 0.0))
            dve.wait_ge(dst_in, 32)
            link(dve.tensor_scalar(work_a.bitcast(I32), dst_i, P.bit_length() - 1, None, ALU.arith_shift_right))
            dve.tensor_copy(block_bf, work_a.bitcast(I32)).then_inc(counted, 1)
            link(dve.tensor_scalar(next_dst[0:ER - 1, :], next_dst[0:ER - 1, :], P.bit_length() - 1, None,
                                   ALU.arith_shift_right))
            link(dve.tensor_copy(next_dst_f[0:ER - 1, :], next_dst[0:ER - 1, :]))
            dve.wait_ge(counted, 1)
            link(dve.tensor_tensor(work_b[:, 0:EC - 1], block_bf[:, 0:EC - 1], block_bf[:, 1:EC], ALU.is_gt))
            link(dve.tensor_reduce(cum[0:ER, NBX + 1:NBX + 2], work_b[:, 0:EC - 1], AX_X, ALU.add))
            link(dve.tensor_tensor(cum[0:ER - 1, NBX + 2:NBX + 3], block_bf[0:ER - 1, EC - 1:EC], next_dst_f[0:ER - 1, :],
                                   ALU.is_gt))
            dve.tensor_tensor(cum[0:ER, NBX + 1:NBX + 2], cum[0:ER, NBX + 1:NBX + 2],
                              cum[0:ER, NBX + 2:NBX + 3], ALU.add).then_inc(disorder_counted, 1)

            link(dve.memset(cum[0:ER, NB:NB + 2], float(EC)))
            for b in range(1, ACT_FROM):
                dve.tensor_scalar(work_a.bitcast(BF16)[:, 0:EC], block_bf, float(b), 0.0, ALU.is_lt, ALU.add,
                                  accum_out=cum[0:ER, b:b + 1]).then_inc(counted, 1)
                dve.wait_ge(counted, b + 1)
                if b == 2:
                    dve.wait_ge(prep_pe, 1)
                    dve.tensor_copy(disorder[:, :], bank[4][0:1, 2:3]).then_inc(disorder_set, 1)
                    dve.wait_ge(const_iota, 9)
                    dve.tensor_scalar(ident[:, :], iota_free[:, :], iota_part[:, :], None, ALU.is_equal).then_inc(const_done, 1)
                    dve.tensor_scalar(earlier[:, :], iota_free[:, :], iota_part[:, :], None, ALU.is_lt).then_inc(const_done, 1)
                    dve.tensor_scalar(later[:, :], iota_free[:, :], iota_part[:, :], None, ALU.is_gt).then_inc(const_done, 1)
            dve.wait_ge(counted_act, NB - ACT_FROM)
            link(dve.tensor_scalar(cum[0:ER, ACT_FROM:NB], cum_act[0:ER, ACT_FROM:NB], float(EC), 0.5, ALU.add, ALU.mult))
            dve.tensor_tensor(bucket[0:ER, :], cum[0:ER, 1:NBX + 1], cum[0:ER, 0:NBX], ALU.subtract).then_inc(counted, 1)

            dve.wait_ge(prep_pe, 2)
            link(dve.tensor_copy(starts[0:NBX, 0:2], bank[4][0:NBX, 0:2]))
            link(dve.tensor_tensor(starts[0:NBX, 2:3], starts[0:NBX, 1:2], starts[0:NBX, 0:1], ALU.subtract))
            link(dve.tensor_scalar(starts_i[0:NBX, 0:1], starts[0:NBX, 2:3], float(P - 1), None, ALU.add))
            link(dve.tensor_scalar(starts_i[0:NBX, 1:2], starts_i[0:NBX, 0:1], P.bit_length() - 1, None,
                                   ALU.arith_shift_right))
            dve.tensor_copy(starts[0:NBX, 3:4], starts_i[0:NBX, 1:2]).then_inc(starts_done, 1)
            dve.wait_ge(prep_pe, 3)
            link(dve.tensor_copy(starts[0:NBX, 4:5], bank[4][0:NBX, 8:9]))
            link(dve.tensor_scalar(starts[0:NBX, 5:6], starts[0:NBX, 4:5], -float(P), None, ALU.mult))
            link(dve.tensor_tensor(starts[0:NBX, 5:6], starts[0:NBX, 5:6], starts[0:NBX, 0:1], ALU.add))
            link(dve.tensor_scalar(starts[0:NBX, 6:7], iota_part[0:NBX, :], float(NB), float(T), ALU.is_ge, ALU.mult))
            link(dve.tensor_tensor(starts[0:NBX, 6:7], starts[0:NBX, 6:7], starts[0:NBX, 3:4], ALU.add))
            link(dve.tensor_tensor(starts[0:NBX, 6:7], starts[0:NBX, 6:7], starts[0:NBX, 4:5], ALU.add))
            link(dve.tensor_scalar(starts[0:NBX, 7:8], iota_part[0:NBX, :], float(P), None, ALU.mult))
            link(dve.tensor_scalar(below_next, iota_t[0:NBX, :], starts[0:NBX, 6:7], None, ALU.is_lt))
            dve.scalar_tensor_tensor(out=in_block, in0=iota_t[0:NBX, :], scalar=starts[0:NBX, 4:5], in1=below_next,
                                     op0=ALU.is_ge, op1=ALU.mult).then_inc(table_sel, 1)
            dve.wait_ge(prep_pe, 4)
            TH = T // 2
            off_f = acc1[0:1, 11 * EC:11 * EC + T]
            for k in range(2):
                sl = slice(k * TH, (k + 1) * TH)
                link(dve.tensor_copy(tile_base[:, sl], bank[4 + 2 * k][:, 0:TH]))
                link(dve.scalar_tensor_tensor(out=off_f[:, sl], in0=iota_t[0:1, sl], scalar=float(P),
                                              in1=bank[5 + 2 * k][0:1, 0:TH], op0=ALU.mult, op1=ALU.add))
            link(dve.tensor_scalar(tile_offset[:, :], off_f, float(E), None, ALU.min))
            dve.tensor_scalar(acc0_col[:, :], tile_base[0:1, :], float(W0) / P, None, ALU.mult).then_inc(tables_ready, 1)
            dve.tensor_scalar(acc1_col[:, :], tile_base[0:1, :], float(W1) / P, None, ALU.mult).then_inc(tables_ready, 1)
            dve.tensor_scalar(node_col[:, :], tile_base[0:1, :], float(C) / P, None, ALU.mult).then_inc(tables_ready, 1)

            unsorted = dve.value_load(disorder[0:1, 0:1], min_val=0, max_val=2 * E)
            with dve.If(unsorted > 0):
                dve.wait_ge(prep_pe, 5)
                dve.tensor_copy(first_pos[0:ER, :], bank[3][0:ER, 0:NBX]).then_inc(counted, 1)
                dve.tensor_copy(dst_f, dst_i).then_inc(counted, 1)
                dve.memset(pos, -1.0).then_inc(counted, 1)
                dve.wait_ge(counted, ACT_FROM + 4)
                with dve.Fori(0, NB) as b:
                    base = b * 5 + (ACT_FROM + 4)
                    dve.tensor_scalar(work_b, dst_f, limits[0:ER, ds(b, 1)], None, ALU.is_ge).then_inc(counted, 1)
                    dve.wait_ge(counted, base + 1)
                    dve.scalar_tensor_tensor(out=work_b, in0=dst_f, scalar=limits[0:ER, ds(b + 1, 1)], in1=work_b,
                                             op0=ALU.is_lt, op1=ALU.mult).then_inc(counted, 1)
                    dve.wait_ge(counted, base + 2)
                    dve.tensor_tensor_scan(work_c, ones[0:ER, 0:1].broadcast_to([ER, EC]), work_b,
                                           first_pos[0:ER, ds(b, 1)], ALU.mult, ALU.add).then_inc(counted, 1)
                    dve.wait_ge(counted, base + 3)
                    dve.tensor_tensor(work_c, work_c, work_b, ALU.mult).then_inc(counted, 1)
                    dve.wait_ge(counted, base + 4)
                    dve.tensor_tensor(pos, pos, work_c, ALU.add).then_inc(counted, 1)
                    dve.wait_ge(counted, base + 5)
                dve.tensor_copy(pos_i, pos).then_inc(pos_ready, 1)

            for q in range(2):
                link(dve.memset(combined[q], 0.0))
            dve.wait_ge(zeroed, 16 * COPIES)
            dve.wait_ge(x_in, 16)
            dve.wait_ge(x_tail_in, 16)

            def field(i, q, f):
                return records[:, ds(i * (8 * UNROLL) + 4 * UNROLL * q, 4 * UNROLL)].rearrange(
                    "p (s f) -> p s f", f=4)[:, :, f]

            def bcast(ap):
                return ap.unsqueeze(2).broadcast_to([P, UNROLL, P])

            def every(ap):
                return ap.unsqueeze(1).broadcast_to([P, UNROLL, P])

            def keys(i, q):
                n = i * 2 + (q + 1)
                dve.wait_ge(rec_in, i * (32 * UNROLL) + 32 * UNROLL)
                dve.tensor_tensor(local[q][:, :], field(i, q, 0),
                                  tile_base[:, ds(i * (2 * UNROLL) + q * UNROLL, UNROLL)],
                                  ALU.subtract).then_inc(local_ready, 1)
                dve.wait_ge(local_ready, n)
                dve.tensor_scalar(not_neg[:, :], local[q][:, :], 0.0, None, ALU.is_ge).then_inc(not_neg_ready, 1)
                dve.wait_ge(not_neg_ready, n)
                dve.scalar_tensor_tensor(out=valid[:, :], in0=local[q][:, :], scalar=float(P), in1=not_neg[:, :],
                                         op0=ALU.is_lt, op1=ALU.mult).then_inc(valid_ready, 1)
                dve.wait_ge(valid_ready, n)
                dve.scalar_tensor_tensor(out=src_rel[q][:, :], in0=field(i, q, 1), scalar=spare[:, 0:1], in1=valid[:, :],
                                         op0=ALU.subtract, op1=ALU.mult).then_inc(src_rel_ready, 1)
                dve.wait_ge(src_rel_ready, n)
                dve.tensor_scalar(src_key[q][:, :], src_rel[q][:, :], spare[:, 0:1], None, ALU.add).then_inc(key_ready, 1)
                dve.wait_ge(summed, n)
                dve.tensor_tensor(tiles(onehot[q][:, :], UNROLL), every(iota_free[:, :]), bcast(local[q][:, :]),
                                  ALU.is_equal).then_inc(onehot_ready, 1)
                dve.wait_ge(onehot_ready, n)
                dve.tensor_tensor(tiles(onehot_w[q][:, :], UNROLL), tiles(onehot[q][:, :], UNROLL),
                                  bcast(field(i, q, 2)), ALU.mult).then_inc(onehot_w_ready, 1)

            def equal_sources(q, n):
                dve.wait_ge(keys_spread, n)
                dve.tensor_tensor(tiles(same, UNROLL), tiles(bank[q][:, :], UNROLL), bcast(src_key[q][:, :]),
                                  ALU.is_equal).then_inc(same_ready, 1)

            def first_of_equal(q, n, peel):
                dve.wait_ge(same_ready, n)
                dve.tensor_tensor(tiles(same_earlier, UNROLL), tiles(same, UNROLL), every(earlier[:, :]),
                                  ALU.mult).then_inc(same_earlier_ready, 1)
                if not peel:
                    for s in range(UNROLL):
                        dve.wait_ge(added[s], (n - 2) * 16)
                dve.tensor_reduce(tiles(combined[q], UNROLL)[:, :, H], tiles(same, UNROLL), AX_X,
                                  ALU.add).then_inc(degree_ready, 1)
                dve.wait_ge(same_earlier_ready, n)
                dve.tensor_reduce(n_earlier[:, :], tiles(same_earlier, UNROLL), AX_X, ALU.add).then_inc(n_earlier_ready, 1)
                dve.wait_ge(n_earlier_ready, n)
                dve.scalar_tensor_tensor(out=first_rel[:, :], in0=n_earlier[:, :], scalar=0.0, in1=src_rel[q][:, :],
                                         op0=ALU.is_equal, op1=ALU.mult).then_inc(first_ready, 1)
                dve.wait_ge(first_ready, n)
                dve.tensor_tensor(scatter_idx[q][:, :], first_rel[:, :], spare[:, :],
                                  ALU.add).then_inc(scatter_idx_ready, 1)

            def add_sums(i, q, n):
                cols = columns(mybir.EngineType.DVE, acc0_col, i, q, NB * W0)
                dve.wait_ge(summed, n + 2)
                for s in range(UNROLL):
                    here = acc0[:, ds(cols[s], H + 1)]
                    dve.wait_ge(acc0_added, n * UNROLL + s)
                    dve.tensor_tensor(here, here, bank[4 + s // 2][:, (s % 2) * C:(s % 2) * C + H + 1],
                                      ALU.add).then_inc(acc0_added, 1)

            def edges0(i, peel=False, last=False):
                for q in range(2):
                    n = i * 2 + (q + 1)
                    equal_sources(q, n)
                    if q == 0:
                        keys(i, 1)
                    elif not last:
                        keys(i + 1, 0)
                    if q:
                        add_sums(i, 0, n - 1)
                    elif not peel:
                        add_sums(i - 1, 1, n - 1)
                    first_of_equal(q, n, peel)

            dve.sem_inc(acc0_added, UNROLL)
            keys(0, 0)
            edges0(0, peel=True)

            dve.wait_ge(weights_in, 16 * (2 * B4 * B4 + 5))
            link(dve.memset(rel_out[0:RT, :], 0.0))
            for k in range(RK):
                dve.tensor_tensor(rel_out[0:RT, k * W1:k * W1 + C].rearrange("p (b c) -> p b c", b=B4),
                                  rel_sb[0:RT, k * C:(k + 1) * C].rearrange("p (b c) -> p b c", b=B4),
                                  gate_wb[0:RT, :].rearrange("p (c b) -> p b c", b=B4), ALU.mult).then_inc(gate_lin, 1)
            dve.wait_ge(gate_lin, RK)
            dve.tensor_reduce(gate_z[0:RT, :], tiles(rel_out[0:RT, :], RK), AX_X, ALU.add).then_inc(gate_lin, 1)
            dve.wait_ge(gate_ready, 1)
            for k in range(RK):
                link(dve.tensor_scalar(rel_out[0:RT, k * W1:k * W1 + C], rel_sb[0:RT, k * C:(k + 1) * C],
                                       gate[0:RT, k:k + 1], None, ALU.mult))
            dve.tensor_copy(tiles(rel_out[0:RT, :], RK)[:, :, C:C + 1].rearrange("p k a -> p (k a)"),
                            gate[0:RT, :]).then_inc(rel_ready, 1)
            link(dve.tensor_copy(upd_bias[:, :].rearrange("p (c b) -> p b c", b=B4),
                                 bias_raw[:, :].rearrange("p (b c) -> p b c", b=B4)))

            with dve.Fori(1, PAIRS - 1) as i:
                edges0(i)
            edges0(PAIRS - 1, last=True)
            add_sums(PAIRS - 1, 1, G)

            dve.wait_ge(acc0_added, UNROLL * (G + 1))
            dve.tensor_scalar(deg_dst[:, :], acc0[:, 0:NB * W0].rearrange("p (b w) -> p b w", w=W0)[:, :, H], 1.0, None,
                              ALU.max).then_inc(deg_dst_ready, 1)
            dve.wait_ge(deg_dst_ready, 1)
            dve.reciprocal(rdeg_dst[:, :], deg_dst[:, :]).then_inc(dst_scale_ready, 1)
            dve.wait_ge(root_dst_ready, 1)
            dve.reciprocal(dst_scale[:, :], root_dst[:, :]).then_inc(dst_scale_ready, 1)
            dve.wait_ge(dst_scale_ready, 2)

            def pairs_of(ap, k):
                return ap.rearrange("p (j two) -> p j two", two=2)[:, :, k]

            def mean_and_var(y, q, n, under, stats_sem, var_sem, eps_sem):
                for j in range(BN):
                    bn = dve.bn_stats(stats[:, 6 * j:6 * j + 6], y[q][:, j * C:(j + 1) * C])
                bn.then_inc(stats_sem, 1)
                dve.wait_ge(stats_sem, n)
                dve.sem_inc(wait_holder, 1)
                for j in range(BN):
                    bn = dve.bn_aggr(mean_var[q][:, 2 * j:2 * j + 2], stats[:, 6 * j:6 * j + 6])
                bn.then_inc(var_sem, 1)
                dve.wait_ge(var_sem, n)
                dve.tensor_scalar(under, pairs_of(mean_var[q], 1), EPS, None, ALU.add).then_inc(eps_sem, 1)

            def residual0(i, q, n):
                dve.wait_ge(h_built, n * 2)
                for j in range(BN):
                    b = i * (2 * BN) + (q * BN + j)
                    dve.scalar_tensor_tensor(out=y0[q][:, j * C + H:(j + 1) * C], in0=acc0[:, ds(b * W0, H)],
                                             scalar=rdeg_dst[:, ds(b, 1)], in1=nodes[:, ds(b * C + H, H)],
                                             op0=ALU.mult, op1=ALU.add)
                dve.wait_ge(copies_summed, n * 2)
                sums = tiles(sum_buf[q][:, 0:BN * W0], BN)
                dve.tensor_scalar(pairs_of(under_root[q], 0), sums[:, :, H], 1.0, None, ALU.max).then_inc(deg_src_ready, 1)
                dve.wait_ge(deg_src_ready, n)
                dve.reciprocal(rdeg_src[:, :], pairs_of(under_root[q], 0)).then_inc(rdeg_ready, 1)
                dve.wait_ge(rdeg_ready, n)
                for j in range(BN):
                    b = i * (2 * BN) + (q * BN + j)
                    y = dve.scalar_tensor_tensor(out=y0[q][:, j * C:j * C + H], in0=sums[:, j, 0:H],
                                                 scalar=rdeg_src[:, j:j + 1], in1=nodes[:, ds(b * C, H)],
                                                 op0=ALU.mult, op1=ALU.add)
                y.then_inc(y_ready, 1)
                dve.wait_ge(y_ready, n)
                mean_and_var(y0, q, n, pairs_of(under_root[q], 1), stats_ready, var_ready, eps_added)

            def normalise0(q, n):
                dve.wait_ge(roots_ready, n)
                dve.reciprocal(rroots[q][:, :], roots[q][:, :]).then_inc(rroots_ready, 1)
                dve.wait_ge(rroots_ready, n)
                for j in range(BN):
                    here = y0[q][:, j * C:(j + 1) * C]
                    y = dve.tensor_scalar(here, here, mean_var[q][:, 2 * j:2 * j + 1], rroots[q][:, 2 * j + 1:2 * j + 2],
                                          ALU.subtract, ALU.mult)
                y.then_inc(x1_ready, 1)

            def keep_updates(i, q):
                for j in range(BN):
                    b = i * (2 * BN) + (q * BN + j)
                    dve.wait_ge(x1_linear_done, b + 1)
                    dve.tensor_tensor(nodes[:, ds(b * C, C)], linear_bank[j][:, 0:C], upd_bias[:, :],
                                      ALU.add).then_inc(nodes_ready, 1)

            residual0(0, 0, 1)
            dve.wait_ge(folded, 5)
            for k in range(2):
                here = upd_t[:, k * C + k * P:k * C + (k + 1) * P]
                dve.tensor_tensor(here, here, ident[:, :], ALU.add).then_inc(upd_plus_ready, 1)
            normalise0(0, 1)
            with dve.Fori(0, (BATCHES - 1) // 2) as i:
                residual0(i, 1, i * 2 + 2)
                keep_updates(i, 0)
                normalise0(1, i * 2 + 2)
                residual0(i + 1, 0, i * 2 + 3)
                keep_updates(i, 1)
                normalise0(0, i * 2 + 3)
            keep_updates((BATCHES - 1) // 2, 0)
            dve.wait_ge(h_built, 2 * BATCHES + 4)
            dve.memset(acc1[:, :], 0.0).then_inc(acc1_zero, 1)

            def onehots(i, q):
                n = i * 2 + (q + 1)
                dve.tensor_tensor(local[q][:, :], field(i, q, 0),
                                  tile_base[:, ds(i * (2 * UNROLL) + q * UNROLL, UNROLL)],
                                  ALU.subtract).then_inc(local1_ready, 1)
                dve.wait_ge(local1_ready, n)
                dve.wait_ge(summed1, n * UNROLL)
                dve.tensor_tensor(tiles(onehot_w[q][:, :], UNROLL), every(iota_free[:, :]), bcast(local[q][:, :]),
                                  ALU.is_equal).then_inc(onehot1_ready, 1)

            def type_onehots(q, n):
                dve.wait_ge(types_copied, n)
                for k in range(RK):
                    eq = dve.tensor_scalar(type_onehot[q][:, k * BY_PE * P:(k + 1) * BY_PE * P], types_bf[0:RT, :],
                                           iota_type[0:RT, k:k + 1], None, ALU.is_equal)
                eq.then_inc(type_onehot_ready, 1)

            def products(i, q):
                n = i * 2 + (q + 1)
                dve.wait_ge(rows_gathered[q], i * GATHERED + GATHERED)
                dve.wait_ge(summed1, n * UNROLL)
                mul = dve.tensor_tensor(product[q][:, 0:BY_DMA * W1], hg[q][:, 0:BY_DMA * W1], rg[q][:, 0:BY_DMA * W1],
                                        ALU.mult)
                for t in range(BY_PE):
                    here = slice((BY_DMA + t) * W1, (BY_DMA + t) * W1 + C + 1)
                    dve.wait_ge(rel_rows_ready, n * BY_PE - (BY_PE - 1 - t))
                    mul = dve.tensor_tensor(product[q][:, here], hg[q][:, here], row_bank[q][t][:, 0:C + 1], ALU.mult)
                mul.then_inc(product_ready, 1)

            def add_sums1(i, q):
                n = i * 2 + (q + 1)
                cols = columns(mybir.EngineType.DVE, acc1_col, i, q, NB * W1)
                for s in range(UNROLL):
                    here = acc1[:, ds(cols[s], C + 1)]
                    dve.wait_ge(summed1, n * UNROLL + UNROLL + s + 1)
                    dve.wait_ge(acc1_added, n * UNROLL + s)
                    dve.tensor_tensor(here, here, bank[s % SUM_BANKS][:, 0:C + 1], ALU.add).then_inc(acc1_added, 1)

            dve.wait_ge(acc1_zero, 1)
            dve.sem_inc(product_ready, 2)
            dve.sem_inc(acc1_added, UNROLL)
            type_onehots(0, 1)
            type_onehots(1, 2)
            onehots(0, 0)

            def edges1(i, last=False):
                for q in range(2):
                    products(i, q)
                    if not last:
                        type_onehots(q, i * 2 + (q + 3))
                    if q == 0:
                        onehots(i, 1)
                    elif not last:
                        onehots(i + 1, 0)
                    add_sums1(i, q)

            with dve.Fori(0, PAIRS - 1) as i:
                edges1(i)
            edges1(PAIRS - 1, last=True)

            def residual1(i, q, n, first=False):
                if not first:
                    dve.wait_ge(out_stored[q], i * 16)
                for j in range(BN):
                    b = i * (2 * BN) + (q * BN + j)
                    p = (q * BN + j) % 2
                    dve.wait_ge(linear_done, b + 1)
                    dve.scalar_tensor_tensor(out=agg_part[p], in0=msg_bias[:, :], scalar=acc1[:, ds(b * W1 + C, 1)],
                                             in1=linear_bank[j][:, 0:C], op0=ALU.mult, op1=ALU.add).then_inc(agg_ready, 1)
                    dve.wait_ge(agg_ready, b + (BN + 1))
                    y = dve.scalar_tensor_tensor(out=y1[q][:, j * C:(j + 1) * C], in0=agg_part[p],
                                                 scalar=dst_scale[:, ds(b, 1)], in1=nodes[:, ds(b * C, C)],
                                                 op0=ALU.mult, op1=ALU.add)
                y.then_inc(y1_ready, 1)
                dve.wait_ge(y1_ready, n)
                mean_and_var(y1, q, n, under_root[q][:, 0:BN], stats1_ready, var1_ready, eps1_added)

            def normalise1(q, n):
                dve.wait_ge(std_ready, n)
                dve.reciprocal(rroots[q][:, 0:BN], roots[q][:, 0:BN]).then_inc(rstd_ready, 1)
                dve.wait_ge(rstd_ready, n)
                for j in range(BN):
                    here = y1[q][:, j * C:(j + 1) * C]
                    y = dve.tensor_scalar(here, here, mean_var[q][:, 2 * j:2 * j + 1], rroots[q][:, j:j + 1],
                                          ALU.subtract, ALU.mult)
                y.then_inc(out_built, 1)

            dve.wait_ge(rel_rows_ready, G * BY_PE)
            dve.sem_inc(agg_ready, BN)
            residual1(0, 0, 1, True)
            residual1(0, 1, 2, True)
            normalise1(0, 1)
            with dve.Fori(1, (BATCHES - 1) // 2) as i:
                residual1(i, 0, i * 2 + 1)
                normalise1(1, i * 2)
                residual1(i, 1, i * 2 + 2)
                normalise1(0, i * 2 + 1)
            residual1((BATCHES - 1) // 2, 0, BATCHES)
            normalise1(1, BATCHES - 1)
            normalise1(0, BATCHES)

        @block.tensor
        def _(pe):
            pe.wait_ge(const_done, 1)
            pe.wait_ge(disorder_counted, 1)
            pe.matmul(bank[4][0:1, 2:3], cum[0:ER, NBX + 1:NBX + 2], ones[0:ER, 0:1], start=True,
                      stop=True).then_inc(prep_pe, 1)
            pe.wait_ge(counted, ACT_FROM + 1)
            pe.matmul(bank[4][0:NBX, 0:1], cum[0:ER, 0:NBX], ones[0:ER, 0:1], start=True, stop=True)
            pe.matmul(bank[4][0:NBX, 1:2], cum[0:ER, 1:NBX + 1], ones[0:ER, 0:1], start=True,
                      stop=True).then_inc(prep_pe, 1)
            pe.wait_ge(const_done, 5)
            pe.wait_ge(starts_done, 1)
            pe.matmul(bank[4][0:NBX, 8:9], later[0:NBX, 0:NBX], starts[0:NBX, 3:4], start=True,
                      stop=True).then_inc(prep_pe, 1)
            pe.wait_ge(table_sel, 1)
            TH = T // 2
            for k in range(2):
                for f in range(2):
                    mm = pe.matmul(bank[4 + 2 * k + f][:, 0:TH],
                                   starts[0:NBX, (7, 5)[f]:(7, 5)[f] + 1].broadcast_to([NBX, P]),
                                   in_block[:, k * TH:(k + 1) * TH], start=True, stop=True)
            mm.then_inc(prep_pe, 1)
            pe.matmul(bank[3][0:ER, 0:NBX], later[0:ER, 0:ER], bucket[0:ER, :], start=True, stop=False)
            pe.matmul(bank[3][0:ER, 0:NBX], ones[0:ER, 0:ER], cum[0:ER, 0:NBX], start=False,
                      stop=True).then_inc(prep_pe, 1)

            pe.sem_inc(summed, 2)
            pe.wait_ge(x_in, 16)
            pe.wait_ge(x_tail_in, 16)
            pe.wait_ge(tables_ready, 3)
            def spread_keys(q, n):
                pe.wait_ge(key_ready, n)
                for s in range(UNROLL):
                    mm = pe.matmul(bank[q][:, s * P:(s + 1) * P], src_key[q][:, s:s + 1].broadcast_to([P, P]),
                                   ident[:, :], start=True, stop=True)
                mm.then_inc(keys_spread, 1)

            def edges0(i, last=False):
                for q in range(2):
                    n = i * 2 + (q + 1)
                    cols = columns(mybir.EngineType.PE, node_col, i, q, NB * C)
                    pe.wait_ge(onehot_w_ready, n)
                    pe.wait_ge(same_ready, n)
                    for s in range(UNROLL):
                        mm = pe.matmul(bank[2][:, s * P:(s + 1) * P], onehot_w[q][:, s * P:(s + 1) * P],
                                       same[:, s * P:(s + 1) * P], start=True, stop=True)
                    mm.then_inc(spread_done, 1)
                    if not (last and q):
                        spread_keys(1 - q, n + 1)
                    pe.wait_ge(spread_copied, n)
                    for s in range(UNROLL):
                        mm = pe.matmul(bank[3][:, s * P:(s + 1) * P], spread_sb[:, s * P:(s + 1) * P],
                                       nodes[:, ds(cols[s], H)], start=True, stop=True)
                    mm.then_inc(combined_done, 1)
                    pe.wait_ge(x_gathered[q], i * (16 * UNROLL) + 16 * UNROLL)
                    pe.wait_ge(acc0_added, n * UNROLL)
                    for s in range(UNROLL):
                        c0 = (s % 2) * C
                        pe.matmul(bank[4 + s // 2][:, c0:c0 + H], onehot_w[q][:, s * P:(s + 1) * P],
                                  xg[q][:, s * H:(s + 1) * H], start=True, stop=True)
                        mm = pe.matmul(bank[4 + s // 2][:, c0 + H:c0 + H + 1], onehot[q][:, s * P:(s + 1) * P],
                                       ones_bf[:, :], start=True, stop=True)
                    mm.then_inc(summed, 1)

            spread_keys(0, 1)
            with pe.Fori(0, PAIRS - 1) as i:
                edges0(i)
            edges0(PAIRS - 1, last=True)

            pe.wait_ge(acc0_added, UNROLL * (G + 1))
            pe.wait_ge(negated, 6)
            for k in range(2):
                for o in range(2):
                    mm = pe.transpose(bank[6 + k][:, o * P:(o + 1) * P],
                                      w_nat[:, (2 + o) * C + k * P:(2 + o) * C + (k + 1) * P], ident[:, :])
                mm.then_inc(folded, 1)
            pe.wait_ge(fold_ready, 2)
            for k in range(2):
                for o in range(2):
                    mm = pe.matmul(bank[6 + k][:, 0:C], w_nat[:, o * C + k * P:o * C + (k + 1) * P],
                                   upd_t[:, o * C:(o + 1) * C], start=(o == 0), stop=(o == 1))
                mm.then_inc(folded, 1)
            for o in range(2):
                mm = pe.matmul(bank[5][:, 0:C], bias_col[:, o:o + 1].broadcast_to([P, P]),
                               upd_t[:, o * C:(o + 1) * C], start=(o == 0), stop=(o == 1))
            mm.then_inc(folded, 1)

            pe.sem_inc(nodes_ready, BN)
            pe.wait_ge(fold_ready, 5)
            pe.wait_ge(upd_plus_ready, 2)

            def turn0(n, q, j):
                if j:
                    pe.wait_ge(x1_turned_copied, n - 1)
                for k in range(2):
                    mm = pe.transpose(turned_bank[:, k * P:(k + 1) * P], y0[q][:, j * C + k * P:j * C + (k + 1) * P],
                                      ident[:, :])
                mm.then_inc(x1_turned, 1)

            def batch0(i, g, q):
                pe.wait_ge(x1_ready, g + 1)
                n = i * (2 * BN) + (q * BN + 1)
                turn0(n, q, 0)
                for j in range(BN):
                    n = i * (2 * BN) + (q * BN + j + 1)
                    p = (q * BN + j) % 2
                    if j < BN - 1:
                        turn0(i * (2 * BN) + (q * BN + j + 2), q, j + 1)
                    pe.wait_ge(x1_turned_copied, n)
                    pe.wait_ge(nodes_ready, n)
                    for k in range(2):
                        mm = pe.matmul(linear_bank[j][:, 0:C], turned[p][:, k * P:(k + 1) * P],
                                       upd_t[:, k * C:(k + 1) * C], start=(k == 0), stop=(k == 1))
                    mm.then_inc(x1_linear_done, 1)

            with pe.Fori(0, (BATCHES - 1) // 2) as i:
                for q in range(2):
                    batch0(i, i * 2 + q, q)
            batch0((BATCHES - 1) // 2, BATCHES - 1, 0)
            pe.wait_ge(nodes_ready, NB + BN)

            pe.sem_inc(summed1, 2 * UNROLL)

            def spread_types(q, n, first=False):
                pe.wait_ge(type_col_ready, n)
                if not first:
                    pe.wait_ge(types_copied, n - 1)
                for t in range(BY_PE):
                    mm = pe.matmul(type_bank[:, t * P:(t + 1) * P], type_col[q][:, t:t + 1].broadcast_to([P, P]),
                                   ident[:, :], start=True, stop=True)
                mm.then_inc(types_spread, 1)

            def relation_rows(q, n, t):
                pe.wait_ge(type_onehot_ready, n)
                for part in range(3):
                    for k in range(RK):
                        c0 = (k * BY_PE + t) * P
                        mm = pe.matmul(row_bank[q][t][:, 0:C + 1], type_onehot[q][:, c0:c0 + P],
                                       rel_part[part][:, k * W1:k * W1 + C + 1], start=(part == 0 and k == 0),
                                       stop=(part == 2 and k == RK - 1))
                mm.then_inc(rel_rows_ready, 1)

            def edges1(i, last=False):
                for q in range(2):
                    n = i * 2 + (q + 1)
                    if not last:
                        spread_types(q, n + 2)
                    pe.wait_ge(onehot1_ready, n)
                    pe.wait_ge(product_ready, n + 2)
                    pe.wait_ge(acc1_added, n * UNROLL)
                    for s in range(UNROLL):
                        if s >= SUM_BANKS:
                            pe.wait_ge(acc1_added, n * UNROLL + (s - SUM_BANKS + 1))
                        pe.matmul(bank[s % SUM_BANKS][:, 0:C + 1], onehot_w[q][:, s * P:(s + 1) * P],
                                  product[q][:, s * W1:s * W1 + C + 1], start=True, stop=True).then_inc(summed1, 1)
                        if not last and s >= BY_DMA:
                            relation_rows(q, n + 2, s - BY_DMA)

            spread_types(0, 1, True)
            spread_types(1, 2)
            pe.wait_ge(rel_split, 5)
            for q in range(2):
                for t in range(BY_PE):
                    relation_rows(q, q + 1, t)
            with pe.Fori(0, PAIRS - 1) as i:
                edges1(i)
            edges1(PAIRS - 1, last=True)

            def turn(b, p, first=False):
                pe.wait_ge(staged_ready, b + 1)
                if not first:
                    pe.wait_ge(turned_copied, b)
                for k in range(2):
                    mm = pe.transpose(turned_bank[:, k * P:(k + 1) * P], staged[p][:, k * P:(k + 1) * P], ident[:, :])
                mm.then_inc(turned_done, 1)

            def batch1(i, q, last=False):
                for j in range(BN):
                    b = i * (2 * BN) + (q * BN + j)
                    p = (q * BN + j) % 2
                    if not last or j < BN - 1:
                        turn(i * (2 * BN) + (q * BN + j + 1), 1 - p)
                    pe.wait_ge(turned_copied, b + 1)
                    pe.wait_ge(agg_ready, b + 1)
                    for k in range(2):
                        mm = pe.matmul(linear_bank[j][:, 0:C], turned[p][:, k * P:(k + 1) * P],
                                       both_t[:, k * C:(k + 1) * C], start=(k == 0), stop=(k == 1))
                    mm.then_inc(linear_done, 1)

            pe.wait_ge(acc1_added, UNROLL * (G + 1))
            turn(0, 0, True)
            with pe.Fori(0, (BATCHES - 1) // 2) as i:
                for q in range(2):
                    batch1(i, q)
            batch1((BATCHES - 1) // 2, 0, last=True)


_INS = ['x', 'src', 'dst', 'edge_type_500', 'edge_weight', 'L1_gnn_relation_emb', 'L1_gnn_msg_w', 'L1_gnn_msg_b',
        'L1_gnn_upd_w', 'L1_gnn_upd_b', 'L1_gnn_gate_w', 'L1_gnn_gate_b']


def kernel(**inputs):
    import numpy as _np
    import concourse.bacc as _bacc
    from concourse import mybir as _mybir
    from concourse.bass_utils import run_bass_kernel_spmd as _run

    nc = _bacc.Bacc("TRN2", target_bir_lowering=False, num_devices=1)
    arrays, args = {}, []
    for name in _INS:
        a = _np.ascontiguousarray(inputs[name])
        arrays[f"in_{name}_dram"] = a
        args.append(nc.dram_tensor(f"in_{name}_dram", a.shape, _mybir.dt.from_np(a.dtype), kind="ExternalInput").ap())
    shape = tuple(inputs['x'].shape)
    args.append(nc.dram_tensor("out_0_dram", shape, _mybir.dt.float32, kind="ExternalOutput").ap())
    build_gnn(nc, *args)
    r = _run(nc, [arrays], core_ids=[0])
    return r.results[0]["out_0_dram"]
```
